# Optimizing a Trainium2 kernel written in Bass

```python
import numpy as np
import jax
import jax.numpy as jnp

def _softmax(x, axis=-1):
    return jax.nn.softmax(x, axis=axis)

def _gelu(x):
    return jax.nn.gelu(x, approximate=True)

def _silu(x):
    return jax.nn.silu(x)

def _sigmoid(x):
    return jax.nn.sigmoid(x)

def _layernorm(x, axis=-1, eps=1e-05):
    m = jnp.mean(x, axis=axis, keepdims=True)
    v = jnp.var(x, axis=axis, keepdims=True)
    return (x - m) / jnp.sqrt(v + eps)

def _scatter_add(tgt, idx, src, axis=0):
    return tgt.at[idx].add(src)

def _segment_sum(src, seg, n):
    return jax.ops.segment_sum(src, seg, n)
kernel_name = 'mk_hybrid_d1_jaxref_r4_46b8cd'

def setup_inputs(seed: int=0):
    np.random.seed(seed)
    _w = jnp.asarray

    def _L0_attn_a_setup():
        import jax, jax.numpy as jnp
        import numpy as np
        D = 256
        B = 16
        L = 512

        def _lin_init(key, din, dout):
            kw, kb = jax.random.split(key)
            s = 1.0 / np.sqrt(din)
            w = jax.random.uniform(kw, (dout, din), minval=-s, maxval=s, dtype=jnp.float32)
            b = jax.random.uniform(kb, (dout,), minval=-s, maxval=s, dtype=jnp.float32)
            return (w, b)

        def _rms_norm(x, w, eps=1e-06):
            x32 = x.astype(jnp.float32)
            y = x32 * jax.lax.rsqrt(jnp.mean(x32 * x32, axis=-1, keepdims=True) + eps)
            return y.astype(x.dtype) * w
        key = jax.random.key(seed)
        ks = jax.random.split(key, 9)
        fc_w, fc_b = _lin_init(ks[0], D, D)
        fc_r_w, fc_r_b = _lin_init(ks[1], D, D)
        fc_i_w, fc_i_b = _lin_init(ks[2], D, D)
        fc_gate_w, fc_gate_b = _lin_init(ks[3], D, D)
        mlp_gate_w, mlp_gate_b = _lin_init(ks[4], D, 3 * D)
        mlp_fc_w, mlp_fc_b = _lin_init(ks[5], D, 3 * D)
        out_w, out_b = _lin_init(ks[6], 3 * D, D)
        alpha = jax.random.uniform(ks[7], (1, 1, D), dtype=jnp.float32) * (0.999 - 0.9) + 0.9
        hidden_states = jax.random.normal(ks[8], (B, L, D), dtype=jnp.float32)
        return dict(hidden_states=hidden_states, alpha=alpha, fc_w=fc_w, fc_b=fc_b, fc_r_w=fc_r_w, fc_r_b=fc_r_b, fc_i_w=fc_i_w, fc_i_b=fc_i_b, fc_gate_w=fc_gate_w, fc_gate_b=fc_gate_b, norm_w=jnp.ones((D,), jnp.float32), norm2_w=jnp.ones((D,), jnp.float32), mlp_gate_w=mlp_gate_w, mlp_gate_b=mlp_gate_b, mlp_fc_w=mlp_fc_w, mlp_fc_b=mlp_fc_b, out_w=out_w, out_b=out_b)
    _L0_attn_a_in = _L0_attn_a_setup()

    def _L0_attn_b_setup():
        import jax, jax.numpy as jnp
        import numpy as np
        D_MODEL = 256
        N_STATE = 16
        D_INNER = 2 * D_MODEL
        DT_RANK = (D_MODEL + 15) // 16
        K_CONV = 4
        B, L = (1, 256)

        def _causal_dw_conv(x, w, b):
            K = w.shape[1]
            xp = jnp.pad(x, ((0, 0), (K - 1, 0), (0, 0)))
            Lx = x.shape[1]
            out = b
            for k in range(K):
                out = out + xp[:, k:k + Lx, :] * w[:, k]
            return out

        def _selective_scan(u, delta, A, Bm, Cm, D):
            dA = jnp.exp(delta[..., None] * A)
            dBu = delta[..., None] * Bm[:, :, None, :] * u[..., None]
            dA_t = jnp.moveaxis(dA, 1, 0)
            dBu_t = jnp.moveaxis(dBu, 1, 0)
            C_t = jnp.moveaxis(Cm, 1, 0)

            def step(h, inp):
                dA_i, dBu_i, C_i = inp
                h = dA_i * h + dBu_i
                y = jnp.einsum('bdn,bn->bd', h, C_i)
                return (h, y)
            h0 = jnp.zeros(u.shape[:1] + A.shape, dtype=u.dtype)
            _, ys = jax.lax.scan(step, h0, (dA_t, dBu_t, C_t))
            y = jnp.moveaxis(ys, 0, 1)
            return y + u * D
        key = jax.random.key(seed)
        ks = jax.random.split(key, 9)
        s = lambda fan_in: 1.0 / np.sqrt(fan_in)
        x = jax.random.normal(ks[0], (B, L, D_MODEL), dtype=jnp.float32)
        W_in = jax.random.normal(ks[1], (D_MODEL, 2 * D_INNER), dtype=jnp.float32) * s(D_MODEL)
        conv_w = jax.random.normal(ks[2], (D_INNER, K_CONV), dtype=jnp.float32) * s(K_CONV)
        conv_b = jnp.zeros((D_INNER,), dtype=jnp.float32)
        W_x = jax.random.normal(ks[3], (D_INNER, DT_RANK + 2 * N_STATE), dtype=jnp.float32) * s(D_INNER)
        W_dt = jax.random.normal(ks[4], (DT_RANK, D_INNER), dtype=jnp.float32) * s(DT_RANK)
        b_dt = jax.random.normal(ks[5], (D_INNER,), dtype=jnp.float32) * 0.01
        A_log = jnp.log(jnp.broadcast_to(jnp.arange(1, N_STATE + 1, dtype=jnp.float32), (D_INNER, N_STATE)))
        D = jnp.ones((D_INNER,), dtype=jnp.float32)
        W_out = jax.random.normal(ks[6], (D_INNER, D_MODEL), dtype=jnp.float32) * s(D_INNER)
        return {'x': x, 'W_in': W_in, 'conv_w': conv_w, 'conv_b': conv_b, 'W_x': W_x, 'W_dt': W_dt, 'b_dt': b_dt, 'A_log': A_log, 'D': D, 'W_out': W_out}
    _L0_attn_b_in = _L0_attn_b_setup()

    def _L0_ffn_setup():
        import jax, jax.numpy as jnp
        import numpy as np
        import math
        B, L, D = (4, 1024, 256)
        F = 1024
        E = 16
        CAP_FACTOR = 1.0
        EPS = 1e-05
        key = jax.random.key(seed)
        ks = jax.random.split(key, 8)
        std = 0.02
        return {'x': jax.random.normal(ks[0], (B, L, D), dtype=jnp.float32), 'norm_weight': jnp.ones((D,), dtype=jnp.float32), 'router_weight': jax.random.normal(ks[1], (E, D), dtype=jnp.float32) * std, 'router_bias': jnp.zeros((E,), dtype=jnp.float32), 'fc1_weight': jax.random.normal(ks[2], (E, F, D), dtype=jnp.float32) * std, 'fc1_bias': jnp.zeros((E, F), dtype=jnp.float32), 'fc2_weight': jax.random.normal(ks[3], (E, D, F), dtype=jnp.float32) * std, 'fc2_bias': jnp.zeros((E, D), dtype=jnp.float32)}
    _L0_ffn_in = _L0_ffn_setup()
    _d = {'L0_attn_a_hidden_states': _L0_attn_a_in['hidden_states'], 'L0_attn_a_alpha': _L0_attn_a_in['alpha'], 'L0_attn_a_fc_w': _L0_attn_a_in['fc_w'], 'L0_attn_a_fc_b': _L0_attn_a_in['fc_b'], 'L0_attn_a_fc_r_w': _L0_attn_a_in['fc_r_w'], 'L0_attn_a_fc_r_b': _L0_attn_a_in['fc_r_b'], 'L0_attn_a_fc_i_w': _L0_attn_a_in['fc_i_w'], 'L0_attn_a_fc_i_b': _L0_attn_a_in['fc_i_b'], 'L0_attn_a_fc_gate_w': _L0_attn_a_in['fc_gate_w'], 'L0_attn_a_fc_gate_b': _L0_attn_a_in['fc_gate_b'], 'L0_attn_a_norm_w': _L0_attn_a_in['norm_w'], 'L0_attn_a_norm2_w': _L0_attn_a_in['norm2_w'], 'L0_attn_a_mlp_gate_w': _L0_attn_a_in['mlp_gate_w'], 'L0_attn_a_mlp_gate_b': _L0_attn_a_in['mlp_gate_b'], 'L0_attn_a_mlp_fc_w': _L0_attn_a_in['mlp_fc_w'], 'L0_attn_a_mlp_fc_b': _L0_attn_a_in['mlp_fc_b'], 'L0_attn_a_out_w': _L0_attn_a_in['out_w'], 'L0_attn_a_out_b': _L0_attn_a_in['out_b'], 'L0_attn_b_W_in': _L0_attn_b_in['W_in'], 'L0_attn_b_conv_w': _L0_attn_b_in['conv_w'], 'L0_attn_b_conv_b': _L0_attn_b_in['conv_b'], 'L0_attn_b_W_x': _L0_attn_b_in['W_x'], 'L0_attn_b_W_dt': _L0_attn_b_in['W_dt'], 'L0_attn_b_b_dt': _L0_attn_b_in['b_dt'], 'L0_attn_b_A_log': _L0_attn_b_in['A_log'], 'L0_attn_b_D': _L0_attn_b_in['D'], 'L0_attn_b_W_out': _L0_attn_b_in['W_out'], 'L0_ffn_norm_weight': _L0_ffn_in['norm_weight'], 'L0_ffn_router_weight': _L0_ffn_in['router_weight'], 'L0_ffn_router_bias': _L0_ffn_in['router_bias'], 'L0_ffn_fc1_weight': _L0_ffn_in['fc1_weight'], 'L0_ffn_fc1_bias': _L0_ffn_in['fc1_bias'], 'L0_ffn_fc2_weight': _L0_ffn_in['fc2_weight'], 'L0_ffn_fc2_bias': _L0_ffn_in['fc2_bias']}
    _x0 = _d['L0_attn_a_hidden_states']
    _d['L0_attn_a_hidden_states'] = jax.random.normal(jax.random.fold_in(jax.random.key(seed), 1), (8, 1024, 256), dtype=_x0.dtype)
    del _x0
    return _d

def reference(L0_attn_a_hidden_states, L0_attn_a_alpha, L0_attn_a_fc_w, L0_attn_a_fc_b, L0_attn_a_fc_r_w, L0_attn_a_fc_r_b, L0_attn_a_fc_i_w, L0_attn_a_fc_i_b, L0_attn_a_fc_gate_w, L0_attn_a_fc_gate_b, L0_attn_a_norm_w, L0_attn_a_norm2_w, L0_attn_a_mlp_gate_w, L0_attn_a_mlp_gate_b, L0_attn_a_mlp_fc_w, L0_attn_a_mlp_fc_b, L0_attn_a_out_w, L0_attn_a_out_b, L0_attn_b_W_in, L0_attn_b_conv_w, L0_attn_b_conv_b, L0_attn_b_W_x, L0_attn_b_W_dt, L0_attn_b_b_dt, L0_attn_b_A_log, L0_attn_b_D, L0_attn_b_W_out, L0_ffn_norm_weight, L0_ffn_router_weight, L0_ffn_router_bias, L0_ffn_fc1_weight, L0_ffn_fc1_bias, L0_ffn_fc2_weight, L0_ffn_fc2_bias):

    def _L0_attn_a_ref(hidden_states, alpha, fc_w, fc_b, fc_r_w, fc_r_b, fc_i_w, fc_i_b, fc_gate_w, fc_gate_b, norm_w, norm2_w, mlp_gate_w, mlp_gate_b, mlp_fc_w, mlp_fc_b, out_w, out_b):
        import jax, jax.numpy as jnp
        import numpy as np
        D = 256
        B = 16
        L = 512

        def _lin_init(key, din, dout):
            kw, kb = jax.random.split(key)
            s = 1.0 / np.sqrt(din)
            w = jax.random.uniform(kw, (dout, din), minval=-s, maxval=s, dtype=jnp.float32)
            b = jax.random.uniform(kb, (dout,), minval=-s, maxval=s, dtype=jnp.float32)
            return (w, b)

        def _rms_norm(x, w, eps=1e-06):
            x32 = x.astype(jnp.float32)
            y = x32 * jax.lax.rsqrt(jnp.mean(x32 * x32, axis=-1, keepdims=True) + eps)
            return y.astype(x.dtype) * w
        residual = hidden_states
        h = _rms_norm(hidden_states, norm_w)
        gate = jax.nn.gelu(h @ fc_gate_w.T + fc_gate_b, approximate=False)
        hs = h @ fc_w.T + fc_b
        r = jax.nn.sigmoid(h @ fc_r_w.T + fc_r_b)
        i = jax.nn.sigmoid(h @ fc_i_w.T + fc_i_b)
        a = jnp.exp(-8.0 * jax.nn.softplus(alpha) * r)
        s = jnp.sqrt(1.0 - a * a) * hs * i

        def step(carry, xs):
            a_t, s_t = xs
            o = a_t * carry + s_t
            return (o, o)
        a_l = jnp.swapaxes(a, 0, 1)
        s_l = jnp.swapaxes(s, 0, 1)
        _, out_l = jax.lax.scan(step, jnp.zeros_like(s_l[0]), (a_l, s_l))
        out = jnp.swapaxes(out_l, 0, 1)
        hs2 = out * gate + residual
        h2 = _rms_norm(hs2, norm2_w)
        g2 = jax.nn.gelu(h2 @ mlp_gate_w.T + mlp_gate_b, approximate=False)
        f2 = h2 @ mlp_fc_w.T + mlp_fc_b
        return f2 * g2 @ out_w.T + out_b + hs2

    def _L0_attn_b_ref(x, W_in, conv_w, conv_b, W_x, W_dt, b_dt, A_log, D, W_out):
        import jax, jax.numpy as jnp
        import numpy as np
        D_MODEL = 256
        N_STATE = 16
        D_INNER = 2 * D_MODEL
        DT_RANK = (D_MODEL + 15) // 16
        K_CONV = 4
        B, L = (1, 256)

        def _causal_dw_conv(x, w, b):
            K = w.shape[1]
            xp = jnp.pad(x, ((0, 0), (K - 1, 0), (0, 0)))
            Lx = x.shape[1]
            out = b
            for k in range(K):
                out = out + xp[:, k:k + Lx, :] * w[:, k]
            return out

        def _selective_scan(u, delta, A, Bm, Cm, D):
            dA = jnp.exp(delta[..., None] * A)
            dBu = delta[..., None] * Bm[:, :, None, :] * u[..., None]
            dA_t = jnp.moveaxis(dA, 1, 0)
            dBu_t = jnp.moveaxis(dBu, 1, 0)
            C_t = jnp.moveaxis(Cm, 1, 0)

            def step(h, inp):
                dA_i, dBu_i, C_i = inp
                h = dA_i * h + dBu_i
                y = jnp.einsum('bdn,bn->bd', h, C_i)
                return (h, y)
            h0 = jnp.zeros(u.shape[:1] + A.shape, dtype=u.dtype)
            _, ys = jax.lax.scan(step, h0, (dA_t, dBu_t, C_t))
            y = jnp.moveaxis(ys, 0, 1)
            return y + u * D
        silu = jax.nn.silu
        x_and_res = x @ W_in
        x_in, res = jnp.split(x_and_res, 2, axis=-1)
        x_conv = silu(_causal_dw_conv(x_in, conv_w, conv_b))
        x_dbl = x_conv @ W_x
        dt, Bm, Cm = jnp.split(x_dbl, [DT_RANK, DT_RANK + N_STATE], axis=-1)
        delta = jax.nn.softplus(dt @ W_dt + b_dt)
        A = -jnp.exp(A_log)
        y = _selective_scan(x_conv, delta, A, Bm, Cm, D)
        return y * silu(res) @ W_out

    def _L0_ffn_ref(x, norm_weight, router_weight, router_bias, fc1_weight, fc1_bias, fc2_weight, fc2_bias):
        import jax, jax.numpy as jnp
        import numpy as np
        import math
        B, L, D = (4, 1024, 256)
        F = 1024
        E = 16
        CAP_FACTOR = 1.0
        EPS = 1e-05
        b, l, d = x.shape
        n_tokens = b * l
        n_experts = router_weight.shape[0]
        capacity = max(1, math.ceil(CAP_FACTOR * n_tokens / n_experts))
        top_k = min(capacity, n_tokens)
        xf = x.reshape(n_tokens, d)
        rms = jnp.sqrt(jnp.mean(xf * xf, axis=-1, keepdims=True) + EPS)
        xn = xf / rms * norm_weight
        logits = xn @ router_weight.T + router_bias
        probs = jax.nn.softmax(logits, axis=-1)
        _, idx = jax.lax.top_k(logits.T, top_k)
        xe = xn[idx]
        h = jnp.einsum('ecd,efd->ecf', xe, fc1_weight) + fc1_bias[:, None, :]
        h = jax.nn.gelu(h, approximate=False)
        y = jnp.einsum('ecf,edf->ecd', h, fc2_weight) + fc2_bias[:, None, :]
        gates = jnp.take_along_axis(probs.T, idx, axis=1)
        flat_idx = idx.reshape(-1)
        contrib = (y * gates[:, :, None]).reshape(-1, d)
        output = jnp.zeros((n_tokens, d), dtype=x.dtype).at[flat_idx].add(contrib)
        gate_sums = jnp.zeros((n_tokens, 1), dtype=x.dtype).at[flat_idx].add(gates.reshape(-1, 1))
        assigned = gate_sums > 0
        output = jnp.where(assigned, output / jnp.where(assigned, gate_sums, 1.0), output)
        return output.reshape(b, l, d)
    x = L0_attn_a_hidden_states
    x = x + _L0_attn_a_ref(_layernorm(x, axis=-1), L0_attn_a_alpha, L0_attn_a_fc_w, L0_attn_a_fc_b, L0_attn_a_fc_r_w, L0_attn_a_fc_r_b, L0_attn_a_fc_i_w, L0_attn_a_fc_i_b, L0_attn_a_fc_gate_w, L0_attn_a_fc_gate_b, L0_attn_a_norm_w, L0_attn_a_norm2_w, L0_attn_a_mlp_gate_w, L0_attn_a_mlp_gate_b, L0_attn_a_mlp_fc_w, L0_attn_a_mlp_fc_b, L0_attn_a_out_w, L0_attn_a_out_b)
    x = x + _L0_ffn_ref(_layernorm(x, axis=-1), L0_ffn_norm_weight, L0_ffn_router_weight, L0_ffn_router_bias, L0_ffn_fc1_weight, L0_ffn_fc1_bias, L0_ffn_fc2_weight, L0_ffn_fc2_bias)
    x = x + _L0_attn_b_ref(_layernorm(x, axis=-1), L0_attn_b_W_in, L0_attn_b_conv_w, L0_attn_b_conv_b, L0_attn_b_W_x, L0_attn_b_W_dt, L0_attn_b_b_dt, L0_attn_b_A_log, L0_attn_b_D, L0_attn_b_W_out)
    x = x + _L0_ffn_ref(_layernorm(x, axis=-1), L0_ffn_norm_weight, L0_ffn_router_weight, L0_ffn_router_bias, L0_ffn_fc1_weight, L0_ffn_fc1_bias, L0_ffn_fc2_weight, L0_ffn_fc2_bias)
    return x

_drawn_inputs = setup_inputs


def setup_inputs(seed=0):
    import zlib

    import numpy as np

    out = dict(_drawn_inputs(seed))
    spreads = {'L0_attn_a_norm_w': (1.0, 0.6),
     'L0_attn_a_norm2_w': (1.0, 0.6),
     'L0_attn_b_conv_b': (0.0, 0.1),
     'L0_attn_b_D': (1.0, 0.2),
     'L0_ffn_norm_weight': (1.0, 0.2),
     'L0_ffn_router_bias': (0.0, 2.0),
     'L0_ffn_fc1_bias': (0.0, 0.325),
     'L0_ffn_fc2_bias': (0.0, 0.1)}
    factors = {'L0_attn_a_alpha': 64.0,
     'L0_attn_a_fc_b': 8.0,
     'L0_attn_a_fc_r_w': 8.0,
     'L0_attn_a_fc_r_b': 37.01,
     'L0_attn_a_fc_i_w': 2.735,
     'L0_attn_a_fc_i_b': 22.592,
     'L0_attn_a_fc_gate_b': 7.544,
     'L0_attn_a_mlp_gate_b': 7.451,
     'L0_attn_a_mlp_fc_b': 7.585,
     'L0_attn_a_out_b': 4.569,
     'L0_attn_b_b_dt': 34.774}
    for name, (base, spread) in spreads.items():
        noise = np.random.default_rng([zlib.crc32(name.encode()), seed]).standard_normal(out[name].shape)
        drawn = base * np.exp(spread * noise) if base else spread * noise
        out[name] = jnp.asarray(drawn.astype(out[name].dtype))
    for name, factor in factors.items():
        out[name] = (out[name] * factor).astype(out[name].dtype)
    return out
```

```python
from contextlib import ExitStack

import concourse.bass as bass
from concourse import mybir

F32 = mybir.dt.float32
BF16 = mybir.dt.bfloat16
U32 = mybir.dt.uint32
ALU = mybir.AluOpType
ACT = mybir.ActivationFunctionType
AX_X = mybir.AxisListType.X

P = 128
D = 256
KD = D // P
B, L = 8, 1024
T = B * L
CH = 512
NCH = T // CH
TB = CH // P
H3 = 3 * D
KM = H3 // P
E, F, CAP = 16, 1024, T // 16
KF = F // P
DI, NS, DTR, KC = 2 * D, 16, D // 16, 4
KI = DI // P
LN_EPS, RMS_EPS, FFN_EPS = 1e-5, 1e-6, 1e-5


class Place:

    def __init__(self, pair, parity):
        self.pair, self.parity = pair, parity
        self.n = pair * 2 + parity
        self.fixed = isinstance(self.n, int)

    def shift(self, by):
        return Place(self.pair + (self.parity + by) // 2, (self.parity + by) % 2)

    def wait(self, eng, sem, count, least=1):
        if isinstance(count, int) and count < least:
            return
        eng.wait_ge(sem, count)


def wait_alone(eng, sem, count, passed):
    eng.wait_ge(sem, count)
    eng.sem_inc(passed, 1)



def recurrence_block(nc, x_in, x_out, w):
    x_rows = x_in.rearrange("(c t p) d -> c p t d", p=P, t=TB)
    y_rows = x_out.rearrange("(c t p) d -> c p t d", p=P, t=TB)
    col = {}
    at = 0
    for name, n in (("r", 2), ("i", 2), ("fc", 2), ("gate", 2), ("mg", KM), ("mf", KM),
                    ("norm", 2), ("norm2", 2), ("alpha", 2)):
        col[name] = at
        at += n
    ncols = at
    with ExitStack() as ctx:
        def sb(name, shape, dt=F32):
            return ctx.enter_context(nc.sbuf_tensor("a_" + name, shape, dt))

        def sem(name):
            return nc.alloc_semaphore("a_" + name)

        w_proj = sb("w_proj", [P, KD, 4, D])
        w_mlp = sb("w_mlp", [P, KD, 2, H3])
        w_out = sb("w_out", [P, KM, D])
        table = sb("table", [P, ncols])
        outb = sb("outb", [P, D])
        ident = sb("ident", [P, P])
        mean_w = sb("mean_w", [P, P])
        one = sb("one", [P, 1])
        eps6 = sb("eps6", [P, 1])
        sp = sb("sp", [P, 6, KD])
        xt = sb("xt", [P, 2, TB, D])
        u_rows = sb("u_rows", [P, TB, D])
        h_rows = sb("h_rows", [P, TB, D])
        xr = sb("xr", [P, TB, D])
        xb = sb("xb", [P, TB, D])
        yt = sb("yt", [P, 2, TB, D])
        stats = sb("stats", [P, TB, 6])
        mv = sb("mv", [P, TB, 2])
        var2 = sb("var2", [P, 2, TB])
        std2 = sb("std2", [P, 2, TB])
        inv2 = sb("inv2", [P, 2, TB])
        hscale = sb("hscale", [P, TB])
        u_cols = sb("u_cols", [P, 2, KD, CH])
        h_cols = sb("h_cols", [P, KD, CH])
        sig_r = sb("sig_r", [P, KD, CH])
        sig_i = sb("sig_i", [P, KD, CH])
        decay = sb("decay", [P, KD, CH])
        na2 = sb("na2", [P, KD, CH])
        beta = sb("beta", [P, KD, CH])
        drive = sb("drive", [P, KD, CH])
        state = sb("state", [P, 2, KD, CH])
        gate = sb("gate", [P, KD, CH])
        hs2 = sb("hs2", [P, 2, KD, CH])
        sq = sb("sq", [P, KD, CH])
        rms = sb("rms", [P, CH])
        inv_rms = sb("inv_rms", [P, CH])
        h2 = sb("h2", [P, KD, CH])
        g2 = sb("g2", [P, 2, CH])
        v = sb("v", [P, KM, CH])
        RING = 4
        ring = ctx.enter_context(nc.psum_tensor("a_ring", [P, RING, CH], F32))
        ps_out = ctx.enter_context(nc.psum_tensor("a_ps_out", [P, 2, CH], F32))
        ps_tr = ctx.enter_context(nc.psum_tensor("a_ps_tr", [P, 2, CH], F32))

        weights_in = sem("weights_in")
        setup = sem("setup")
        alpha_abs, alpha_exp, alpha_ln = sem("alpha_abs"), sem("alpha_exp"), sem("alpha_ln")
        consts = sem("consts")
        ident0 = sem("ident0")
        x_loaded = [sem("x_loaded0"), sem("x_loaded1")]
        xr_loaded = sem("xr_loaded")
        xb_ready = sem("xb_ready")
        t1_steps, t2_steps = sem("t1_steps"), sem("t2_steps")
        stats_ready, std_ready, rows_ready = sem("stats_ready"), sem("std_ready"), sem("rows_ready")
        tr_done, tr_read = sem("tr_done"), sem("tr_read")
        proj_done = sem("proj_done")
        ri_read, hs_read, g_read = sem("ri_read"), sem("hs_read"), sem("g_read")
        decay_ready, na2_ready, beta_ready = sem("decay_ready"), sem("na2_ready"), sem("beta_ready")
        drive_steps = sem("drive_steps")
        hs2_steps, hs2_ready, sq_ready = sem("hs2_steps"), sem("hs2_ready"), sem("sq_ready")
        norm_steps, stats_steps, dve_passed = sem("norm_steps"), sem("stats_steps"), sem("dve_passed")
        ms_done, rms_ready, inv_ready, h2_ready = sem("ms_done"), sem("rms_ready"), sem("inv_ready"), sem("h2_ready")
        mlp_done, mg_read, mf_read = sem("mlp_done"), sem("mg_read"), sem("mf_read")
        out_done, out_read = sem("out_done"), sem("out_read")
        y_stored = [sem("y_stored0"), sem("y_stored1")]
        NW = 6

        def pipeline(eng, stages):
            for k in range(-1, 4):
                stages(Place(k // 2, k % 2), k)
            with eng.Fori(2, NCH // 2 - 1) as i:
                stages(Place(i, 0), None)
                stages(Place(i, 1), None)
            for k in range(NCH - 2, NCH + 2):
                stages(Place(k // 2, k % 2), k)

        def has(k, stage):
            return k is None or 0 <= k + {"T": 1, "P": 0, "M": -1, "O": -2}[stage] < NCH

        block = ctx.enter_context(nc.Block())

        @block.sync
        def _(eng):
            eng.dma_start(table[:, :], w["a_table"]).then_inc(weights_in, 16)
            eng.dma_start(xt[:, 0], x_rows[0]).then_inc(x_loaded[0], 16)
            eng.dma_start(w_proj[:, :, :, :], w["a_proj"].rearrange("(k p) q d -> p k q d", p=P)).then_inc(weights_in, 16)
            eng.dma_start(outb[:, :], w["a_out_b"].partition_broadcast(P)).then_inc(weights_in, 16)
            eng.dma_start(xt[:, 1], x_rows[1]).then_inc(x_loaded[1], 16)
            for q in range(2):
                eng.dma_start(w_mlp[:, :, q, :], w["a_mlp"][q].rearrange("(k p) d -> p k d", p=P)).then_inc(weights_in, 16)
            eng.dma_start(w_out[:, :, :], w["a_out"].rearrange("(k p) d -> p k d", p=P)).then_inc(weights_in, 16)

            def stages(at, k):
                if has(k, "O"):
                    c = at.shift(-2)
                    c.wait(eng, xb_ready, c.n)
                    eng.dma_start(xr[:, :, :], x_rows[c.n]).then_inc(xr_loaded, 16)
                if has(k, "T") and (k is None or k + 3 < NCH):
                    nxt = at.shift(1)
                    eng.wait_ge(rows_ready, nxt.n + 1)
                    eng.dma_start(xt[:, nxt.parity], x_rows[at.shift(3).n]).then_inc(x_loaded[nxt.parity], 16)
                if has(k, "O"):
                    c = at.shift(-2)
                    eng.wait_ge(out_read, TB * c.n + TB)
                    eng.dma_start(y_rows[c.n], yt[:, c.parity]).then_inc(y_stored[c.parity], 16)

            for k in range(-1, 4):
                stages(Place(k // 2, k % 2), k)
            with eng.Fori(2, NCH // 2 - 2) as i:
                stages(Place(i, 0), None)
                stages(Place(i, 1), None)
            for k in range(NCH - 4, NCH + 2):
                stages(Place(k // 2, k % 2), k)
            for s in y_stored:
                eng.wait_ge(s, 16 * (NCH // 2))

        @block.gpsimd
        def _(eng):
            eng.memset(mean_w[:, :], 1.0 / D).then_inc(consts, 1)
            eng.memset(one[:, :], 1.0).then_inc(consts, 1)
            eng.memset(eps6[:, :], RMS_EPS).then_inc(consts, 1)
            eng.memset(ident[:, :], 0.0).then_inc(ident0, 1)
            eng.wait_ge(ident0, 1)
            eng.affine_select(out=ident[:, :], in_=ident[:, :], compare_op=ALU.not_equal, fill=1.0,
                              base=0, pattern=[[-1, P]], channel_multiplier=1).then_inc(consts, 1)
            eng.wait_ge(weights_in, 16 * NW)

            def stages(at, k):
                if has(k, "O"):
                    c = at.shift(-2)
                    eng.wait_ge(xr_loaded, 16 * c.n + 16)
                    c.wait(eng, out_read, TB * c.n)
                    eng.tensor_tensor(xb[:, :, :], xr[:, :, :],
                                      outb[:, :].unsqueeze(1).broadcast_to([P, TB, D]), ALU.add).then_inc(xb_ready, 1)
                if has(k, "P"):
                    eng.wait_ge(hs2_ready, at.n + 1)
                    eng.tensor_tensor(sq[:, :, :], hs2[:, at.parity], hs2[:, at.parity], ALU.mult).then_inc(sq_ready, 1)

            pipeline(eng, stages)

        @block.scalar
        def _(eng):
            eng.wait_ge(weights_in, 16 * NW)
            eng.wait_ge(consts, 4)
            eng.activation(sp[:, 0], table[:, col["alpha"]:col["alpha"] + 2], ACT.Abs).then_inc(alpha_abs, 1)
            eng.wait_ge(alpha_abs, 1)
            eng.activation(sp[:, 1], sp[:, 0], ACT.Exp, scale=-1.0).then_inc(alpha_exp, 1)
            eng.wait_ge(alpha_exp, 1)
            eng.activation(sp[:, 2], sp[:, 1], ACT.Ln, bias=one[:, 0:1]).then_inc(alpha_ln, 1)
            eng.wait_ge(setup, 3 + KD)

            def stages(at, k):
                if has(k, "P"):
                    at.wait(eng, hs_read, KD * at.n)
                    for j, (dst, name) in enumerate(((sig_r, "r"), (sig_r, "r"), (sig_i, "i"), (sig_i, "i"))):
                        eng.wait_ge(proj_done, 8 * at.n + j + 1)
                        half = j % 2
                        bias = table[:, col[name] + half:col[name] + half + 1]
                        eng.activation(dst[:, half], ring[:, j % RING], ACT.Sigmoid, bias=bias).then_inc(ri_read, 1)
                    at.wait(eng, drive_steps, 3 * at.n)
                    eng.wait_ge(ri_read, 4 * at.n + 2)
                    for half in range(KD):
                        eng.activation(decay[:, half], sig_r[:, half], ACT.Exp, scale=sp[:, 5, half:half + 1]).then_inc(decay_ready, 1)
                if has(k, "M"):
                    c = at.shift(-1)
                    eng.wait_ge(ms_done, c.n + 1)
                    c.wait(eng, inv_ready, c.n)
                    eng.activation(rms[:, :], ps_tr[:, 1], ACT.Sqrt, bias=eps6[:, 0:1]).then_inc(rms_ready, 1)
                if has(k, "T"):
                    c = at.shift(1)
                    eng.wait_ge(stats_ready, c.n + 1)
                    eng.activation(std2[:, :, :], var2[:, :, :], ACT.Sqrt).then_inc(std_ready, 1)
                if has(k, "P"):
                    eng.wait_ge(na2_ready, at.n + 1)
                    eng.activation(beta[:, :, :], na2[:, :, :], ACT.Sqrt, bias=one[:, 0:1]).then_inc(beta_ready, 1)
                    at.wait(eng, hs2_ready, at.n)
                    for half in range(KD):
                        eng.wait_ge(proj_done, 8 * at.n + 7 + half)
                        bias = table[:, col["gate"] + half:col["gate"] + half + 1]
                        eng.activation(gate[:, half], ring[:, (6 + half) % RING], ACT.Gelu, bias=bias).then_inc(g_read, 1)
                if has(k, "M"):
                    c = at.shift(-1)
                    for j in range(KM):
                        eng.wait_ge(mlp_done, 2 * KM * c.n + 2 * j + 1)
                        if j >= 2 or not (c.fixed and c.n == 0):
                            eng.wait_ge(mf_read, KM * c.n + j - 1)
                        bias = table[:, col["mg"] + j:col["mg"] + j + 1]
                        eng.activation(g2[:, j % 2], ring[:, (8 + 2 * j) % RING], ACT.Gelu, bias=bias).then_inc(mg_read, 1)

            pipeline(eng, stages)

        @block.tensor
        def _(eng):
            eng.wait_ge(setup, 3 + KD)
            eng.wait_ge(consts, 4)

            def stages(at, k):
                if has(k, "P"):
                    eng.wait_ge(tr_read, 4 * at.n + 4)
                    prev = at.shift(-2)
                    for j in range(8):
                        if j < RING:
                            s = 20 + j - RING - 8
                            at.wait(eng, mf_read if s % 2 else mg_read, KM * prev.n + s // 2 + 1)
                        else:
                            eng.wait_ge(ri_read, 4 * at.n + j - RING + 1)
                        for kb in range(KD):
                            mm = eng.matmul(ring[:, j % RING], w_proj[:, kb, j // 2, (j % 2) * P:(j % 2) * P + P],
                                            h_cols[:, kb], start=kb == 0, stop=kb == KD - 1)
                        mm.then_inc(proj_done, 1)
                if has(k, "O"):
                    c = at.shift(-2)
                    eng.wait_ge(mf_read, KM * c.n + KM)
                    for t in range(TB):
                        if t >= 2 or not (c.fixed and c.n == 0):
                            eng.wait_ge(out_read, TB * c.n + t - 1)
                        dst = ps_out[:, t % 2, 0:D]
                        for j in range(KM):
                            eng.matmul(dst, v[:, j, t * P:t * P + P], w_out[:, j], start=j == 0, stop=False,
                                       skip_group_check=True)
                        for kb in range(KD):
                            mm = eng.matmul(dst[:, kb * P:kb * P + P], hs2[:, c.parity, kb, t * P:t * P + P],
                                            ident[:, :], start=False, stop=True, skip_group_check=True)
                        mm.then_inc(out_done, 1)
                if has(k, "T"):
                    c = at.shift(1)
                    eng.wait_ge(rows_ready, c.n + 1)
                    for q in range(4):
                        src = (u_rows, h_rows)[q // 2]
                        if q < 2:
                            c.wait(eng, tr_read, 4 * c.n)
                            if q == 1:
                                last = at.shift(-1)
                                last.wait(eng, rms_ready, last.n + 1)
                        else:
                            eng.wait_ge(tr_read, 4 * c.n + q - 1)
                        for t in range(TB):
                            mm = eng.transpose(ps_tr[:, q % 2, t * P:t * P + P], src[:, t, (q % 2) * P:(q % 2) * P + P],
                                               ident[:, :])
                        mm.then_inc(tr_done, 1)
                if has(k, "M"):
                    c = at.shift(-1)
                    eng.wait_ge(h2_ready, c.n + 1)
                    for s in range(8, 20):
                        j = (s - 8) // 2
                        if s - RING >= 8:
                            q = s - RING - 8
                            eng.wait_ge(mf_read if q % 2 else mg_read, KM * c.n + q // 2 + 1)
                        elif has(k, "P"):
                            q = s - RING
                            if q < 4:
                                eng.wait_ge(ri_read, 4 * at.n + q + 1)
                            elif q < 6:
                                eng.wait_ge(hs_read, KD * at.n + q - 3)
                            else:
                                eng.wait_ge(g_read, KD * at.n + q - 5)
                        elif s == 8:
                            eng.wait_ge(mf_read, KM * c.n)
                            eng.wait_ge(mg_read, KM * c.n)
                            eng.wait_ge(g_read, KD * NCH)
                        for kb in range(KD):
                            mm = eng.matmul(ring[:, s % RING], w_mlp[:, kb, s % 2, j * P:j * P + P], h2[:, kb],
                                            start=kb == 0, stop=kb == KD - 1)
                        mm.then_inc(mlp_done, 1)
                if has(k, "P"):
                    eng.wait_ge(sq_ready, at.n + 1)
                    if has(k, "T"):
                        eng.wait_ge(tr_read, 4 * at.n + 8)
                    for kb in range(KD):
                        mm = eng.matmul(ps_tr[:, 1], mean_w[:, :], sq[:, kb], start=kb == 0, stop=kb == KD - 1)
                    mm.then_inc(ms_done, 1)

            pipeline(eng, stages)

        @block.vector
        def _(eng):
            eng.wait_ge(weights_in, 16 * NW)
            eng.tensor_scalar(sp[:, 3], table[:, col["alpha"]:col["alpha"] + 2], 0.0, None, ALU.max).then_inc(setup, 1)
            eng.wait_ge(alpha_ln, 1)
            eng.wait_ge(setup, 1)
            eng.tensor_tensor(sp[:, 4], sp[:, 3], sp[:, 2], ALU.add).then_inc(setup, 1)
            eng.wait_ge(setup, 2)
            eng.tensor_scalar(sp[:, 5], sp[:, 4], -8.0, None, ALU.mult).then_inc(setup, 1)
            for kb in range(KD):
                n1, n2 = col["norm"] + kb, col["norm2"] + kb
                eng.tensor_scalar(w_proj[:, kb], w_proj[:, kb], table[:, n1:n1 + 1], None, ALU.mult)
                eng.tensor_scalar(w_mlp[:, kb], w_mlp[:, kb], table[:, n2:n2 + 1], None, ALU.mult).then_inc(setup, 1)
            
            def stats_stage(c):
                steps = [0]

                def link(ins):
                    steps[0] += 1
                    ins.then_inc(t1_steps, 1)
                    eng.wait_ge(t1_steps, 3 * c.n + steps[0])

                eng.wait_ge(x_loaded[c.parity], 16 * c.pair + 16)
                for t in range(TB):
                    ins = eng.bn_stats(stats[:, t], xt[:, c.parity, t])
                ins.then_inc(stats_steps, 1)
                wait_alone(eng, stats_steps, c.n + 1, dve_passed)
                for t in range(TB):
                    ins = eng.bn_aggr(mv[:, t], stats[:, t])
                link(ins)
                link(eng.tensor_scalar(var2[:, 0], mv[:, :, 1], LN_EPS, None, ALU.add))
                link(eng.reciprocal(inv2[:, 0], var2[:, 0]))
                eng.tensor_tensor(inv2[:, 1], inv2[:, 0], mv[:, :, 1], ALU.mult).then_inc(norm_steps, 1)
                eng.wait_ge(norm_steps, c.n + 1)
                eng.tensor_scalar(var2[:, 1], inv2[:, 1], RMS_EPS, None, ALU.add).then_inc(stats_ready, 1)

            def rows_stage(c):
                eng.wait_ge(std_ready, c.n + 1)
                eng.reciprocal(inv2[:, :, :], std2[:, :, :]).then_inc(t2_steps, 1)
                eng.wait_ge(t2_steps, 2 * c.n + 1)
                eng.tensor_tensor(hscale[:, :], inv2[:, 0], inv2[:, 1], ALU.mult).then_inc(t2_steps, 1)
                eng.wait_ge(t2_steps, 2 * c.n + 2)
                c.wait(eng, tr_done, 4 * c.n)
                for t in range(TB):
                    eng.tensor_scalar(u_rows[:, t], xt[:, c.parity, t], mv[:, t, 0:1], inv2[:, 0, t:t + 1],
                                      ALU.subtract, ALU.mult)
                    ins = eng.tensor_scalar(h_rows[:, t], xt[:, c.parity, t], mv[:, t, 0:1], hscale[:, t:t + 1],
                                            ALU.subtract, ALU.mult)
                ins.then_inc(rows_ready, 1)

            def turn_stage(c):
                for q in range(4):
                    eng.wait_ge(tr_done, 4 * c.n + q + 1)
                    dst = u_cols[:, c.parity, q] if q < 2 else h_cols[:, q - 2]
                    eng.tensor_copy(dst, ps_tr[:, q % 2]).then_inc(tr_read, 1)

            def out_read_stage(c, t):
                eng.wait_ge(out_done, TB * c.n + t + 1)
                if t == 0:
                    eng.wait_ge(xb_ready, c.n + 1)
                    c.wait(eng, y_stored[c.parity], 16 * c.pair)
                eng.tensor_tensor(yt[:, c.parity, t], ps_out[:, t % 2, 0:D], xb[:, t], ALU.add).then_inc(out_read, 1)

            def stages(at, k):
                if has(k, "P"):
                    for half in range(KD):
                        eng.wait_ge(proj_done, 8 * at.n + 5 + half)
                        eng.wait_ge(ri_read, 4 * at.n + 3 + half)
                        bias = table[:, col["fc"] + half:col["fc"] + half + 1]
                        eng.scalar_tensor_tensor(drive[:, half], ring[:, (4 + half) % RING], bias, sig_i[:, half],
                                                 ALU.add, ALU.mult).then_inc(hs_read, 1)
                if has(k, "T"):
                    stats_stage(at.shift(1))
                if has(k, "P"):
                    eng.wait_ge(decay_ready, KD * at.n + KD)
                    at.wait(eng, beta_ready, at.n)
                    eng.scalar_tensor_tensor(na2[:, :, :], decay[:, :, :], -1.0, decay[:, :, :],
                                             ALU.mult, ALU.mult).then_inc(na2_ready, 1)
                if has(k, "O"):
                    out_read_stage(at.shift(-2), 0)
                if has(k, "M"):
                    c = at.shift(-1)
                    eng.wait_ge(rms_ready, c.n + 1)
                    eng.reciprocal(inv_rms[:, :], rms[:, :]).then_inc(inv_ready, 1)
                    eng.wait_ge(inv_ready, c.n + 1)
                    eng.tensor_tensor(h2[:, :, :], hs2[:, c.parity], inv_rms[:, :].unsqueeze(1).broadcast_to([P, KD, CH]),
                                      ALU.mult).then_inc(h2_ready, 1)
                if has(k, "O"):
                    out_read_stage(at.shift(-2), 1)
                if has(k, "T"):
                    rows_stage(at.shift(1))
                if has(k, "O"):
                    out_read_stage(at.shift(-2), 2)
                if has(k, "P"):
                    eng.wait_ge(beta_ready, at.n + 1)
                    eng.wait_ge(hs_read, KD * at.n + KD)
                    eng.tensor_tensor(drive[:, :, :], drive[:, :, :], beta[:, :, :], ALU.mult).then_inc(drive_steps, 1)
                    eng.wait_ge(drive_steps, 3 * at.n + 1)
                    for half in range(KD):
                        initial = 0.0 if at.parity == 0 else state[:, 0, half, CH - 1:CH]
                        eng.tensor_tensor_scan(state[:, at.parity, half], decay[:, half], drive[:, half], initial,
                                               ALU.mult, ALU.add).then_inc(drive_steps, 1)
                if has(k, "O"):
                    out_read_stage(at.shift(-2), 3)
                if has(k, "T"):
                    turn_stage(at.shift(1))
                if has(k, "P"):
                    eng.wait_ge(g_read, KD * at.n + KD)
                    eng.wait_ge(drive_steps, 3 * at.n + 3)
                    eng.tensor_tensor(gate[:, :, :], state[:, at.parity], gate[:, :, :], ALU.mult).then_inc(hs2_steps, 1)
                    eng.wait_ge(hs2_steps, at.n + 1)
                    eng.tensor_tensor(hs2[:, at.parity], gate[:, :, :], u_cols[:, at.parity], ALU.add).then_inc(hs2_ready, 1)
                if has(k, "M"):
                    c = at.shift(-1)
                    for j in range(KM):
                        eng.wait_ge(mlp_done, 2 * KM * c.n + 2 * j + 2)
                        eng.wait_ge(mg_read, KM * c.n + j + 1)
                        bias = table[:, col["mf"] + j:col["mf"] + j + 1]
                        eng.scalar_tensor_tensor(v[:, j], ring[:, (9 + 2 * j) % RING], bias, g2[:, j % 2],
                                                 ALU.add, ALU.mult).then_inc(mf_read, 1)

            pipeline(eng, stages)


def experts_block(nc, tag, x_tab, rows_tab, list_tab, w):
    NT = T // P
    NJ = P // E
    NQ = NT // NJ
    SPAN = NQ * P
    LO, HI = 32, CAP // 32
    SLOTS = CAP // P
    RW = D + E
    x_chunks = x_tab.rearrange("(c t p) d -> c p t d", p=P, t=TB)
    rows_chunks = rows_tab.rearrange("(c t p) d -> c p t d", p=P, t=TB)
    with ExitStack() as ctx:
        def sb(name, shape, dt=F32):
            return ctx.enter_context(nc.sbuf_tensor(tag + name, shape, dt))

        def sem(name):
            return nc.alloc_semaphore(tag + name)

        def ps(name, shape):
            return ctx.enter_context(nc.psum_tensor(tag + name, shape, F32))

        ident = sb("ident", [P, P])
        xt = sb("xt", [P, 2, TB, D])
        xn = sb("xn", [P, 2, TB, D])
        stats = sb("stats", [P, TB, 6])
        mv = sb("mv", [P, TB, 2])
        var2 = sb("var2", [P, 2, TB])
        std2 = sb("std2", [P, 2, TB])
        inv2 = sb("inv2", [P, 2, TB])
        hscale = sb("hscale", [P, TB])
        xcols = sb("xcols", [P, 2, KD, CH])
        w_router = sb("w_router", [P, KD, E])
        b_router = sb("b_router", [P, E])
        normw = sb("normw", [P, KD])
        logits = sb("logits", [P, NT, E])
        probs = sb("probs", [P, NT, E])
        tile_max = sb("tile_max", [P, NT])
        tile_sum = sb("tile_sum", [P, NT])
        by_e = sb("by_e", [P, SPAN])
        signed = sb("signed", [P, SPAN])
        flags = sb("flags", [P, SPAN])
        above = sb("above", [P, SPAN])
        equal = sb("equal", [P, SPAN])
        running = sb("running", [P, SPAN])
        ones = sb("ones", [P, SPAN])
        slot1 = sb("slot1", [P, SPAN])
        same_e = sb("same_e", [P, P])
        before = sb("before", [P, P])
        col_e = sb("col_e", [P, P])
        col_j = sb("col_j", [P, P])
        row_e = sb("row_e", [P, 1])
        row_j = sb("row_j", [P, 1])
        row_n = sb("row_n", [P, 1])
        iota_i = sb("iota_i", [P, LO, NT], U32)
        row_i = sb("row_i", [P, 3], U32)
        count = sb("count", [P, 4])
        sign = sb("sign", [P, 4])
        zero1 = sb("zero1", [P, 1])
        bits = sb("bits", [P, 4], U32)
        slot_i = sb("slot_i", [P, NQ, NJ, E], mybir.dt.int32)
        digit_i = sb("digit_i", [P, 2, NQ, NJ, E], mybir.dt.int32)
        lo_b = sb("lo_b", [P, E, NT], BF16)
        hi_b = sb("hi_b", [P, E, NT], BF16)
        taken = sb("taken", [P, NQ, NJ, E])
        part = sb("part", [P, NT, E])
        shares = sb("shares", [P, NJ, NQ, E])
        iota_lo = sb("iota_lo", [P, LO, NT], BF16)
        iota_hi = sb("iota_hi", [P, HI, NT], BF16)
        tile_no = sb("tile_no", [P, NT], BF16)
        hot_lo = sb("hot_lo", [P, 2, LO, NT], BF16)
        hot_hi = sb("hot_hi", [P, 2, HI, NT], BF16)
        values = sb("values", [P, 2, 2, HI, NT], BF16)
        part_sum = sb("part_sum", [LO, 2 * HI])
        lists = sb("lists", [LO, E, HI], U32)
        slots = sb("slots", [P, E, SLOTS], U32)
        w1 = sb("w1", [P, 2, KD, F])
        w2 = sb("w2", [P, 2, KF, D])
        b1 = sb("b1", [P, 2, KF])
        b2 = sb("b2", [P, 2, D])
        gather_at = sb("gather_at", [P, 2, SLOTS], U32)
        scatter_at = sb("scatter_at", [P, 2, SLOTS], U32)
        rows = sb("rows", [P, 2, SLOTS, RW])
        share = sb("share", [P, 2, SLOTS])
        xe = sb("xe", [P, KD, CAP])
        hid = sb("hid", [P, KF, CAP])
        ysum = sb("ysum", [P, SLOTS, D])
        ye = sb("ye", [P, 2, SLOTS, D])
        RING = 4
        ring = ps("ring", [P, RING, CH])
        ps_tr = ps("ps_tr", [P, 2, CH])
        ps_y = ps("ps_y", [P, 2, CH])

        weights_in, consts, ident0 = sem("weights_in"), sem("consts"), sem("ident0")
        consts2 = sem("consts2")
        x_loaded = [sem("x_loaded0"), sem("x_loaded1")]
        rows_stored = [sem("rows_stored0"), sem("rows_stored1")]
        stats_steps, t_steps, passed = sem("stats_steps"), sem("t_steps"), sem("passed")
        stats_ready, std_ready, rows_ready = sem("stats_ready"), sem("std_ready"), sem("rows_ready")
        tr_done, tr_read, logits_done, logits_read = sem("tr_done"), sem("tr_read"), sem("logits_done"), sem("logits_read")
        soft, exp_in, exp_done = sem("soft"), sem("exp_in"), sem("exp_done")
        by_e_done, counts_in, counts_out = sem("by_e_done"), sem("counts_in"), sem("counts_out")
        sel = sem("sel")
        slot_done, tokens_done = sem("slot_done"), sem("tokens_done")
        shares_ready, shares_stored = sem("shares_ready"), sem("shares_stored")
        hot_hi_ready, hot_lo_ready, list_done, list_read = sem("hot_hi_ready"), sem("hot_lo_ready"), sem("list_done"), sem("list_read")
        row_values_ready, tile_values_ready = sem("row_values_ready"), sem("tile_values_ready")
        list_stored, slots_in = sem("list_stored"), sem("slots_in")
        w_in = [sem("w_in0"), sem("w_in1")]
        gather_idx, scatter_idx = sem("gather_idx"), sem("scatter_idx")
        gathered, scattered = [sem("gathered0"), sem("gathered1")], sem("scattered")
        etr_done, etr_read, share_ready = sem("etr_done"), sem("etr_read"), sem("share_ready")
        hid_done, hid_ready = sem("hid_done"), sem("hid_ready")
        y_done, y_read, y_ready = sem("y_done"), sem("y_read"), sem("y_ready")
        pool_passed = sem("pool_passed")
        list_sum = sem("list_sum")
        NCONST = 9

        def experts(eng, stages):
            for k in range(-2, 2):
                stages(Place(k // 2, k % 2), k)
            with eng.Fori(1, E // 2 - 1) as i:
                stages(Place(i, 0), None)
                stages(Place(i, 1), None)
            for k in range(E - 2, E):
                stages(Place(k // 2, k % 2), k)

        def router_steps(eng, step):
            for k in range(-1, 4):
                step(Place(k // 2, k % 2), k)
            with eng.Fori(2, NCH // 2 - 1) as i:
                step(Place(i, 0), None)
                step(Place(i, 1), None)
            for k in range(NCH - 2, NCH + 2):
                step(Place(k // 2, k % 2), k)

        def in_router(k, ahead):
            return k is None or 0 <= k + ahead < NCH

        def has(k, ahead):
            return k is None or 0 <= k + ahead < E

        block = ctx.enter_context(nc.Block())

        @block.sync
        def _(eng):
            eng.dma_start(w_router[:, :, :], w["f_router"].rearrange("(k p) e -> p k e", p=P)).then_inc(weights_in, 16)
            eng.dma_start(b_router[:, :], w["f_router_b"].partition_broadcast(P)).then_inc(weights_in, 16)
            eng.dma_start(normw[:, :], w["f_norm"]).then_inc(weights_in, 16)
            for c in range(2):
                eng.dma_start(xt[:, c], x_chunks[c]).then_inc(x_loaded[c], 16)

            def router(c, more):
                eng.wait_ge(rows_ready, c.n + 1)
                eng.dma_start(rows_chunks[c.n][:, :, 0:D], xn[:, c.parity]).then_inc(rows_stored[c.parity], 16)
                if more:
                    eng.dma_start(xt[:, c.parity], x_chunks[c.shift(2).n]).then_inc(x_loaded[c.parity], 16)

            with eng.Fori(0, NCH // 2 - 1) as i:
                router(Place(i, 0), True)
                router(Place(i, 1), True)
            router(Place(NCH // 2 - 1, 0), False)
            router(Place(NCH // 2 - 1, 1), False)
            eng.wait_ge(shares_ready, 1)
            eng.dma_start(rows_tab.rearrange("(t p) d -> p t d", p=P)[:, :, D:RW],
                          shares[:, :, :, :].rearrange("p j q e -> p (j q) e")).then_inc(shares_stored, 16)
            eng.wait_ge(list_read, E)
            eng.dma_start(list_tab.rearrange("e (l h) -> l e h", l=LO), lists[:, :, :]).then_inc(list_stored, 16)
            eng.wait_ge(list_stored, 16)
            eng.dma_start(slots[:, :, :], list_tab.rearrange("e (p s) -> p e s", p=P)).then_inc(slots_in, 16)

            def stages(at, k):
                if has(k, 2):
                    c = at.shift(2)
                    if k is None or k >= 0:
                        eng.wait_ge(y_read, SLOTS * at.n + SLOTS)
                    s = w_in[c.parity]
                    eng.dma_start(w1[:, c.parity], w["f_w1"][c.n].rearrange("(k p) f -> p k f", p=P)).then_inc(s, 16)
                    eng.dma_start(b1[:, c.parity], w["f_b1"][c.n]).then_inc(s, 16)
                    eng.dma_start(w2[:, c.parity], w["f_w2"][c.n].rearrange("(k p) d -> p k d", p=P)).then_inc(s, 16)
                    eng.dma_start(b2[:, c.parity], w["f_b2"][c.n].partition_broadcast(P)).then_inc(s, 16)

            experts(eng, stages)

        @block.gpsimd
        def _(eng):
            eng.memset(ident[:, :], 0.0).then_inc(ident0, 1)
            eng.wait_ge(ident0, 1)
            eng.affine_select(out=ident[:, :], in_=ident[:, :], compare_op=ALU.not_equal, fill=1.0,
                              base=0, pattern=[[-1, P]], channel_multiplier=1).then_inc(consts, 1)
            eng.memset(zero1[:, :], 0.0).then_inc(consts, 1)
            eng.iota(row_i[:, 0:1], [[0, 1]], base=0, channel_multiplier=1).then_inc(consts, 1)
            eng.iota(iota_i[:, :, :], [[1, LO], [0, NT]], base=0, channel_multiplier=0).then_inc(consts, 1)
            eng.iota(col_e[:, :].bitcast(U32), [[0, NJ], [1, E]], base=0, channel_multiplier=0).then_inc(consts, 1)
            eng.iota(col_j[:, :].bitcast(U32), [[1, NJ], [0, E]], base=0, channel_multiplier=0).then_inc(consts, 1)
            eng.iota(bits[:, 0:4], [[0, 4]], base=0, channel_multiplier=0).then_inc(consts, 1)
            eng.iota(slot_i[:, 0, 0:4, :].bitcast(U32), [[1, NQ], [NQ, NJ]], base=0, channel_multiplier=0).then_inc(consts, 1)
            eng.memset(ones[:, :], 1.0).then_inc(consts, 1)

            def stages(at, k):
                if has(k, 2):
                    c = at.shift(2)
                    if k is None or k >= 0:
                        eng.wait_ge(etr_done, KD * at.n + KD)
                        eng.sem_inc(pool_passed, 1)
                        wait_alone(eng, share_ready, at.n + 1, pool_passed)
                    eng.tensor_copy(gather_at[:, c.parity], slots[:, c.n]).then_inc(gather_idx, 1)
                    wait_alone(eng, gather_idx, c.n + 1, pool_passed)
                    for s in range(SLOTS):
                        eng.indirect_dma_start(
                            out=rows[:, c.parity, s], out_offset=None, in_=rows_tab,
                            in_offset=bass.IndirectOffsetOnAxis(ap=gather_at[:, c.parity, s:s + 1], axis=0),
                        ).then_inc(gathered[c.parity], 16)
                if has(k, 0):
                    if k is None or k >= 1:
                        wait_alone(eng, scattered, 16 * SLOTS * at.n, pool_passed)
                    eng.tensor_copy(scatter_at[:, at.parity], slots[:, at.n]).then_inc(scatter_idx, 1)
                    wait_alone(eng, scatter_idx, at.n + 1, pool_passed)
                    for s in range(SLOTS):
                        wait_alone(eng, y_ready, SLOTS * at.n + s + 1, pool_passed)
                        eng.indirect_dma_start(
                            out=x_tab, out_offset=bass.IndirectOffsetOnAxis(ap=scatter_at[:, at.parity, s:s + 1], axis=0),
                            in_=ye[:, at.parity, s], in_offset=None, compute_op=ALU.add,
                        ).then_inc(scattered, 16)

            def tile_values(c):
                eng.wait_ge(hot_hi_ready, c.n + 1)
                eng.tensor_tensor(values[:, c.parity, 1], hot_hi[:, c.parity],
                                  tile_no[:, :].unsqueeze(1).broadcast_to([P, HI, NT]), ALU.mult).then_inc(tile_values_ready, 1)

            with eng.Fori(0, E // 2) as i:
                tile_values(Place(i, 0))
                tile_values(Place(i, 1))
            eng.wait_ge(slots_in, 16)
            eng.wait_ge(shares_stored, 16)
            for s in rows_stored:
                eng.wait_ge(s, 16 * (NCH // 2))
            experts(eng, stages)
            eng.wait_ge(scattered, 16 * SLOTS * E)

        @block.scalar
        def _(eng):
            def router(c):
                eng.wait_ge(stats_ready, c.n + 1)
                eng.activation(std2[:, :, :], var2[:, :, :], ACT.Sqrt).then_inc(std_ready, 1)

            with eng.Fori(0, NCH // 2) as i:
                router(Place(i, 0))
                router(Place(i, 1))
            eng.wait_ge(exp_in, 1)
            eng.activation(probs[:, :, :], probs[:, :, :], ACT.Exp).then_inc(exp_done, 1)

            def row_values(c):
                eng.wait_ge(hot_hi_ready, c.n + 1)
                eng.activation(values[:, c.parity, 0], hot_hi[:, c.parity], ACT.Copy, scale=row_n[:, 0:1]).then_inc(row_values_ready, 1)

            with eng.Fori(0, E // 2) as i:
                row_values(Place(i, 0))
                row_values(Place(i, 1))

            def stages(at, k):
                if has(k, 0):
                    eng.wait_ge(w_in[at.parity], 64 * at.pair + 64)
                    for j in range(KF):
                        eng.wait_ge(hid_done, KF * at.n + j + 1)
                        eng.activation(hid[:, j], ring[:, j % RING], ACT.Gelu, bias=b1[:, at.parity, j:j + 1]).then_inc(hid_ready, 1)

            experts(eng, stages)

        @block.tensor
        def _(eng):
            eng.wait_ge(consts, NCONST)
            eng.wait_ge(weights_in, 16 * 3)

            def turn(c):
                eng.wait_ge(rows_ready, c.n + 1)
                for q in range(KD):
                    if not (c.fixed and c.n == 0):
                        eng.wait_ge(tr_read, KD * (c.n - 1) + q + 1)
                    for t in range(TB):
                        mm = eng.transpose(ps_tr[:, q, t * P:t * P + P], xn[:, c.parity, t, q * P:q * P + P], ident[:, :])
                    mm.then_inc(tr_done, 1)

            def route(c):
                eng.wait_ge(tr_read, KD * c.n + KD)
                c.wait(eng, logits_read, c.n - 1)
                for t in range(TB):
                    for kb in range(KD):
                        mm = eng.matmul(ps_y[:, c.parity, t * E:t * E + E], xcols[:, c.parity, kb, t * P:t * P + P],
                                        w_router[:, kb], start=kb == 0, stop=kb == KD - 1)
                mm.then_inc(logits_done, 1)

            def router(at, k):
                if in_router(k, 0):
                    turn(at)
                if in_router(k, -1):
                    route(at.shift(-1))

            router_steps(eng, router)

            eng.wait_ge(logits_read, NCH)
            for q in range(NQ):
                mm = eng.transpose(ring[:, q // 4, (q % 4) * P:(q % 4) * P + P], logits[:, q * NJ:q * NJ + NJ].rearrange("p j e -> p (j e)"), ident[:, :])
            mm.then_inc(by_e_done, 1)
            for n in range(1 + 31 + 1):
                eng.wait_ge(counts_in, n + 1)
                eng.matmul(ring[:, 2, 0:1], same_e[:, :], count[:, n % 2:n % 2 + 1], start=True, stop=True).then_inc(counts_out, 1)
            for n in range(2):
                eng.wait_ge(counts_in, 34 + n)
                eng.matmul(ring[:, 3, 0:1], before[:, :], running[:, SPAN - 1:SPAN], start=True, stop=True).then_inc(counts_out, 1)
            eng.wait_ge(slot_done, 1)
            for q in range(NQ):
                mm = eng.transpose(ring[:, q // 4, (q % 4) * P:(q % 4) * P + P], slot1[:, q * P:q * P + P], ident[:, :])
            mm.then_inc(tokens_done, 1)

            def listed(c):
                eng.wait_ge(hot_lo_ready, c.n + 1)
                eng.wait_ge(row_values_ready, c.n + 1)
                eng.wait_ge(tile_values_ready, c.n + 1)
                c.wait(eng, list_read, c.n - 1)
                for t in range(NT):
                    mm = eng.matmul(ps_y[0:LO, c.parity, 0:2 * HI], hot_lo[:, c.parity, :, t],
                                    values[:, c.parity, :, :, t].rearrange("p v h -> p (v h)"),
                                    start=t == 0, stop=t == NT - 1)
                mm.then_inc(list_done, 1)

            for n in range(2):
                listed(Place(0, n))
            with eng.Fori(1, E // 2) as i:
                for n in range(2):
                    listed(Place(i, n))

            eng.wait_ge(list_read, E)

            def stages(at, k):
                if has(k, 0):
                    eng.wait_ge(w_in[at.parity], 64 * at.pair + 64)
                    eng.wait_ge(etr_read, KD * at.n + KD)
                    for j in range(KF):
                        if j >= RING or not (at.fixed and at.n == 0):
                            eng.wait_ge(hid_ready, KF * at.n + j - RING + 1)
                        for kb in range(KD):
                            mm = eng.matmul(ring[:, j % RING], w1[:, at.parity, kb, j * P:j * P + P], xe[:, kb],
                                            start=kb == 0, stop=kb == KD - 1)
                        mm.then_inc(hid_done, 1)
                if has(k, 1) and (k is None or k >= -1):
                    c = at.shift(1)
                    eng.wait_ge(gathered[c.parity], 16 * SLOTS * c.pair + 16 * SLOTS)
                    if not (c.fixed and c.n == 0):
                        eng.wait_ge(etr_read, KD * c.n)
                    for q in range(KD):
                        for s in range(SLOTS):
                            mm = eng.transpose(ps_tr[:, q, s * P:s * P + P], rows[:, c.parity, s, q * P:q * P + P], ident[:, :])
                        mm.then_inc(etr_done, 1)
                if has(k, 0):
                    for s in range(SLOTS):
                        if s >= 2 or not (at.fixed and at.n == 0):
                            eng.wait_ge(y_read, SLOTS * at.n + s - 1)
                        for j in range(KF):
                            if s == 0:
                                eng.wait_ge(hid_ready, KF * at.n + j + 1)
                            mm = eng.matmul(ps_y[:, s % 2, 0:D], hid[:, j, s * P:s * P + P], w2[:, at.parity, j],
                                            start=j == 0, stop=j == KF - 1)
                        mm.then_inc(y_done, 1)

            experts(eng, stages)

        @block.vector
        def _(eng):
            n = [0]

            def link(ins, s=None):
                n[0] += 1
                ins.then_inc(sel, 1)
                eng.wait_ge(sel, n[0])

            eng.wait_ge(consts, NCONST)
            eng.wait_ge(weights_in, 16 * 3)
            eng.tensor_copy(iota_lo[:, :, :], iota_i[:, :, :])
            eng.tensor_copy(iota_hi[:, :, :], iota_i[:, 0:HI])
            eng.tensor_copy(tile_no[:, :], slot_i[:, 0, 0:4, :].rearrange("p a b -> p (a b)"))
            eng.tensor_copy(same_e[:, :], col_e[:, :].bitcast(U32))
            eng.tensor_copy(before[:, :], col_j[:, :].bitcast(U32))
            eng.tensor_copy(row_n[:, :], row_i[:, 0:1])
            eng.tensor_scalar(row_i[:, 1:2], row_i[:, 0:1], E - 1, None, ALU.bitwise_and)
            link(eng.tensor_scalar(row_i[:, 2:3], row_i[:, 0:1], 4, None, ALU.logical_shift_right))
            eng.tensor_copy(row_e[:, :], row_i[:, 1:2])
            link(eng.tensor_copy(row_j[:, :], row_i[:, 2:3]))
            link(eng.tensor_scalar(same_e[:, :], same_e[:, :], row_e[:, 0:1], None, ALU.is_equal))
            link(eng.scalar_tensor_tensor(before[:, :], before[:, :], row_j[:, 0:1], same_e[:, :], ALU.is_gt, ALU.mult))

            def link_router(c, n, ins):
                ins.then_inc(t_steps, 1)
                eng.wait_ge(t_steps, 6 * c.n + n)

            def stats_stage(c):
                eng.wait_ge(x_loaded[c.parity], 16 * c.pair + 16)
                for t in range(TB):
                    ins = eng.bn_stats(stats[:, t], xt[:, c.parity, t])
                ins.then_inc(stats_steps, 1)
                c.wait(eng, rows_ready, c.n)
                wait_alone(eng, stats_steps, c.n + 1, passed)
                for t in range(TB):
                    ins = eng.bn_aggr(mv[:, t], stats[:, t])
                link_router(c, 1, ins)
                link_router(c, 2, eng.tensor_scalar(var2[:, 0], mv[:, :, 1], LN_EPS, None, ALU.add))
                link_router(c, 3, eng.reciprocal(inv2[:, 0], var2[:, 0]))
                link_router(c, 4, eng.tensor_tensor(inv2[:, 1], inv2[:, 0], mv[:, :, 1], ALU.mult))
                eng.tensor_scalar(var2[:, 1], inv2[:, 1], FFN_EPS, None, ALU.add).then_inc(stats_ready, 1)

            def rows_stage(c):
                eng.wait_ge(std_ready, c.n + 1)
                link_router(c, 5, eng.reciprocal(inv2[:, :, :], std2[:, :, :]))
                link_router(c, 6, eng.tensor_tensor(hscale[:, :], inv2[:, 0], inv2[:, 1], ALU.mult))
                if not (c.fixed and c.n < 2):
                    eng.wait_ge(rows_stored[c.parity], 16 * c.pair)
                    eng.wait_ge(tr_done, KD * (c.n - 1))
                for t in range(TB):
                    ins = eng.tensor_scalar(xn[:, c.parity, t], xt[:, c.parity, t], mv[:, t, 0:1], hscale[:, t:t + 1],
                                            ALU.subtract, ALU.mult)
                ins.then_inc(rows_ready, 1)

            def turned_stage(c):
                c.wait(eng, logits_done, c.n - 1)
                for q in range(KD):
                    eng.wait_ge(tr_done, KD * c.n + q + 1)
                    eng.tensor_scalar(xcols[:, c.parity, q], ps_tr[:, q], normw[:, q:q + 1], None, ALU.mult).then_inc(tr_read, 1)

            def logits_stage(c):
                eng.wait_ge(logits_done, c.n + 1)
                eng.tensor_tensor(logits[:, :, :].rearrange("p (q j) e -> p q j e", j=NJ)[:, TB * c.parity:TB * c.parity + TB, c.pair],
                                  ps_y[:, c.parity, 0:TB * E].rearrange("p (t e) -> p t e", e=E),
                                  b_router[:, :].unsqueeze(1).broadcast_to([P, TB, E]), ALU.add).then_inc(logits_read, 1)

            def router(at, k):
                if in_router(k, -1):
                    turned_stage(at.shift(-1))
                if in_router(k, 0):
                    rows_stage(at)
                if in_router(k, -2):
                    logits_stage(at.shift(-2))
                if in_router(k, 1):
                    stats_stage(at.shift(1))

            router_steps(eng, router)

            eng.wait_ge(logits_read, NCH)

            def softmax_step(b):
                if b == 30:
                    eng.tensor_reduce(tile_max[:, :], logits[:, :, :], AX_X, ALU.max).then_inc(soft, 1)
                elif b == 29:
                    eng.wait_ge(soft, 1)
                    eng.tensor_tensor(probs[:, :, :], logits[:, :, :], tile_max[:, :].unsqueeze(2).broadcast_to([P, NT, E]),
                                      ALU.subtract).then_inc(exp_in, 1)
                elif b == 26:
                    eng.wait_ge(exp_done, 1)
                    eng.tensor_reduce(tile_sum[:, :], probs[:, :, :], AX_X, ALU.add).then_inc(soft, 1)
                elif b == 25:
                    eng.wait_ge(soft, 2)
                    eng.reciprocal(tile_sum[:, :], tile_sum[:, :]).then_inc(soft, 1)
                elif b == 24:
                    eng.wait_ge(soft, 3)
                    eng.tensor_tensor(probs[:, :, :], probs[:, :, :], tile_sum[:, :].unsqueeze(2).broadcast_to([P, NT, E]),
                                      ALU.mult).then_inc(soft, 1)

            eng.wait_ge(by_e_done, 1)
            link(eng.tensor_copy(by_e[:, :], ring[:, 0:2].rearrange("p a b -> p (a b)")))
            rounds = [0]

            def total(src, threshold, op, b=None):
                m = rounds[0]
                rounds[0] += 1
                eng.tensor_scalar(flags[:, :], src, threshold, None, op, ALU.add,
                                  accum_out=count[:, m % 2:m % 2 + 1]).then_inc(counts_in, 1)
                softmax_step(b)
                eng.wait_ge(counts_out, m + 1)
                return ring[:, 2, 0:1]

            def prefix(src):
                ins = eng.tensor_tensor_scan(running[:, :], ones[:, :], src[:, :], 0.0, ALU.mult, ALU.add)
                ins.then_inc(counts_in, 1)
                eng.wait_ge(counts_in, prefix_at[0])
                prefix_at[0] += 1

            prefix_at = [34]
            c0 = total(by_e[:, :], zero1[:, 0:1], ALU.is_ge)
            link(eng.tensor_scalar(sign[:, 3:4], c0, float(CAP), None, ALU.is_ge))
            eng.tensor_scalar(sign[:, 0:1], sign[:, 3:4], 2.0, -1.0, ALU.mult, ALU.add)
            link(eng.tensor_scalar(sign[:, 1:2], sign[:, 3:4], float(2 * CAP - T - 1), float(T - CAP + 1), ALU.mult, ALU.add))
            link(eng.tensor_scalar(signed[:, :], by_e[:, :], sign[:, 0:1], None, ALU.mult))
            link(eng.tensor_scalar(bits[:, 3:4], bits[:, 0:1], 1 << 30, None, ALU.bitwise_or))
            for b in range(30, -1, -1):
                if b:
                    eng.tensor_scalar(bits[:, 1:2], bits[:, 0:1], 1 << (b - 1), None, ALU.bitwise_or)
                got = total(signed[:, :], bits[:, 3:4].bitcast(F32), ALU.is_ge, b)
                link(eng.tensor_scalar(bits[:, 2:3], got, sign[:, 1:2], None, ALU.is_ge))
                if b:
                    eng.scalar_tensor_tensor(bits[:, 3:4], bits[:, 2:3], b, bits[:, 1:2],
                                             ALU.logical_shift_left, ALU.bitwise_or)
                link(eng.scalar_tensor_tensor(bits[:, 0:1], bits[:, 2:3], b, bits[:, 0:1],
                                              ALU.logical_shift_left, ALU.bitwise_or))
            link(eng.tensor_tensor(sign[:, 2:3], bits[:, 0:1].bitcast(F32), sign[:, 0:1], ALU.mult))

            eng.tensor_scalar(above[:, :], by_e[:, :], sign[:, 2:3], None, ALU.is_gt)
            link(eng.tensor_scalar(equal[:, :], by_e[:, :], sign[:, 2:3], None, ALU.is_equal))
            got = total(by_e[:, :], sign[:, 2:3], ALU.is_gt)
            link(eng.tensor_scalar(sign[:, 3:4], got, -1.0, float(CAP), ALU.mult, ALU.add))
            prefix(equal)
            eng.wait_ge(counts_out, 34)
            link(eng.tensor_tensor(sign[:, 3:4], sign[:, 3:4], ring[:, 3, 0:1], ALU.subtract))
            link(eng.scalar_tensor_tensor(equal[:, :], running[:, :], sign[:, 3:4], equal[:, :], ALU.is_le, ALU.mult))
            link(eng.tensor_tensor(above[:, :], above[:, :], equal[:, :], ALU.add))
            prefix(above)
            eng.wait_ge(counts_out, 35)
            link(eng.tensor_copy(count[:, 2:3], ring[:, 3, 0:1]))
            eng.scalar_tensor_tensor(slot1[:, :], running[:, :], count[:, 2:3], above[:, :], ALU.add, ALU.mult).then_inc(slot_done, 1)

            eng.wait_ge(tokens_done, 1)
            link(eng.tensor_scalar(slot_i[:, :, :, :].rearrange("p q j e -> p (q j e)"),
                                   ring[:, 0:2].rearrange("p a b -> p (a b)"), -1.0, None, ALU.add))
            eng.tensor_scalar(taken[:, :, :, :], slot_i[:, :, :, :], 0.0, None, ALU.is_ge)
            eng.tensor_scalar(digit_i[:, 0], slot_i[:, :, :, :], LO - 1, None, ALU.bitwise_and)
            link(eng.tensor_scalar(digit_i[:, 1], slot_i[:, :, :, :], 5, None, ALU.arith_shift_right))
            for m, dst in ((0, lo_b), (1, hi_b)):
                link(eng.tensor_copy(dst[:, :, :].rearrange("p e t -> p t e"),
                                     digit_i[:, m].rearrange("p q j e -> p (q j) e")))
            eng.wait_ge(soft, 4)
            link(eng.tensor_tensor(part[:, :, :], probs[:, :, :], taken[:, :, :, :].rearrange("p q j e -> p (q j) e"), ALU.mult))
            link(eng.tensor_reduce(tile_sum[:, :], part[:, :, :], AX_X, ALU.add))
            link(eng.tensor_scalar(tile_max[:, :], tile_sum[:, :], 0.0, None, ALU.is_le))
            link(eng.tensor_tensor(tile_sum[:, :], tile_sum[:, :], tile_max[:, :], ALU.add))
            link(eng.reciprocal(tile_sum[:, :], tile_sum[:, :]))
            for q in range(NQ):
                tiles = slice(q * NJ, q * NJ + NJ)
                ins = eng.tensor_tensor(shares[:, :, q], part[:, tiles], tile_sum[:, tiles].unsqueeze(2).broadcast_to([P, NJ, E]),
                                        ALU.mult)
            ins.then_inc(shares_ready, 1)

            def hot_stage(c):
                c.wait(eng, list_done, c.n - 1)
                eng.tensor_tensor(hot_hi[:, c.parity], iota_hi[:, :, :],
                                  hi_b[:, c.n].unsqueeze(1).broadcast_to([P, HI, NT]), ALU.is_equal).then_inc(hot_hi_ready, 1)
                eng.tensor_tensor(hot_lo[:, c.parity], iota_lo[:, :, :],
                                  lo_b[:, c.n].unsqueeze(1).broadcast_to([P, LO, NT]), ALU.is_equal).then_inc(hot_lo_ready, 1)

            def list_stage(c):
                eng.wait_ge(list_done, c.n + 1)
                if not (c.fixed and c.n == 0):
                    eng.wait_ge(list_read, c.n)
                eng.tensor_copy(part_sum[:, :], ps_y[0:LO, c.parity, 0:2 * HI]).then_inc(list_sum, 1)
                eng.wait_ge(list_sum, c.n + 1)
                eng.scalar_tensor_tensor(lists[:, c.n], part_sum[:, HI:2 * HI], float(P), part_sum[:, 0:HI],
                                         ALU.mult, ALU.add).then_inc(list_read, 1)

            hot_stage(Place(0, 0))
            hot_stage(Place(0, 1))
            for m in range(2):
                list_stage(Place(0, m))
                hot_stage(Place(1, m))
            with eng.Fori(1, E // 2 - 1) as i:
                for m in range(2):
                    list_stage(Place(i, m))
                    hot_stage(Place(i, m).shift(2))
            for m in range(2):
                list_stage(Place(E // 2 - 1, m))

            def stages(at, k):
                if has(k, 1) and (k is None or k >= -1):
                    c = at.shift(1)
                    for q in range(KD):
                        eng.wait_ge(etr_done, KD * c.n + q + 1)
                        eng.tensor_scalar(xe[:, q], ps_tr[:, q], normw[:, q:q + 1], None, ALU.mult).then_inc(etr_read, 1)
                if has(k, 0):
                    eng.wait_ge(w_in[at.parity], 64 * at.pair + 64)
                    if k is None or k >= 2:
                        eng.wait_ge(scattered, 16 * SLOTS * (at.n - 1))
                    if k is None or k >= 1:
                        eng.wait_ge(y_ready, SLOTS * at.n)
                    for s in range(SLOTS):
                        eng.wait_ge(y_done, SLOTS * at.n + s + 1)
                        eng.tensor_tensor(ysum[:, s], ps_y[:, s % 2, 0:D], b2[:, at.parity], ALU.add).then_inc(y_read, 1)
                        eng.wait_ge(y_read, SLOTS * at.n + s + 1)
                        if s == 0:
                            eng.wait_ge(share_ready, at.n + 1)
                        eng.tensor_scalar(ye[:, at.parity, s], ysum[:, s], share[:, at.parity, s:s + 1], None, ALU.mult).then_inc(y_ready, 1)
                if has(k, 1) and (k is None or k >= -1):
                    c = at.shift(1)
                    eng.wait_ge(gathered[c.parity], 16 * SLOTS * c.pair + 16 * SLOTS)
                    eng.tensor_copy(share[:, c.parity], rows[:, c.parity, :, bass.ds(c.n + D, 1)].rearrange("p s o -> p (s o)")).then_inc(share_ready, 1)

            experts(eng, stages)


def state_space_block(nc, x_in, x_out, w):
    M = 2 * NS
    NT = L // P
    NH = L // CH
    BC = 2 * NS
    XD = 3 * BC + DTR
    x_rows = x_in.rearrange("(b t p) d -> b p t d", p=P, t=NT)
    y_rows = x_out.rearrange("(b t p) d -> b t p d", p=P, t=NT)
    x_tiles = x_in.rearrange("(b t p) d -> b t p d", p=P, t=NT)
    OUT, GATE, DELTA23, PREP = 9, 13, 17, 19
    PER_STEP = 23
    TURN, PROJ, XDBL, DELTA01 = 0, 4, 20, 22

    def after(eng, sem, count):
        if not isinstance(count, int) or count > 0:
            eng.wait_ge(sem, count)

    with ExitStack() as ctx:
        def sb(name, shape, dt=F32):
            return ctx.enter_context(nc.sbuf_tensor("b_" + name, shape, dt))

        def sem(name):
            return nc.alloc_semaphore("b_" + name)

        def ps(name, shape):
            return ctx.enter_context(nc.psum_tensor("b_" + name, shape, F32))

        w_in = sb("w_in", [P, KD, 2 * DI])
        w_x = sb("w_x", [P, KI, XD])
        w_dt = sb("w_dt", [P, DI])
        w_out = sb("w_out", [P, KI, D])
        taps = sb("taps", [P, KI, KC])
        tab = sb("tab", [P, 3, KI])
        a_log = sb("a_log", [P, KI, NS])
        ident = sb("ident", [P, P])
        diag_conv = sb("diag_conv", [P, KI, KC, P])
        diag_d = sb("diag_d", [P, KI, P])
        pick_i = sb("pick_i", [P, BC], U32)
        pick_r = sb("pick_r", [P, 2], U32)
        pick_f = sb("pick_f", [P, BC])
        pick_rf = sb("pick_rf", [P, 1])
        pick = sb("pick", [P, BC], BF16)
        one = sb("one", [P, 1])
        xt = sb("xt", [P, NT, D])
        stats = sb("stats", [P, NT, 6])
        mv = sb("mv", [P, NT, 2])
        var = sb("var", [P, NT])
        std = sb("std", [P, NT])
        inv = sb("inv", [P, NT])
        u_cols = sb("u_cols", [P, KD, L])
        PAD = KC - 1
        xin = sb("xin", [P, 2, PAD + L])
        xc = sb("xc", [P, KI, L])
        sres = sb("sres", [P, KI, L])
        xd = sb("xd", [P, L])
        parts = sb("parts", [P, L], BF16)
        rest = sb("rest", [P, L])
        delta = sb("delta", [P, KI, L])
        soft = sb("soft", [P, L])
        du = sb("du", [P, KI, L])
        bbc = sb("bbc", [P, 2, L])
        cbc = sb("cbc", [P, 2, L])
        da = sb("da", [P, 2, L])
        dbu = sb("dbu", [P, 2, L])
        h = sb("h", [P, 2, L])
        hc = sb("hc", [P, 2, L])
        yg = sb("yg", [P, KI, L])
        xr = sb("xr", [P, 2, D])
        yt = sb("yt", [P, 2, D])
        ps_y = ps("ps_y", [P, 2, L])
        ps_bc = ps("ps_bc", [P, L])
        side = ps("side", [P, 2, CH])

        weights_in, consts, ident0 = sem("weights_in"), sem("consts"), sem("ident0")
        setup, a_exp = sem("setup"), sem("a_exp")
        x_loaded = sem("x_loaded")
        ln_steps, stats_ready, std_ready, rows_ready = sem("ln_steps"), sem("stats_ready"), sem("std_ready"), sem("rows_ready")
        passed, pool_passed = sem("passed"), sem("pool_passed")
        side_done, side_read = [sem("side_done0"), sem("side_done1")], [sem("side_read0"), sem("side_read1")]
        xc_ready, gate_ready = sem("xc_ready"), sem("gate_ready")
        high_ready, rest_ready, mid_ready, parts_ready = (
            sem("high_ready"), sem("rest_ready"), sem("mid_ready"), sem("parts_ready"))
        soft_abs, soft_exp, soft_ready = sem("soft_abs"), sem("soft_exp"), sem("soft_ready")
        delta_ready, du_ready = sem("delta_ready"), sem("du_ready")
        bc_done, bbc_ready, cbc_ready = sem("bc_done"), sem("bbc_ready"), sem("cbc_ready")
        da_ready, dbu_ready, scanned, hc_ready, added = sem("da_ready"), sem("dbu_ready"), sem("scanned"), sem("hc_ready"), sem("added")
        y_read = sem("y_read")
        xr_loaded = [sem("xr_loaded0"), sem("xr_loaded1")]
        y_stored = [sem("y_stored0"), sem("y_stored1")]
        NW = 7

        def steps(eng, step):
            step(-1, False, False, True)
            step(0, True, False, True)
            with eng.Fori(1, B - 1) as b:
                step(b, True, True, True)
            step(B - 1, True, True, False)
            step(B, False, True, False)

        def bank_count(b, stage, slot):
            before = PER_STEP * b + stage + slot // 2
            if isinstance(b, int):
                if b == -1:
                    before = slot // 2
                elif b == B:
                    before -= 13
            return before

        def taken(eng, b, stage, slot):
            for k in (slot, slot + 1):
                eng.wait_ge(side_read[k % 2], bank_count(b, stage, k) + 1)

        block = ctx.enter_context(nc.Block())

        @block.sync
        def _(eng):
            eng.dma_start(xt[:, :, :], x_rows[0]).then_inc(x_loaded, 16)
            eng.dma_start(w_in[:, :, :], w["b_in"].rearrange("(k p) n -> p k n", p=P)).then_inc(weights_in, 16)
            eng.dma_start(w_x[:, :, :], w["b_x"].rearrange("(k p) n -> p k n", p=P)).then_inc(weights_in, 16)
            eng.dma_start(w_dt[3 * BC:XD, :], w["b_dt"]).then_inc(weights_in, 16)
            eng.dma_start(w_out[:, :, :], w["b_out"].rearrange("(k p) n -> p k n", p=P)).then_inc(weights_in, 16)
            eng.dma_start(taps[:, :, :], w["b_taps"].rearrange("(k p) n -> p k n", p=P)).then_inc(weights_in, 16)
            eng.dma_start(tab[:, :, :], w["b_tab"]).then_inc(weights_in, 16)
            eng.dma_start(a_log[:, :, :], w["b_a_log"].rearrange("(k p) n -> p k n", p=P)).then_inc(weights_in, 16)

            def step(b, units, out, prep):
                if prep and not (isinstance(b, int) and b == -1):
                    taken(eng, b - 1, PREP, TURN + 2)
                    eng.dma_start(xt[:, :, :], x_rows[b + 1]).then_inc(x_loaded, 16)
                if out:
                    for t in range(NT):
                        if t >= 2:
                            eng.wait_ge(side_read[t % 2], bank_count(b, OUT, t - 2) + 1)
                        else:
                            eng.wait_ge(side_read[t % 2], bank_count(b - 1, OUT, t + NT - 2) + 1)
                        eng.dma_start(xr[:, t % 2], x_tiles[b - 1][t]).then_inc(xr_loaded[t % 2], 16)
                        if t >= 1:
                            eng.wait_ge(side_read[(t - 1) % 2], bank_count(b, OUT, t - 1) + 1)
                            eng.dma_start(y_rows[b - 1][t - 1], yt[:, (t - 1) % 2]).then_inc(y_stored[(t - 1) % 2], 16)
                    eng.wait_ge(side_read[(NT - 1) % 2], bank_count(b, OUT, NT - 1) + 1)
                    eng.dma_start(y_rows[b - 1][NT - 1], yt[:, (NT - 1) % 2]).then_inc(y_stored[(NT - 1) % 2], 16)

            steps(eng, step)
            for s in y_stored:
                eng.wait_ge(s, 16 * B * NT // 2)

        @block.gpsimd
        def _(eng):
            eng.memset(ident[:, :], 0.0).then_inc(ident0, 1)
            eng.wait_ge(ident0, 1)
            eng.affine_select(out=ident[:, :], in_=ident[:, :], compare_op=ALU.not_equal, fill=1.0,
                              base=0, pattern=[[-1, P]], channel_multiplier=1).then_inc(consts, 1)
            eng.memset(one[:, :], 1.0).then_inc(consts, 1)
            eng.iota(pick_i[:, :], [[1, BC]], base=0, channel_multiplier=0).then_inc(consts, 1)
            eng.iota(pick_r[:, 0:1], [[0, 1]], base=0, channel_multiplier=1).then_inc(consts, 1)
            for c in range(2):
                eng.memset(xin[:, c, 0:PAD], 0.0).then_inc(consts, 1)
            eng.memset(w_dt[0:64, 0:4], 0.0).then_inc(consts, 1)

            def deltas(b, c):
                eng.wait_ge(soft_ready, 4 * b + c + 1)
                eng.tensor_tensor(delta[:, c], delta[:, c], soft[:, :], ALU.add).then_inc(delta_ready, 1)
                eng.wait_ge(delta_ready, 4 * b + c + 1)
                eng.wait_ge(xc_ready, b + 1)
                eng.tensor_tensor(du[:, c], delta[:, c], xc[:, c], ALU.mult).then_inc(du_ready, 1)

            def step(b, units, out, prep):
                if units:
                    for m in range(M):
                        for i in range(2):
                            c, u = 2 * (m // NS) + i, 2 * m + i
                            if m == 0 or m == NS:
                                eng.wait_ge(du_ready, 4 * b + c + 1)
                            if i == 0:
                                eng.wait_ge(bbc_ready, M * b + m + 1)
                            after(eng, scanned, 2 * M * b + u - 1)
                            eng.tensor_tensor(dbu[:, i], du[:, c], bbc[:, m % 2], ALU.mult).then_inc(dbu_ready, 1)
                        if m in (11, 12):
                            deltas(b, m - 9)
                if prep:
                    deltas(b + 1, 0)
                    deltas(b + 1, 1)

            steps(eng, step)

        @block.scalar
        def _(eng):
            eng.wait_ge(weights_in, 16 * NW)
            eng.wait_ge(consts, 6)
            eng.activation(a_log[:, :, :], a_log[:, :, :], ACT.Exp).then_inc(a_exp, 1)
            eng.wait_ge(setup, 8)

            def soft_slot(b, stage, slot, nb, c, half):
                bank, n = slot % 2, bank_count(b, stage, slot)
                eng.wait_ge(side_done[bank], n + 1)
                z, bias = side[:, bank], tab[:, 1, c:c + 1]
                if half == 0:
                    after(eng, delta_ready, 4 * nb + c)
                    after(eng, soft_ready, 4 * nb + c)
                cols = slice(half * CH, half * CH + CH)
                eng.activation(delta[:, c, cols], z, ACT.Relu, bias=bias)
                eng.activation(soft[:, cols], z, ACT.Abs, bias=bias).then_inc(side_read[bank], 1)
                if half == 1:
                    eng.wait_ge(side_read[bank], n + 1)
                    eng.activation(soft[:, :], soft[:, :], ACT.Exp, scale=-1.0).then_inc(soft_exp, 1)
                    eng.wait_ge(soft_exp, 4 * nb + c + 1)
                    eng.activation(soft[:, :], soft[:, :], ACT.Ln, bias=one[:, 0:1]).then_inc(soft_ready, 1)

            def std_stage(b):
                eng.wait_ge(stats_ready, b + 1)
                eng.activation(std[:, :], var[:, :], ACT.Sqrt).then_inc(std_ready, 1)

            def xdbl_slot(b, half):
                bank, n = half, bank_count(b, PREP, XDBL + half)
                eng.wait_ge(side_done[bank], n + 1)
                if half == 0:
                    after(eng, parts_ready, b + 1)
                eng.activation(xd[0:XD, half * CH:half * CH + CH], side[0:XD, bank], ACT.Copy).then_inc(side_read[bank], 1)

            def step(b, units, out, prep):
                if prep and not units:
                    std_stage(b + 1)
                if units:
                    for m in range(M):
                        U = 2 * M * b + 2 * m
                        for i, (dst, ready, used) in enumerate(((bbc, bbc_ready, dbu_ready), (cbc, cbc_ready, hc_ready))):
                            eng.wait_ge(bc_done, U + i + 1)
                            after(eng, used, U - 2)
                            eng.activation(dst[:, m % 2], ps_bc[:, :], ACT.Copy).then_inc(ready, 1)
                            c = 2 * (m // NS) + i
                            if m == 0 or m == NS:
                                eng.wait_ge(delta_ready, 4 * b + c + 1)
                            after(eng, scanned, U + i - 1)
                            eng.activation(da[:, i], delta[:, c], ACT.Exp, scale=a_log[:, c, m % NS:m % NS + 1]).then_inc(da_ready, 1)
                        if m == 12:
                            if prep:
                                std_stage(b + 1)
                            taken(eng, b, GATE, 6)
                            eng.activation(sres[:, :, :], sres[:, :, :], ACT.Silu).then_inc(gate_ready, 1)
                        if m in (10, 11):
                            for half in range(NH):
                                soft_slot(b, DELTA23, 2 * (m - 10) + half, b, m - 8, half)
                        if prep and m == 27:
                            taken(eng, b, PREP, PROJ + 14)
                            eng.activation(xc[:, :, :], xc[:, :, :], ACT.Silu).then_inc(xc_ready, 1)
                        if prep and m == 29:
                            for half in range(NH):
                                xdbl_slot(b, half)
                        if prep and m in (30, 31):
                            for half in range(NH):
                                soft_slot(b, PREP, DELTA01 + 2 * (m - 30) + half, b + 1, m - 30, half)
                elif prep:
                    taken(eng, b, PREP, PROJ + 14)
                    eng.activation(xc[:, :, :], xc[:, :, :], ACT.Silu).then_inc(xc_ready, 1)
                    for half in range(NH):
                        xdbl_slot(b, half)
                    for c in range(2):
                        for half in range(NH):
                            soft_slot(b, PREP, DELTA01 + 2 * c + half, 0, c, half)
                if prep:
                    taken(eng, b, PREP, XDBL)
                    after(eng, bc_done, 2 * M * (b + 1))
                    eng.activation(parts[0:3 * BC, :], xd[0:3 * BC, :], ACT.Copy).then_inc(high_ready, 1)
                    eng.wait_ge(rest_ready, 2 * (b + 1) + 2)
                    for r in (BC, 2 * BC):
                        ins = eng.activation(parts[r:r + BC, :], rest[r:r + BC, :], ACT.Copy)
                    ins.then_inc(mid_ready, 1)

            steps(eng, step)

        @block.tensor
        def _(eng):
            eng.wait_ge(setup, 8)
            eng.wait_ge(consts, 7)

            def fill(b, stage, slot, part, products):
                bank, n = slot % 2, bank_count(b, stage, slot)
                after(eng, side_read[bank], n)
                last = len(products) - 1
                for k, (lhs, rhs) in enumerate(products):
                    mm = eng.matmul(part(side[:, bank]), lhs, rhs, start=k == 0, stop=k == last)
                mm.then_inc(side_done[bank], 1)

            def cols(half, shift=0):
                return slice(half * CH + shift, half * CH + CH + shift)

            def turn(b, slots):
                eng.wait_ge(rows_ready, b + 2)
                for slot in slots:
                    kb, half = slot // 2, slot % 2
                    bank, n = slot % 2, bank_count(b, PREP, TURN + slot)
                    after(eng, side_read[bank], n)
                    for t in range(4):
                        mm = eng.transpose(side[:, bank, t * P:t * P + P], xt[:, 4 * half + t, kb * P:kb * P + P], ident[:, :])
                    mm.then_inc(side_done[bank], 1)

            def project(b, c):
                taken(eng, b, PREP, TURN + 2)
                for half in range(NH):
                    fill(b, PREP, PROJ + 4 * c + half, lambda o: o,
                         [(w_in[:, kb, c * P:c * P + P], u_cols[:, kb, cols(half)]) for kb in range(KD)])

            def convolve(b, c):
                taken(eng, b, PREP, PROJ + 4 * c)
                for half in range(NH):
                    fill(b, PREP, PROJ + 4 * c + 2 + half, lambda o: o,
                         [(diag_conv[:, c, k], xin[:, c % 2, cols(half, k)]) for k in range(KC)])

            def xdbl(b):
                eng.wait_ge(xc_ready, b + 2)
                for half in range(NH):
                    fill(b, PREP, XDBL + half, lambda o: o[0:XD],
                         [(w_x[:, kb], xc[:, kb, cols(half)]) for kb in range(KI)])

            def dt(b, stage, slot, nb, c):
                taken(eng, nb - 1, PREP, XDBL)
                for half in range(NH):
                    fill(b, stage, slot + half, lambda o: o,
                         [(w_dt[3 * BC:XD, c * P:c * P + P], xd[3 * BC:XD, cols(half)])])

            def gates(b, c):
                for half in range(NH):
                    fill(b, GATE, 2 * c + half, lambda o: o,
                         [(w_in[:, kb, DI + c * P:DI + c * P + P], u_cols[:, kb, cols(half)]) for kb in range(KD)])

            def outs(b, t):
                if t == 0:
                    eng.wait_ge(y_read, 4 * b)
                fill(b, OUT, t, lambda o: o[:, 0:D],
                     [(yg[:, kb, t * P:t * P + P], w_out[:, kb]) for kb in range(KI)])

            def add(b, m, i):
                c, u = 2 * (m // NS) + i, 2 * M * b + 2 * m + i
                if m % NS == 0:
                    after(eng, y_read, 4 * b + 2 * (m // NS) - 1 + i)
                    for half in range(NH):
                        eng.matmul(ps_y[:, i, cols(half)], diag_d[:, c], xc[:, c, cols(half)], start=True, stop=False,
                                   skip_group_check=True)
                eng.wait_ge(hc_ready, u + 1)
                for half in range(NH):
                    mm = eng.matmul(ps_y[:, i, cols(half)], ident[:, :], hc[:, i, cols(half)], start=False,
                                    stop=m % NS == NS - 1, skip_group_check=True)
                mm.then_inc(added, 1)

            def spread(b, m, i):
                if i == 0:
                    after(eng, cbc_ready, M * b + m)
                else:
                    eng.wait_ge(bbc_ready, M * b + m + 1)
                n = NS * i + m % NS
                for half in range(NH):
                    mm = eng.matmul(ps_bc[:, cols(half)], pick[0:3 * BC, n:n + 1].broadcast_to([3 * BC, P]),
                                    parts[0:3 * BC, cols(half)], start=True, stop=True)
                mm.then_inc(bc_done, 1)

            def step(b, units, out, prep):
                if units:
                    eng.wait_ge(parts_ready, b + 1)
                    for m in range(M):
                        for i in range(2):
                            spread(b, m, i)
                            if m >= 1:
                                add(b, m - 1, i)
                        if out and 2 <= m < 6:
                            outs(b, 2 * (m - 2))
                            outs(b, 2 * (m - 2) + 1)
                        if 6 <= m < 10:
                            gates(b, m - 6)
                        if m in (10, 11):
                            dt(b, DELTA23, 2 * (m - 10), b, m - 8)
                        if prep and m in (17, 18):
                            turn(b, (2 * (m - 17), 2 * (m - 17) + 1))
                        if prep and 19 <= m < 27:
                            (project if m % 2 else convolve)(b, (m - 19) // 2)
                        if prep and m == 29:
                            xdbl(b)
                        if prep and m in (30, 31):
                            dt(b, PREP, DELTA01 + 2 * (m - 30), b + 1, m - 30)
                    for i in range(2):
                        add(b, M - 1, i)
                elif prep:
                    turn(b, range(4))
                    for c in range(KI):
                        project(b, c)
                        convolve(b, c)
                    xdbl(b)
                    for c in range(2):
                        dt(b, PREP, DELTA01 + 2 * c, b + 1, c)
                elif out:
                    for t in range(NT):
                        outs(b, t)

            steps(eng, step)

        @block.vector
        def _(eng):
            eng.wait_ge(consts, 7)
            eng.wait_ge(weights_in, 16 * NW)
            eng.tensor_copy(pick_f[:, :], pick_i[:, :])
            eng.tensor_scalar(pick_r[:, 1:2], pick_r[:, 0:1], BC - 1, None, ALU.bitwise_and).then_inc(setup, 1)
            eng.wait_ge(setup, 1)
            eng.tensor_copy(pick_rf[:, :], pick_r[:, 1:2]).then_inc(setup, 1)
            eng.wait_ge(setup, 2)
            eng.tensor_scalar(pick[:, :], pick_f[:, :], pick_rf[:, 0:1], None, ALU.is_equal).then_inc(setup, 1)
            for c in range(KI):
                for k in range(KC):
                    eng.tensor_scalar(diag_conv[:, c, k], ident[:, :], taps[:, c, k:k + 1], None, ALU.mult)
                eng.tensor_scalar(diag_d[:, c], ident[:, :], tab[:, 2, c:c + 1], None, ALU.mult).then_inc(setup, 1)
            eng.wait_ge(a_exp, 1)
            eng.tensor_scalar(a_log[:, :, :], a_log[:, :, :], -1.0, None, ALU.mult).then_inc(setup, 1)

            def norm(nb):
                eng.wait_ge(x_loaded, 16 * nb + 16)
                for t in range(NT):
                    ins = eng.bn_stats(stats[:, t], xt[:, t])
                ins.then_inc(ln_steps, 1)
                wait_alone(eng, ln_steps, 3 * nb + 1, passed)
                for t in range(NT):
                    ins = eng.bn_aggr(mv[:, t], stats[:, t])
                ins.then_inc(ln_steps, 1)
                eng.wait_ge(ln_steps, 3 * nb + 2)
                eng.tensor_scalar(var[:, :], mv[:, :, 1], LN_EPS, None, ALU.add).then_inc(stats_ready, 1)

            def norm_rows(nb):
                eng.wait_ge(std_ready, nb + 1)
                eng.reciprocal(inv[:, :], std[:, :]).then_inc(ln_steps, 1)
                eng.wait_ge(ln_steps, 3 * nb + 3)
                for t in range(NT):
                    ins = eng.tensor_scalar(xt[:, t], xt[:, t], mv[:, t, 0:1], inv[:, t:t + 1], ALU.subtract, ALU.mult)
                ins.then_inc(rows_ready, 1)

            def read(b, stage, slot):
                bank, n = slot % 2, bank_count(b, stage, slot)
                eng.wait_ge(side_done[bank], n + 1)
                return side[:, bank], side_read[bank]

            def turn_read(b, slots):
                for slot in slots:
                    kb, half = slot // 2, slot % 2
                    src, s = read(b, PREP, TURN + slot)
                    eng.tensor_copy(u_cols[:, kb, half * CH:half * CH + CH], src).then_inc(s, 1)

            def project_read(b, c):
                for half in range(NH):
                    src, s = read(b, PREP, PROJ + 4 * c + half)
                    eng.tensor_copy(xin[:, c % 2, PAD + half * CH:PAD + half * CH + CH], src).then_inc(s, 1)

            def conv_read(b, c):
                for half in range(NH):
                    src, s = read(b, PREP, PROJ + 4 * c + 2 + half)
                    eng.tensor_scalar(xc[:, c, half * CH:half * CH + CH], src, tab[:, 0, c:c + 1], None,
                                      ALU.add).then_inc(s, 1)

            def gate_read(b, c):
                for half in range(NH):
                    src, s = read(b, GATE, 2 * c + half)
                    eng.tensor_copy(sres[:, c, half * CH:half * CH + CH], src).then_inc(s, 1)

            def out_read(b, t):
                src, s = read(b, OUT, t)
                n = NT * (b - 1) + t
                eng.wait_ge(xr_loaded[t % 2], 8 * (n - t % 2) + 16)
                after(eng, y_stored[t % 2], 8 * (n - t % 2))
                eng.tensor_tensor(yt[:, t % 2], src[:, 0:D], xr[:, t % 2], ALU.add).then_inc(s, 1)

            def gated(b, q):
                eng.wait_ge(gate_ready, b + 1)
                for i in range(2):
                    eng.wait_ge(added, 2 * M * b + 2 * NS * (q + 1) - 1 + i)
                    eng.tensor_tensor(yg[:, 2 * q + i], ps_y[:, i], sres[:, 2 * q + i], ALU.mult).then_inc(y_read, 1)

            def split(b):
                n = b + 1
                eng.wait_ge(high_ready, n + 1)
                for r in (BC, 2 * BC):
                    ins = eng.tensor_tensor(rest[r:r + BC, :], xd[r:r + BC, :], parts[r:r + BC, :], ALU.subtract)
                    ins.then_inc(rest_ready, 1)
                eng.wait_ge(mid_ready, n + 1)
                r = 2 * BC
                eng.tensor_tensor(parts[r:r + BC, :], rest[r:r + BC, :], parts[r:r + BC, :], ALU.subtract).then_inc(parts_ready, 1)

            def step(b, units, out, prep):
                if prep and not units:
                    norm(b + 1)
                    norm_rows(b + 1)
                    turn_read(b, range(4))
                    for c in range(KI):
                        project_read(b, c)
                        conv_read(b, c)
                if units:
                    for m in range(M):
                        U = 2 * M * b + 2 * m
                        for i in range(2):
                            eng.wait_ge(da_ready, U + i + 1)
                            eng.wait_ge(dbu_ready, U + i + 1)
                            after(eng, hc_ready, U + i - 1)
                            eng.tensor_tensor_scan(h[:, i], da[:, i], dbu[:, i], 0.0, ALU.mult, ALU.add).then_inc(scanned, 1)
                        for i in range(2):
                            if i == 0:
                                eng.wait_ge(cbc_ready, M * b + m + 1)
                            eng.wait_ge(scanned, U + i + 1)
                            after(eng, added, U + i - 1)
                            eng.tensor_tensor(hc[:, i], h[:, i], cbc[:, m % 2], ALU.mult).then_inc(hc_ready, 1)
                        if m == 0 and out:
                            gated(b - 1, 1)
                        if m == NS:
                            gated(b, 0)
                        if out and 2 <= m < 6:
                            out_read(b, 2 * (m - 2))
                            out_read(b, 2 * (m - 2) + 1)
                        if 6 <= m < 10:
                            gate_read(b, m - 6)
                        if prep and m == 9:
                            norm(b + 1)
                        if prep and m == 14:
                            norm_rows(b + 1)
                        if prep and m in (17, 18):
                            turn_read(b, (2 * (m - 17), 2 * (m - 17) + 1))
                        if prep and 19 <= m < 27:
                            (project_read if m % 2 else conv_read)(b, (m - 19) // 2)
                if out and not units:
                    gated(b - 1, 1)
                    for t in range(NT):
                        out_read(b, t)
                if prep:
                    split(b)

            steps(eng, step)


def program(nc, w, out):
    x1 = nc.dram_tensor("x1", (T, D), F32, kind="Internal").ap()
    rows_tab = nc.dram_tensor("rows_tab", (T, D + E), F32, kind="Internal").ap()
    list_tab = nc.dram_tensor("list_tab", (E, CAP), U32, kind="Internal").ap()
    with nc.cleanup_on_exit():
        recurrence_block(nc, w["x"], x1, w)
    with nc.cleanup_on_exit():
        experts_block(nc, "f_", x1, rows_tab, list_tab, w)
    with nc.cleanup_on_exit():
        state_space_block(nc, x1, out, w)
    with nc.cleanup_on_exit():
        experts_block(nc, "g_", out, rows_tab, list_tab, w)


def kernel(**inputs):
    import numpy as np
    import concourse.bacc as _bacc
    from concourse import mybir as _mybir
    from concourse.bass_utils import run_bass_kernel_spmd as _run

    a = {k: np.asarray(v) for k, v in inputs.items()}

    def g(name):
        return a["L0_" + name]

    def columns(v):
        return np.asarray(v).reshape(-1, 128).T

    cc = np.ascontiguousarray
    arrays = {
        "x": cc(g("attn_a_hidden_states").reshape(T, D)),
        "a_table": cc(np.concatenate([columns(g("attn_a_" + n)) for n in (
            "fc_r_b", "fc_i_b", "fc_b", "fc_gate_b", "mlp_gate_b", "mlp_fc_b", "norm_w", "norm2_w", "alpha")], axis=1)),
        "a_proj": cc(np.stack([g("attn_a_" + n).T for n in ("fc_r_w", "fc_i_w", "fc_w", "fc_gate_w")], axis=1)),
        "a_mlp": cc(np.stack([g("attn_a_mlp_gate_w").T, g("attn_a_mlp_fc_w").T])),
        "a_out": cc(g("attn_a_out_w").T),
        "a_out_b": cc(g("attn_a_out_b")),
        "f_router": cc(g("ffn_router_weight").T),
        "f_router_b": cc(g("ffn_router_bias")),
        "f_norm": cc(columns(g("ffn_norm_weight"))),
        "f_w1": cc(g("ffn_fc1_weight").transpose(0, 2, 1)),
        "f_w2": cc(g("ffn_fc2_weight").transpose(0, 2, 1)),
        "f_b1": cc(g("ffn_fc1_bias").reshape(E, KF, P).transpose(0, 2, 1)),
        "f_b2": cc(g("ffn_fc2_bias")),
        "b_in": cc(g("attn_b_W_in")),
        "b_x": cc(np.concatenate([g("attn_b_W_x")[:, DTR:]] * 3 + [g("attn_b_W_x")[:, :DTR]], axis=1)),
        "b_dt": cc(g("attn_b_W_dt")),
        "b_out": cc(g("attn_b_W_out")),
        "b_taps": cc(g("attn_b_conv_w")),
        "b_tab": cc(np.stack([columns(g("attn_b_" + n)) for n in ("conv_b", "b_dt", "D")], axis=1)),
        "b_a_log": cc(g("attn_b_A_log")),
    }
    nc = _bacc.Bacc("TRN2", target_bir_lowering=False, num_devices=1)
    aps = {}
    for name, v in arrays.items():
        aps[name] = nc.dram_tensor("in_" + name, v.shape, _mybir.dt.from_np(v.dtype), kind="ExternalInput").ap()
    out = nc.dram_tensor("out", (T, D), _mybir.dt.float32, kind="ExternalOutput").ap()
    program(nc, aps, out)
    r = _run(nc, [{"in_" + k: v for k, v in arrays.items()}], core_ids=[0])
    return np.asarray(r.results[0]["out"]).reshape(B, L, D)
```

```python
from contextlib import ExitStack

import concourse.bass as bass
from concourse import mybir

F32 = mybir.dt.float32
BF16 = mybir.dt.bfloat16
U32 = mybir.dt.uint32
ALU = mybir.AluOpType
ACT = mybir.ActivationFunctionType
AX_X = mybir.AxisListType.X

P = 128
D = 256
KD = D // P
B, L = 8, 1024
T = B * L
CH = 512
NCH = T // CH
TB = CH // P
H3 = 3 * D
KM = H3 // P
E, F, CAP = 16, 1024, T // 16
KF = F // P
DI, NS, DTR, KC = 2 * D, 16, D // 16, 4
KI = DI // P
LN_EPS, RMS_EPS, FFN_EPS = 1e-5, 1e-6, 1e-5


class Place:

    def __init__(self, pair, parity):
        self.pair, self.parity = pair, parity
        self.n = pair * 2 + parity
        self.fixed = isinstance(self.n, int)

    def shift(self, by):
        return Place(self.pair + (self.parity + by) // 2, (self.parity + by) % 2)

    def wait(self, eng, sem, count, least=1):
        if isinstance(count, int) and count < least:
            return
        eng.wait_ge(sem, count)


def wait_alone(eng, sem, count, passed):
    eng.wait_ge(sem, count)
    eng.sem_inc(passed, 1)



def recurrence_block(nc, x_in, x_out, w):
    x_rows = x_in.rearrange("(c t p) d -> c p t d", p=P, t=TB)
    y_rows = x_out.rearrange("(c t p) d -> c p t d", p=P, t=TB)
    col = {}
    at = 0
    for name, n in (("r", 2), ("i", 2), ("fc", 2), ("gate", 2), ("mg", KM), ("mf", KM),
                    ("norm", 2), ("norm2", 2), ("alpha", 2)):
        col[name] = at
        at += n
    ncols = at
    with ExitStack() as ctx:
        def sb(name, shape, dt=F32):
            return ctx.enter_context(nc.sbuf_tensor("a_" + name, shape, dt))

        def sem(name):
            return nc.alloc_semaphore("a_" + name)

        w_proj = sb("w_proj", [P, KD, 4, D])
        w_mlp = sb("w_mlp", [P, KD, 2, H3])
        w_out = sb("w_out", [P, KM, D])
        table = sb("table", [P, ncols])
        outb = sb("outb", [P, D])
        ident = sb("ident", [P, P])
        mean_w = sb("mean_w", [P, P])
        one = sb("one", [P, 1])
        eps6 = sb("eps6", [P, 1])
        sp = sb("sp", [P, 6, KD])
        xt = sb("xt", [P, 2, TB, D])
        u_rows = sb("u_rows", [P, TB, D])
        h_rows = sb("h_rows", [P, TB, D])
        xr = sb("xr", [P, TB, D])
        xb = sb("xb", [P, TB, D])
        yt = sb("yt", [P, 2, TB, D])
        stats = sb("stats", [P, TB, 6])
        mv = sb("mv", [P, TB, 2])
        var2 = sb("var2", [P, 2, TB])
        std2 = sb("std2", [P, 2, TB])
        inv2 = sb("inv2", [P, 2, TB])
        hscale = sb("hscale", [P, TB])
        u_cols = sb("u_cols", [P, 2, KD, CH])
        h_cols = sb("h_cols", [P, KD, CH])
        sig_r = sb("sig_r", [P, KD, CH])
        sig_i = sb("sig_i", [P, KD, CH])
        decay = sb("decay", [P, KD, CH])
        na2 = sb("na2", [P, KD, CH])
        beta = sb("beta", [P, KD, CH])
        drive = sb("drive", [P, KD, CH])
        state = sb("state", [P, 2, KD, CH])
        gate = sb("gate", [P, KD, CH])
        hs2 = sb("hs2", [P, 2, KD, CH])
        sq = sb("sq", [P, KD, CH])
        rms = sb("rms", [P, CH])
        inv_rms = sb("inv_rms", [P, CH])
        h2 = sb("h2", [P, KD, CH])
        g2 = sb("g2", [P, 2, CH])
        v = sb("v", [P, KM, CH])
        RING = 4
        ring = ctx.enter_context(nc.psum_tensor("a_ring", [P, RING, CH], F32))
        ps_out = ctx.enter_context(nc.psum_tensor("a_ps_out", [P, 2, CH], F32))
        ps_tr = ctx.enter_context(nc.psum_tensor("a_ps_tr", [P, 2, CH], F32))

        weights_in = sem("weights_in")
        setup = sem("setup")
        alpha_abs, alpha_exp, alpha_ln = sem("alpha_abs"), sem("alpha_exp"), sem("alpha_ln")
        consts = sem("consts")
        ident0 = sem("ident0")
        x_loaded = [sem("x_loaded0"), sem("x_loaded1")]
        xr_loaded = sem("xr_loaded")
        xb_ready = sem("xb_ready")
        t1_steps, t2_steps = sem("t1_steps"), sem("t2_steps")
        stats_ready, std_ready, rows_ready = sem("stats_ready"), sem("std_ready"), sem("rows_ready")
        tr_done, tr_read = sem("tr_done"), sem("tr_read")
        proj_done = sem("proj_done")
        ri_read, hs_read, g_read = sem("ri_read"), sem("hs_read"), sem("g_read")
        decay_ready, na2_ready, beta_ready = sem("decay_ready"), sem("na2_ready"), sem("beta_ready")
        drive_steps = sem("drive_steps")
        hs2_steps, hs2_ready, sq_ready = sem("hs2_steps"), sem("hs2_ready"), sem("sq_ready")
        norm_steps, stats_steps, dve_passed = sem("norm_steps"), sem("stats_steps"), sem("dve_passed")
        ms_done, rms_ready, inv_ready, h2_ready = sem("ms_done"), sem("rms_ready"), sem("inv_ready"), sem("h2_ready")
        mlp_done, mg_read, mf_read = sem("mlp_done"), sem("mg_read"), sem("mf_read")
        out_done, out_read = sem("out_done"), sem("out_read")
        y_stored = [sem("y_stored0"), sem("y_stored1")]
        NW = 6

        def pipeline(eng, stages):
            for k in range(-1, 4):
                stages(Place(k // 2, k % 2), k)
            with eng.Fori(2, NCH // 2 - 1) as i:
                stages(Place(i, 0), None)
                stages(Place(i, 1), None)
            for k in range(NCH - 2, NCH + 2):
                stages(Place(k // 2, k % 2), k)

        def has(k, stage):
            return k is None or 0 <= k + {"T": 1, "P": 0, "M": -1, "O": -2}[stage] < NCH

        block = ctx.enter_context(nc.Block())

        @block.sync
        def _(eng):
            eng.dma_start(table[:, :], w["a_table"]).then_inc(weights_in, 16)
            eng.dma_start(xt[:, 0], x_rows[0]).then_inc(x_loaded[0], 16)
            eng.dma_start(w_proj[:, :, :, :], w["a_proj"].rearrange("(k p) q d -> p k q d", p=P)).then_inc(weights_in, 16)
            eng.dma_start(outb[:, :], w["a_out_b"].partition_broadcast(P)).then_inc(weights_in, 16)
            eng.dma_start(xt[:, 1], x_rows[1]).then_inc(x_loaded[1], 16)
            for q in range(2):
                eng.dma_start(w_mlp[:, :, q, :], w["a_mlp"][q].rearrange("(k p) d -> p k d", p=P)).then_inc(weights_in, 16)
            eng.dma_start(w_out[:, :, :], w["a_out"].rearrange("(k p) d -> p k d", p=P)).then_inc(weights_in, 16)

            def stages(at, k):
                if has(k, "O"):
                    c = at.shift(-2)
                    c.wait(eng, xb_ready, c.n)
                    eng.dma_start(xr[:, :, :], x_rows[c.n]).then_inc(xr_loaded, 16)
                if has(k, "T") and (k is None or k + 3 < NCH):
                    nxt = at.shift(1)
                    eng.wait_ge(rows_ready, nxt.n + 1)
                    eng.dma_start(xt[:, nxt.parity], x_rows[at.shift(3).n]).then_inc(x_loaded[nxt.parity], 16)
                if has(k, "O"):
                    c = at.shift(-2)
                    eng.wait_ge(out_read, TB * c.n + TB)
                    eng.dma_start(y_rows[c.n], yt[:, c.parity]).then_inc(y_stored[c.parity], 16)

            for k in range(-1, 4):
                stages(Place(k // 2, k % 2), k)
            with eng.Fori(2, NCH // 2 - 2) as i:
                stages(Place(i, 0), None)
                stages(Place(i, 1), None)
            for k in range(NCH - 4, NCH + 2):
                stages(Place(k // 2, k % 2), k)
            for s in y_stored:
                eng.wait_ge(s, 16 * (NCH // 2))

        @block.gpsimd
        def _(eng):
            eng.memset(mean_w[:, :], 1.0 / D).then_inc(consts, 1)
            eng.memset(one[:, :], 1.0).then_inc(consts, 1)
            eng.memset(eps6[:, :], RMS_EPS).then_inc(consts, 1)
            eng.memset(ident[:, :], 0.0).then_inc(ident0, 1)
            eng.wait_ge(ident0, 1)
            eng.affine_select(out=ident[:, :], in_=ident[:, :], compare_op=ALU.not_equal, fill=1.0,
                              base=0, pattern=[[-1, P]], channel_multiplier=1).then_inc(consts, 1)
            eng.wait_ge(weights_in, 16 * NW)

            def stages(at, k):
                if has(k, "O"):
                    c = at.shift(-2)
                    eng.wait_ge(xr_loaded, 16 * c.n + 16)
                    c.wait(eng, out_read, TB * c.n)
                    eng.tensor_tensor(xb[:, :, :], xr[:, :, :],
                                      outb[:, :].unsqueeze(1).broadcast_to([P, TB, D]), ALU.add).then_inc(xb_ready, 1)
                if has(k, "P"):
                    eng.wait_ge(hs2_ready, at.n + 1)
                    eng.tensor_tensor(sq[:, :, :], hs2[:, at.parity], hs2[:, at.parity], ALU.mult).then_inc(sq_ready, 1)

            pipeline(eng, stages)

        @block.scalar
        def _(eng):
            eng.wait_ge(weights_in, 16 * NW)
            eng.wait_ge(consts, 4)
            eng.activation(sp[:, 0], table[:, col["alpha"]:col["alpha"] + 2], ACT.Abs).then_inc(alpha_abs, 1)
            eng.wait_ge(alpha_abs, 1)
            eng.activation(sp[:, 1], sp[:, 0], ACT.Exp, scale=-1.0).then_inc(alpha_exp, 1)
            eng.wait_ge(alpha_exp, 1)
            eng.activation(sp[:, 2], sp[:, 1], ACT.Ln, bias=one[:, 0:1]).then_inc(alpha_ln, 1)
            eng.wait_ge(setup, 3 + KD)

            def stages(at, k):
                if has(k, "P"):
                    at.wait(eng, hs_read, KD * at.n)
                    for j, (dst, name) in enumerate(((sig_r, "r"), (sig_r, "r"), (sig_i, "i"), (sig_i, "i"))):
                        eng.wait_ge(proj_done, 8 * at.n + j + 1)
                        half = j % 2
                        bias = table[:, col[name] + half:col[name] + half + 1]
                        eng.activation(dst[:, half], ring[:, j % RING], ACT.Sigmoid, bias=bias).then_inc(ri_read, 1)
                    at.wait(eng, drive_steps, 3 * at.n)
                    eng.wait_ge(ri_read, 4 * at.n + 2)
                    for half in range(KD):
                        eng.activation(decay[:, half], sig_r[:, half], ACT.Exp, scale=sp[:, 5, half:half + 1]).then_inc(decay_ready, 1)
                if has(k, "M"):
                    c = at.shift(-1)
                    eng.wait_ge(ms_done, c.n + 1)
                    c.wait(eng, inv_ready, c.n)
                    eng.activation(rms[:, :], ps_tr[:, 1], ACT.Sqrt, bias=eps6[:, 0:1]).then_inc(rms_ready, 1)
                if has(k, "T"):
                    c = at.shift(1)
                    eng.wait_ge(stats_ready, c.n + 1)
                    eng.activation(std2[:, :, :], var2[:, :, :], ACT.Sqrt).then_inc(std_ready, 1)
                if has(k, "P"):
                    eng.wait_ge(na2_ready, at.n + 1)
                    eng.activation(beta[:, :, :], na2[:, :, :], ACT.Sqrt, bias=one[:, 0:1]).then_inc(beta_ready, 1)
                    at.wait(eng, hs2_ready, at.n)
                    for half in range(KD):
                        eng.wait_ge(proj_done, 8 * at.n + 7 + half)
                        bias = table[:, col["gate"] + half:col["gate"] + half + 1]
                        eng.activation(gate[:, half], ring[:, (6 + half) % RING], ACT.Gelu, bias=bias).then_inc(g_read, 1)
                if has(k, "M"):
                    c = at.shift(-1)
                    for j in range(KM):
                        eng.wait_ge(mlp_done, 2 * KM * c.n + 2 * j + 1)
                        if j >= 2 or not (c.fixed and c.n == 0):
                            eng.wait_ge(mf_read, KM * c.n + j - 1)
                        bias = table[:, col["mg"] + j:col["mg"] + j + 1]
                        eng.activation(g2[:, j % 2], ring[:, (8 + 2 * j) % RING], ACT.Gelu, bias=bias).then_inc(mg_read, 1)

            pipeline(eng, stages)

        @block.tensor
        def _(eng):
            eng.wait_ge(setup, 3 + KD)
            eng.wait_ge(consts, 4)

            def stages(at, k):
                if has(k, "P"):
                    eng.wait_ge(tr_read, 4 * at.n + 4)
                    prev = at.shift(-2)
                    for j in range(8):
                        if j < RING:
                            s = 20 + j - RING - 8
                            at.wait(eng, mf_read if s % 2 else mg_read, KM * prev.n + s // 2 + 1)
                        else:
                            eng.wait_ge(ri_read, 4 * at.n + j - RING + 1)
                        for kb in range(KD):
                            mm = eng.matmul(ring[:, j % RING], w_proj[:, kb, j // 2, (j % 2) * P:(j % 2) * P + P],
                                            h_cols[:, kb], start=kb == 0, stop=kb == KD - 1)
                        mm.then_inc(proj_done, 1)
                if has(k, "O"):
                    c = at.shift(-2)
                    eng.wait_ge(mf_read, KM * c.n + KM)
                    for t in range(TB):
                        if t >= 2 or not (c.fixed and c.n == 0):
                            eng.wait_ge(out_read, TB * c.n + t - 1)
                        dst = ps_out[:, t % 2, 0:D]
                        for j in range(KM):
                            eng.matmul(dst, v[:, j, t * P:t * P + P], w_out[:, j], start=j == 0, stop=False,
                                       skip_group_check=True)
                        for kb in range(KD):
                            mm = eng.matmul(dst[:, kb * P:kb * P + P], hs2[:, c.parity, kb, t * P:t * P + P],
                                            ident[:, :], start=False, stop=True, skip_group_check=True)
                        mm.then_inc(out_done, 1)
                if has(k, "T"):
                    c = at.shift(1)
                    eng.wait_ge(rows_ready, c.n + 1)
                    for q in range(4):
                        src = (u_rows, h_rows)[q // 2]
                        if q < 2:
                            c.wait(eng, tr_read, 4 * c.n)
                            if q == 1:
                                last = at.shift(-1)
                                last.wait(eng, rms_ready, last.n + 1)
                        else:
                            eng.wait_ge(tr_read, 4 * c.n + q - 1)
                        for t in range(TB):
                            mm = eng.transpose(ps_tr[:, q % 2, t * P:t * P + P], src[:, t, (q % 2) * P:(q % 2) * P + P],
                                               ident[:, :])
                        mm.then_inc(tr_done, 1)
                if has(k, "M"):
                    c = at.shift(-1)
                    eng.wait_ge(h2_ready, c.n + 1)
                    for s in range(8, 20):
                        j = (s - 8) // 2
                        if s - RING >= 8:
                            q = s - RING - 8
                            eng.wait_ge(mf_read if q % 2 else mg_read, KM * c.n + q // 2 + 1)
                        elif has(k, "P"):
                            q = s - RING
                            if q < 4:
                                eng.wait_ge(ri_read, 4 * at.n + q + 1)
                            elif q < 6:
                                eng.wait_ge(hs_read, KD * at.n + q - 3)
                            else:
                                eng.wait_ge(g_read, KD * at.n + q - 5)
                        elif s == 8:
                            eng.wait_ge(mf_read, KM * c.n)
                            eng.wait_ge(mg_read, KM * c.n)
                            eng.wait_ge(g_read, KD * NCH)
                        for kb in range(KD):
                            mm = eng.matmul(ring[:, s % RING], w_mlp[:, kb, s % 2, j * P:j * P + P], h2[:, kb],
                                            start=kb == 0, stop=kb == KD - 1)
                        mm.then_inc(mlp_done, 1)
                if has(k, "P"):
                    eng.wait_ge(sq_ready, at.n + 1)
                    if has(k, "T"):
                        eng.wait_ge(tr_read, 4 * at.n + 8)
                    for kb in range(KD):
                        mm = eng.matmul(ps_tr[:, 1], mean_w[:, :], sq[:, kb], start=kb == 0, stop=kb == KD - 1)
                    mm.then_inc(ms_done, 1)

            pipeline(eng, stages)

        @block.vector
        def _(eng):
            eng.wait_ge(weights_in, 16 * NW)
            eng.tensor_scalar(sp[:, 3], table[:, col["alpha"]:col["alpha"] + 2], 0.0, None, ALU.max).then_inc(setup, 1)
            eng.wait_ge(alpha_ln, 1)
            eng.wait_ge(setup, 1)
            eng.tensor_tensor(sp[:, 4], sp[:, 3], sp[:, 2], ALU.add).then_inc(setup, 1)
            eng.wait_ge(setup, 2)
            eng.tensor_scalar(sp[:, 5], sp[:, 4], -8.0, None, ALU.mult).then_inc(setup, 1)
            for kb in range(KD):
                n1, n2 = col["norm"] + kb, col["norm2"] + kb
                eng.tensor_scalar(w_proj[:, kb], w_proj[:, kb], table[:, n1:n1 + 1], None, ALU.mult)
                eng.tensor_scalar(w_mlp[:, kb], w_mlp[:, kb], table[:, n2:n2 + 1], None, ALU.mult).then_inc(setup, 1)
            
            def stats_stage(c):
                steps = [0]

                def link(ins):
                    steps[0] += 1
                    ins.then_inc(t1_steps, 1)
                    eng.wait_ge(t1_steps, 3 * c.n + steps[0])

                eng.wait_ge(x_loaded[c.parity], 16 * c.pair + 16)
                for t in range(TB):
                    ins = eng.bn_stats(stats[:, t], xt[:, c.parity, t])
                ins.then_inc(stats_steps, 1)
                wait_alone(eng, stats_steps, c.n + 1, dve_passed)
                for t in range(TB):
                    ins = eng.bn_aggr(mv[:, t], stats[:, t])
                link(ins)
                link(eng.tensor_scalar(var2[:, 0], mv[:, :, 1], LN_EPS, None, ALU.add))
                link(eng.reciprocal(inv2[:, 0], var2[:, 0]))
                eng.tensor_tensor(inv2[:, 1], inv2[:, 0], mv[:, :, 1], ALU.mult).then_inc(norm_steps, 1)
                eng.wait_ge(norm_steps, c.n + 1)
                eng.tensor_scalar(var2[:, 1], inv2[:, 1], RMS_EPS, None, ALU.add).then_inc(stats_ready, 1)

            def rows_stage(c):
                eng.wait_ge(std_ready, c.n + 1)
                eng.reciprocal(inv2[:, :, :], std2[:, :, :]).then_inc(t2_steps, 1)
                eng.wait_ge(t2_steps, 2 * c.n + 1)
                eng.tensor_tensor(hscale[:, :], inv2[:, 0], inv2[:, 1], ALU.mult).then_inc(t2_steps, 1)
                eng.wait_ge(t2_steps, 2 * c.n + 2)
                c.wait(eng, tr_done, 4 * c.n)
                for t in range(TB):
                    eng.tensor_scalar(u_rows[:, t], xt[:, c.parity, t], mv[:, t, 0:1], inv2[:, 0, t:t + 1],
                                      ALU.subtract, ALU.mult)
                    ins = eng.tensor_scalar(h_rows[:, t], xt[:, c.parity, t], mv[:, t, 0:1], hscale[:, t:t + 1],
                                            ALU.subtract, ALU.mult)
                ins.then_inc(rows_ready, 1)

            def turn_stage(c):
                for q in range(4):
                    eng.wait_ge(tr_done, 4 * c.n + q + 1)
                    dst = u_cols[:, c.parity, q] if q < 2 else h_cols[:, q - 2]
                    eng.tensor_copy(dst, ps_tr[:, q % 2]).then_inc(tr_read, 1)

            def out_read_stage(c, t):
                eng.wait_ge(out_done, TB * c.n + t + 1)
                if t == 0:
                    eng.wait_ge(xb_ready, c.n + 1)
                    c.wait(eng, y_stored[c.parity], 16 * c.pair)
                eng.tensor_tensor(yt[:, c.parity, t], ps_out[:, t % 2, 0:D], xb[:, t], ALU.add).then_inc(out_read, 1)

            def stages(at, k):
                if has(k, "P"):
                    for half in range(KD):
                        eng.wait_ge(proj_done, 8 * at.n + 5 + half)
                        eng.wait_ge(ri_read, 4 * at.n + 3 + half)
                        bias = table[:, col["fc"] + half:col["fc"] + half + 1]
                        eng.scalar_tensor_tensor(drive[:, half], ring[:, (4 + half) % RING], bias, sig_i[:, half],
                                                 ALU.add, ALU.mult).then_inc(hs_read, 1)
                if has(k, "T"):
                    stats_stage(at.shift(1))
                if has(k, "P"):
                    eng.wait_ge(decay_ready, KD * at.n + KD)
                    at.wait(eng, beta_ready, at.n)
                    eng.scalar_tensor_tensor(na2[:, :, :], decay[:, :, :], -1.0, decay[:, :, :],
                                             ALU.mult, ALU.mult).then_inc(na2_ready, 1)
                if has(k, "O"):
                    out_read_stage(at.shift(-2), 0)
                if has(k, "M"):
                    c = at.shift(-1)
                    eng.wait_ge(rms_ready, c.n + 1)
                    eng.reciprocal(inv_rms[:, :], rms[:, :]).then_inc(inv_ready, 1)
                    eng.wait_ge(inv_ready, c.n + 1)
                    eng.tensor_tensor(h2[:, :, :], hs2[:, c.parity], inv_rms[:, :].unsqueeze(1).broadcast_to([P, KD, CH]),
                                      ALU.mult).then_inc(h2_ready, 1)
                if has(k, "O"):
                    out_read_stage(at.shift(-2), 1)
                if has(k, "T"):
                    rows_stage(at.shift(1))
                if has(k, "O"):
                    out_read_stage(at.shift(-2), 2)
                if has(k, "P"):
                    eng.wait_ge(beta_ready, at.n + 1)
                    eng.wait_ge(hs_read, KD * at.n + KD)
                    eng.tensor_tensor(drive[:, :, :], drive[:, :, :], beta[:, :, :], ALU.mult).then_inc(drive_steps, 1)
                    eng.wait_ge(drive_steps, 3 * at.n + 1)
                    for half in range(KD):
                        initial = 0.0 if at.parity == 0 else state[:, 0, half, CH - 1:CH]
                        eng.tensor_tensor_scan(state[:, at.parity, half], decay[:, half], drive[:, half], initial,
                                               ALU.mult, ALU.add).then_inc(drive_steps, 1)
                if has(k, "O"):
                    out_read_stage(at.shift(-2), 3)
                if has(k, "T"):
                    turn_stage(at.shift(1))
                if has(k, "P"):
                    eng.wait_ge(g_read, KD * at.n + KD)
                    eng.wait_ge(drive_steps, 3 * at.n + 3)
                    eng.tensor_tensor(gate[:, :, :], state[:, at.parity], gate[:, :, :], ALU.mult).then_inc(hs2_steps, 1)
                    eng.wait_ge(hs2_steps, at.n + 1)
                    eng.tensor_tensor(hs2[:, at.parity], gate[:, :, :], u_cols[:, at.parity], ALU.add).then_inc(hs2_ready, 1)
                if has(k, "M"):
                    c = at.shift(-1)
                    for j in range(KM):
                        eng.wait_ge(mlp_done, 2 * KM * c.n + 2 * j + 2)
                        eng.wait_ge(mg_read, KM * c.n + j + 1)
                        bias = table[:, col["mf"] + j:col["mf"] + j + 1]
                        eng.scalar_tensor_tensor(v[:, j], ring[:, (9 + 2 * j) % RING], bias, g2[:, j % 2],
                                                 ALU.add, ALU.mult).then_inc(mf_read, 1)

            pipeline(eng, stages)


def experts_block(nc, tag, x_tab, rows_tab, list_tab, w):
    NT = T // P
    NJ = P // E
    NQ = NT // NJ
    SPAN = NQ * P
    LO, HI = 32, CAP // 32
    SLOTS = CAP // P
    RW = D + E
    x_chunks = x_tab.rearrange("(c t p) d -> c p t d", p=P, t=TB)
    rows_chunks = rows_tab.rearrange("(c t p) d -> c p t d", p=P, t=TB)
    with ExitStack() as ctx:
        def sb(name, shape, dt=F32):
            return ctx.enter_context(nc.sbuf_tensor(tag + name, shape, dt))

        def sem(name):
            return nc.alloc_semaphore(tag + name)

        def ps(name, shape):
            return ctx.enter_context(nc.psum_tensor(tag + name, shape, F32))

        ident = sb("ident", [P, P])
        xt = sb("xt", [P, 2, TB, D])
        xn = sb("xn", [P, 2, TB, D])
        stats = sb("stats", [P, TB, 6])
        mv = sb("mv", [P, TB, 2])
        var2 = sb("var2", [P, 2, TB])
        std2 = sb("std2", [P, 2, TB])
        inv2 = sb("inv2", [P, 2, TB])
        hscale = sb("hscale", [P, TB])
        xcols = sb("xcols", [P, 2, KD, CH])
        w_router = sb("w_router", [P, KD, E])
        b_router = sb("b_router", [P, E])
        normw = sb("normw", [P, KD])
        logits = sb("logits", [P, NT, E])
        probs = sb("probs", [P, NT, E])
        tile_max = sb("tile_max", [P, NT])
        tile_sum = sb("tile_sum", [P, NT])
        by_e = sb("by_e", [P, SPAN])
        signed = sb("signed", [P, SPAN])
        flags = sb("flags", [P, SPAN])
        above = sb("above", [P, SPAN])
        equal = sb("equal", [P, SPAN])
        running = sb("running", [P, SPAN])
        ones = sb("ones", [P, SPAN])
        slot1 = sb("slot1", [P, SPAN])
        same_e = sb("same_e", [P, P])
        before = sb("before", [P, P])
        col_e = sb("col_e", [P, P])
        col_j = sb("col_j", [P, P])
        row_e = sb("row_e", [P, 1])
        row_j = sb("row_j", [P, 1])
        row_n = sb("row_n", [P, 1])
        iota_i = sb("iota_i", [P, LO, NT], U32)
        row_i = sb("row_i", [P, 3], U32)
        count = sb("count", [P, 4])
        sign = sb("sign", [P, 4])
        zero1 = sb("zero1", [P, 1])
        bits = sb("bits", [P, 4], U32)
        slot_i = sb("slot_i", [P, NQ, NJ, E], mybir.dt.int32)
        digit_i = sb("digit_i", [P, 2, NQ, NJ, E], mybir.dt.int32)
        lo_b = sb("lo_b", [P, E, NT], BF16)
        hi_b = sb("hi_b", [P, E, NT], BF16)
        taken = sb("taken", [P, NQ, NJ, E])
        part = sb("part", [P, NT, E])
        shares = sb("shares", [P, NJ, NQ, E])
        iota_lo = sb("iota_lo", [P, LO, NT], BF16)
        iota_hi = sb("iota_hi", [P, HI, NT], BF16)
        tile_no = sb("tile_no", [P, NT], BF16)
        hot_lo = sb("hot_lo", [P, 2, LO, NT], BF16)
        hot_hi = sb("hot_hi", [P, 2, HI, NT], BF16)
        values = sb("values", [P, 2, 2, HI, NT], BF16)
        part_sum = sb("part_sum", [LO, 2 * HI])
        lists = sb("lists", [LO, E, HI], U32)
        slots = sb("slots", [P, E, SLOTS], U32)
        w1 = sb("w1", [P, 2, KD, F])
        w2 = sb("w2", [P, 2, KF, D])
        b1 = sb("b1", [P, 2, KF])
        b2 = sb("b2", [P, 2, D])
        gather_at = sb("gather_at", [P, 2, SLOTS], U32)
        scatter_at = sb("scatter_at", [P, 2, SLOTS], U32)
        rows = sb("rows", [P, 2, SLOTS, RW])
        share = sb("share", [P, 2, SLOTS])
        xe = sb("xe", [P, KD, CAP])
        hid = sb("hid", [P, KF, CAP])
        ysum = sb("ysum", [P, SLOTS, D])
        ye = sb("ye", [P, 2, SLOTS, D])
        RING = 4
        ring = ps("ring", [P, RING, CH])
        ps_tr = ps("ps_tr", [P, 2, CH])
        ps_y = ps("ps_y", [P, 2, CH])

        weights_in, consts, ident0 = sem("weights_in"), sem("consts"), sem("ident0")
        consts2 = sem("consts2")
        x_loaded = [sem("x_loaded0"), sem("x_loaded1")]
        rows_stored = [sem("rows_stored0"), sem("rows_stored1")]
        stats_steps, t_steps, passed = sem("stats_steps"), sem("t_steps"), sem("passed")
        stats_ready, std_ready, rows_ready = sem("stats_ready"), sem("std_ready"), sem("rows_ready")
        tr_done, tr_read, logits_done, logits_read = sem("tr_done"), sem("tr_read"), sem("logits_done"), sem("logits_read")
        soft, exp_in, exp_done = sem("soft"), sem("exp_in"), sem("exp_done")
        by_e_done, counts_in, counts_out = sem("by_e_done"), sem("counts_in"), sem("counts_out")
        sel = sem("sel")
        slot_done, tokens_done = sem("slot_done"), sem("tokens_done")
        shares_ready, shares_stored = sem("shares_ready"), sem("shares_stored")
        hot_hi_ready, hot_lo_ready, list_done, list_read = sem("hot_hi_ready"), sem("hot_lo_ready"), sem("list_done"), sem("list_read")
        row_values_ready, tile_values_ready = sem("row_values_ready"), sem("tile_values_ready")
        list_stored, slots_in = sem("list_stored"), sem("slots_in")
        w_in = [sem("w_in0"), sem("w_in1")]
        gather_idx, scatter_idx = sem("gather_idx"), sem("scatter_idx")
        gathered, scattered = [sem("gathered0"), sem("gathered1")], sem("scattered")
        etr_done, etr_read, share_ready = sem("etr_done"), sem("etr_read"), sem("share_ready")
        hid_done, hid_ready = sem("hid_done"), sem("hid_ready")
        y_done, y_read, y_ready = sem("y_done"), sem("y_read"), sem("y_ready")
        pool_passed = sem("pool_passed")
        list_sum = sem("list_sum")
        NCONST = 9

        def experts(eng, stages):
            for k in range(-2, 2):
                stages(Place(k // 2, k % 2), k)
            with eng.Fori(1, E // 2 - 1) as i:
                stages(Place(i, 0), None)
                stages(Place(i, 1), None)
            for k in range(E - 2, E):
                stages(Place(k // 2, k % 2), k)

        def router_steps(eng, step):
            for k in range(-1, 4):
                step(Place(k // 2, k % 2), k)
            with eng.Fori(2, NCH // 2 - 1) as i:
                step(Place(i, 0), None)
                step(Place(i, 1), None)
            for k in range(NCH - 2, NCH + 2):
                step(Place(k // 2, k % 2), k)

        def in_router(k, ahead):
            return k is None or 0 <= k + ahead < NCH

        def has(k, ahead):
            return k is None or 0 <= k + ahead < E

        block = ctx.enter_context(nc.Block())

        @block.sync
        def _(eng):
            eng.dma_start(w_router[:, :, :], w["f_router"].rearrange("(k p) e -> p k e", p=P)).then_inc(weights_in, 16)
            eng.dma_start(b_router[:, :], w["f_router_b"].partition_broadcast(P)).then_inc(weights_in, 16)
            eng.dma_start(normw[:, :], w["f_norm"]).then_inc(weights_in, 16)
            for c in range(2):
                eng.dma_start(xt[:, c], x_chunks[c]).then_inc(x_loaded[c], 16)

            def router(c, more):
                eng.wait_ge(rows_ready, c.n + 1)
                eng.dma_start(rows_chunks[c.n][:, :, 0:D], xn[:, c.parity]).then_inc(rows_stored[c.parity], 16)
                if more:
                    eng.dma_start(xt[:, c.parity], x_chunks[c.shift(2).n]).then_inc(x_loaded[c.parity], 16)

            with eng.Fori(0, NCH // 2 - 1) as i:
                router(Place(i, 0), True)
                router(Place(i, 1), True)
            router(Place(NCH // 2 - 1, 0), False)
            router(Place(NCH // 2 - 1, 1), False)
            eng.wait_ge(shares_ready, 1)
            eng.dma_start(rows_tab.rearrange("(t p) d -> p t d", p=P)[:, :, D:RW],
                          shares[:, :, :, :].rearrange("p j q e -> p (j q) e")).then_inc(shares_stored, 16)
            eng.wait_ge(list_read, E)
            eng.dma_start(list_tab.rearrange("e (l h) -> l e h", l=LO), lists[:, :, :]).then_inc(list_stored, 16)
            eng.wait_ge(list_stored, 16)
            eng.dma_start(slots[:, :, :], list_tab.rearrange("e (p s) -> p e s", p=P)).then_inc(slots_in, 16)

            def stages(at, k):
                if has(k, 2):
                    c = at.shift(2)
                    if k is None or k >= 0:
                        eng.wait_ge(y_read, SLOTS * at.n + SLOTS)
                    s = w_in[c.parity]
                    eng.dma_start(w1[:, c.parity], w["f_w1"][c.n].rearrange("(k p) f -> p k f", p=P)).then_inc(s, 16)
                    eng.dma_start(b1[:, c.parity], w["f_b1"][c.n]).then_inc(s, 16)
                    eng.dma_start(w2[:, c.parity], w["f_w2"][c.n].rearrange("(k p) d -> p k d", p=P)).then_inc(s, 16)
                    eng.dma_start(b2[:, c.parity], w["f_b2"][c.n].partition_broadcast(P)).then_inc(s, 16)

            experts(eng, stages)

        @block.gpsimd
        def _(eng):
            eng.memset(ident[:, :], 0.0).then_inc(ident0, 1)
            eng.wait_ge(ident0, 1)
            eng.affine_select(out=ident[:, :], in_=ident[:, :], compare_op=ALU.not_equal, fill=1.0,
                              base=0, pattern=[[-1, P]], channel_multiplier=1).then_inc(consts, 1)
            eng.memset(zero1[:, :], 0.0).then_inc(consts, 1)
            eng.iota(row_i[:, 0:1], [[0, 1]], base=0, channel_multiplier=1).then_inc(consts, 1)
            eng.iota(iota_i[:, :, :], [[1, LO], [0, NT]], base=0, channel_multiplier=0).then_inc(consts, 1)
            eng.iota(col_e[:, :].bitcast(U32), [[0, NJ], [1, E]], base=0, channel_multiplier=0).then_inc(consts, 1)
            eng.iota(col_j[:, :].bitcast(U32), [[1, NJ], [0, E]], base=0, channel_multiplier=0).then_inc(consts, 1)
            eng.iota(bits[:, 0:4], [[0, 4]], base=0, channel_multiplier=0).then_inc(consts, 1)
            eng.iota(slot_i[:, 0, 0:4, :].bitcast(U32), [[1, NQ], [NQ, NJ]], base=0, channel_multiplier=0).then_inc(consts, 1)
            eng.memset(ones[:, :], 1.0).then_inc(consts, 1)

            def stages(at, k):
                if has(k, 2):
                    c = at.shift(2)
                    if k is None or k >= 0:
                        eng.wait_ge(etr_done, KD * at.n + KD)
                        eng.sem_inc(pool_passed, 1)
                        wait_alone(eng, share_ready, at.n + 1, pool_passed)
                    eng.tensor_copy(gather_at[:, c.parity], slots[:, c.n]).then_inc(gather_idx, 1)
                    wait_alone(eng, gather_idx, c.n + 1, pool_passed)
                    for s in range(SLOTS):
                        eng.indirect_dma_start(
                            out=rows[:, c.parity, s], out_offset=None, in_=rows_tab,
                            in_offset=bass.IndirectOffsetOnAxis(ap=gather_at[:, c.parity, s:s + 1], axis=0),
                        ).then_inc(gathered[c.parity], 16)
                if has(k, 0):
                    if k is None or k >= 1:
                        wait_alone(eng, scattered, 16 * SLOTS * at.n, pool_passed)
                    eng.tensor_copy(scatter_at[:, at.parity], slots[:, at.n]).then_inc(scatter_idx, 1)
                    wait_alone(eng, scatter_idx, at.n + 1, pool_passed)
                    for s in range(SLOTS):
                        wait_alone(eng, y_ready, SLOTS * at.n + s + 1, pool_passed)
                        eng.indirect_dma_start(
                            out=x_tab, out_offset=bass.IndirectOffsetOnAxis(ap=scatter_at[:, at.parity, s:s + 1], axis=0),
                            in_=ye[:, at.parity, s], in_offset=None, compute_op=ALU.add,
                        ).then_inc(scattered, 16)

            def tile_values(c):
                eng.wait_ge(hot_hi_ready, c.n + 1)
                eng.tensor_tensor(values[:, c.parity, 1], hot_hi[:, c.parity],
                                  tile_no[:, :].unsqueeze(1).broadcast_to([P, HI, NT]), ALU.mult).then_inc(tile_values_ready, 1)

            with eng.Fori(0, E // 2) as i:
                tile_values(Place(i, 0))
                tile_values(Place(i, 1))
            eng.wait_ge(slots_in, 16)
            eng.wait_ge(shares_stored, 16)
            for s in rows_stored:
                eng.wait_ge(s, 16 * (NCH // 2))
            experts(eng, stages)
            eng.wait_ge(scattered, 16 * SLOTS * E)

        @block.scalar
        def _(eng):
            def router(c):
                eng.wait_ge(stats_ready, c.n + 1)
                eng.activation(std2[:, :, :], var2[:, :, :], ACT.Sqrt).then_inc(std_ready, 1)

            with eng.Fori(0, NCH // 2) as i:
                router(Place(i, 0))
                router(Place(i, 1))
            eng.wait_ge(exp_in, 1)
            eng.activation(probs[:, :, :], probs[:, :, :], ACT.Exp).then_inc(exp_done, 1)

            def row_values(c):
                eng.wait_ge(hot_hi_ready, c.n + 1)
                eng.activation(values[:, c.parity, 0], hot_hi[:, c.parity], ACT.Copy, scale=row_n[:, 0:1]).then_inc(row_values_ready, 1)

            with eng.Fori(0, E // 2) as i:
                row_values(Place(i, 0))
                row_values(Place(i, 1))

            def stages(at, k):
                if has(k, 0):
                    eng.wait_ge(w_in[at.parity], 64 * at.pair + 64)
                    for j in range(KF):
                        eng.wait_ge(hid_done, KF * at.n + j + 1)
                        eng.activation(hid[:, j], ring[:, j % RING], ACT.Gelu, bias=b1[:, at.parity, j:j + 1]).then_inc(hid_ready, 1)

            experts(eng, stages)

        @block.tensor
        def _(eng):
            eng.wait_ge(consts, NCONST)
            eng.wait_ge(weights_in, 16 * 3)

            def turn(c):
                eng.wait_ge(rows_ready, c.n + 1)
                for q in range(KD):
                    if not (c.fixed and c.n == 0):
                        eng.wait_ge(tr_read, KD * (c.n - 1) + q + 1)
                    for t in range(TB):
                        mm = eng.transpose(ps_tr[:, q, t * P:t * P + P], xn[:, c.parity, t, q * P:q * P + P], ident[:, :])
                    mm.then_inc(tr_done, 1)

            def route(c):
                eng.wait_ge(tr_read, KD * c.n + KD)
                c.wait(eng, logits_read, c.n - 1)
                for t in range(TB):
                    for kb in range(KD):
                        mm = eng.matmul(ps_y[:, c.parity, t * E:t * E + E], xcols[:, c.parity, kb, t * P:t * P + P],
                                        w_router[:, kb], start=kb == 0, stop=kb == KD - 1)
                mm.then_inc(logits_done, 1)

            def router(at, k):
                if in_router(k, 0):
                    turn(at)
                if in_router(k, -1):
                    route(at.shift(-1))

            router_steps(eng, router)

            eng.wait_ge(logits_read, NCH)
            for q in range(NQ):
                mm = eng.transpose(ring[:, q // 4, (q % 4) * P:(q % 4) * P + P], logits[:, q * NJ:q * NJ + NJ].rearrange("p j e -> p (j e)"), ident[:, :])
            mm.then_inc(by_e_done, 1)
            for n in range(1 + 31 + 1):
                eng.wait_ge(counts_in, n + 1)
                eng.matmul(ring[:, 2, 0:1], same_e[:, :], count[:, n % 2:n % 2 + 1], start=True, stop=True).then_inc(counts_out, 1)
            for n in range(2):
                eng.wait_ge(counts_in, 34 + n)
                eng.matmul(ring[:, 3, 0:1], before[:, :], running[:, SPAN - 1:SPAN], start=True, stop=True).then_inc(counts_out, 1)
            eng.wait_ge(slot_done, 1)
            for q in range(NQ):
                mm = eng.transpose(ring[:, q // 4, (q % 4) * P:(q % 4) * P + P], slot1[:, q * P:q * P + P], ident[:, :])
            mm.then_inc(tokens_done, 1)

            def listed(c):
                eng.wait_ge(hot_lo_ready, c.n + 1)
                eng.wait_ge(row_values_ready, c.n + 1)
                eng.wait_ge(tile_values_ready, c.n + 1)
                c.wait(eng, list_read, c.n - 1)
                for t in range(NT):
                    mm = eng.matmul(ps_y[0:LO, c.parity, 0:2 * HI], hot_lo[:, c.parity, :, t],
                                    values[:, c.parity, :, :, t].rearrange("p v h -> p (v h)"),
                                    start=t == 0, stop=t == NT - 1)
                mm.then_inc(list_done, 1)

            for n in range(2):
                listed(Place(0, n))
            with eng.Fori(1, E // 2) as i:
                for n in range(2):
                    listed(Place(i, n))

            eng.wait_ge(list_read, E)

            def stages(at, k):
                if has(k, 0):
                    eng.wait_ge(w_in[at.parity], 64 * at.pair + 64)
                    eng.wait_ge(etr_read, KD * at.n + KD)
                    for j in range(KF):
                        if j >= RING or not (at.fixed and at.n == 0):
                            eng.wait_ge(hid_ready, KF * at.n + j - RING + 1)
                        for kb in range(KD):
                            mm = eng.matmul(ring[:, j % RING], w1[:, at.parity, kb, j * P:j * P + P], xe[:, kb],
                                            start=kb == 0, stop=kb == KD - 1)
                        mm.then_inc(hid_done, 1)
                if has(k, 1) and (k is None or k >= -1):
                    c = at.shift(1)
                    eng.wait_ge(gathered[c.parity], 16 * SLOTS * c.pair + 16 * SLOTS)
                    if not (c.fixed and c.n == 0):
                        eng.wait_ge(etr_read, KD * c.n)
                    for q in range(KD):
                        for s in range(SLOTS):
                            mm = eng.transpose(ps_tr[:, q, s * P:s * P + P], rows[:, c.parity, s, q * P:q * P + P], ident[:, :])
                        mm.then_inc(etr_done, 1)
                if has(k, 0):
                    for s in range(SLOTS):
                        if s >= 2 or not (at.fixed and at.n == 0):
                            eng.wait_ge(y_read, SLOTS * at.n + s - 1)
                        for j in range(KF):
                            if s == 0:
                                eng.wait_ge(hid_ready, KF * at.n + j + 1)
                            mm = eng.matmul(ps_y[:, s % 2, 0:D], hid[:, j, s * P:s * P + P], w2[:, at.parity, j],
                                            start=j == 0, stop=j == KF - 1)
                        mm.then_inc(y_done, 1)

            experts(eng, stages)

        @block.vector
        def _(eng):
            n = [0]

            def link(ins, s=None):
                n[0] += 1
                ins.then_inc(sel, 1)
                eng.wait_ge(sel, n[0])

            eng.wait_ge(consts, NCONST)
            eng.wait_ge(weights_in, 16 * 3)
            eng.tensor_copy(iota_lo[:, :, :], iota_i[:, :, :])
            eng.tensor_copy(iota_hi[:, :, :], iota_i[:, 0:HI])
            eng.tensor_copy(tile_no[:, :], slot_i[:, 0, 0:4, :].rearrange("p a b -> p (a b)"))
            eng.tensor_copy(same_e[:, :], col_e[:, :].bitcast(U32))
            eng.tensor_copy(before[:, :], col_j[:, :].bitcast(U32))
            eng.tensor_copy(row_n[:, :], row_i[:, 0:1])
            eng.tensor_scalar(row_i[:, 1:2], row_i[:, 0:1], E - 1, None, ALU.bitwise_and)
            link(eng.tensor_scalar(row_i[:, 2:3], row_i[:, 0:1], 4, None, ALU.logical_shift_right))
            eng.tensor_copy(row_e[:, :], row_i[:, 1:2])
            link(eng.tensor_copy(row_j[:, :], row_i[:, 2:3]))
            link(eng.tensor_scalar(same_e[:, :], same_e[:, :], row_e[:, 0:1], None, ALU.is_equal))
            link(eng.scalar_tensor_tensor(before[:, :], before[:, :], row_j[:, 0:1], same_e[:, :], ALU.is_gt, ALU.mult))

            def link_router(c, n, ins):
                ins.then_inc(t_steps, 1)
                eng.wait_ge(t_steps, 6 * c.n + n)

            def stats_stage(c):
                eng.wait_ge(x_loaded[c.parity], 16 * c.pair + 16)
                for t in range(TB):
                    ins = eng.bn_stats(stats[:, t], xt[:, c.parity, t])
                ins.then_inc(stats_steps, 1)
                c.wait(eng, rows_ready, c.n)
                wait_alone(eng, stats_steps, c.n + 1, passed)
                for t in range(TB):
                    ins = eng.bn_aggr(mv[:, t], stats[:, t])
                link_router(c, 1, ins)
                link_router(c, 2, eng.tensor_scalar(var2[:, 0], mv[:, :, 1], LN_EPS, None, ALU.add))
                link_router(c, 3, eng.reciprocal(inv2[:, 0], var2[:, 0]))
                link_router(c, 4, eng.tensor_tensor(inv2[:, 1], inv2[:, 0], mv[:, :, 1], ALU.mult))
                eng.tensor_scalar(var2[:, 1], inv2[:, 1], FFN_EPS, None, ALU.add).then_inc(stats_ready, 1)

            def rows_stage(c):
                eng.wait_ge(std_ready, c.n + 1)
                link_router(c, 5, eng.reciprocal(inv2[:, :, :], std2[:, :, :]))
                link_router(c, 6, eng.tensor_tensor(hscale[:, :], inv2[:, 0], inv2[:, 1], ALU.mult))
                if not (c.fixed and c.n < 2):
                    eng.wait_ge(rows_stored[c.parity], 16 * c.pair)
                    eng.wait_ge(tr_done, KD * (c.n - 1))
                for t in range(TB):
                    ins = eng.tensor_scalar(xn[:, c.parity, t], xt[:, c.parity, t], mv[:, t, 0:1], hscale[:, t:t + 1],
                                            ALU.subtract, ALU.mult)
                ins.then_inc(rows_ready, 1)

            def turned_stage(c):
                c.wait(eng, logits_done, c.n - 1)
                for q in range(KD):
                    eng.wait_ge(tr_done, KD * c.n + q + 1)
                    eng.tensor_scalar(xcols[:, c.parity, q], ps_tr[:, q], normw[:, q:q + 1], None, ALU.mult).then_inc(tr_read, 1)

            def logits_stage(c):
                eng.wait_ge(logits_done, c.n + 1)
                eng.tensor_tensor(logits[:, :, :].rearrange("p (q j) e -> p q j e", j=NJ)[:, TB * c.parity:TB * c.parity + TB, c.pair],
                                  ps_y[:, c.parity, 0:TB * E].rearrange("p (t e) -> p t e", e=E),
                                  b_router[:, :].unsqueeze(1).broadcast_to([P, TB, E]), ALU.add).then_inc(logits_read, 1)

            def router(at, k):
                if in_router(k, -1):
                    turned_stage(at.shift(-1))
                if in_router(k, 0):
                    rows_stage(at)
                if in_router(k, -2):
                    logits_stage(at.shift(-2))
                if in_router(k, 1):
                    stats_stage(at.shift(1))

            router_steps(eng, router)

            eng.wait_ge(logits_read, NCH)

            def softmax_step(b):
                if b == 30:
                    eng.tensor_reduce(tile_max[:, :], logits[:, :, :], AX_X, ALU.max).then_inc(soft, 1)
                elif b == 29:
                    eng.wait_ge(soft, 1)
                    eng.tensor_tensor(probs[:, :, :], logits[:, :, :], tile_max[:, :].unsqueeze(2).broadcast_to([P, NT, E]),
                                      ALU.subtract).then_inc(exp_in, 1)
                elif b == 26:
                    eng.wait_ge(exp_done, 1)
                    eng.tensor_reduce(tile_sum[:, :], probs[:, :, :], AX_X, ALU.add).then_inc(soft, 1)
                elif b == 25:
                    eng.wait_ge(soft, 2)
                    eng.reciprocal(tile_sum[:, :], tile_sum[:, :]).then_inc(soft, 1)
                elif b == 24:
                    eng.wait_ge(soft, 3)
                    eng.tensor_tensor(probs[:, :, :], probs[:, :, :], tile_sum[:, :].unsqueeze(2).broadcast_to([P, NT, E]),
                                      ALU.mult).then_inc(soft, 1)

            eng.wait_ge(by_e_done, 1)
            link(eng.tensor_copy(by_e[:, :], ring[:, 0:2].rearrange("p a b -> p (a b)")))
            rounds = [0]

            def total(src, threshold, op, b=None):
                m = rounds[0]
                rounds[0] += 1
                eng.tensor_scalar(flags[:, :], src, threshold, None, op, ALU.add,
                                  accum_out=count[:, m % 2:m % 2 + 1]).then_inc(counts_in, 1)
                softmax_step(b)
                eng.wait_ge(counts_out, m + 1)
                return ring[:, 2, 0:1]

            def prefix(src):
                ins = eng.tensor_tensor_scan(running[:, :], ones[:, :], src[:, :], 0.0, ALU.mult, ALU.add)
                ins.then_inc(counts_in, 1)
                eng.wait_ge(counts_in, prefix_at[0])
                prefix_at[0] += 1

            prefix_at = [34]
            c0 = total(by_e[:, :], zero1[:, 0:1], ALU.is_ge)
            link(eng.tensor_scalar(sign[:, 3:4], c0, float(CAP), None, ALU.is_ge))
            eng.tensor_scalar(sign[:, 0:1], sign[:, 3:4], 2.0, -1.0, ALU.mult, ALU.add)
            link(eng.tensor_scalar(sign[:, 1:2], sign[:, 3:4], float(2 * CAP - T - 1), float(T - CAP + 1), ALU.mult, ALU.add))
            link(eng.tensor_scalar(signed[:, :], by_e[:, :], sign[:, 0:1], None, ALU.mult))
            link(eng.tensor_scalar(bits[:, 3:4], bits[:, 0:1], 1 << 30, None, ALU.bitwise_or))
            for b in range(30, -1, -1):
                if b:
                    eng.tensor_scalar(bits[:, 1:2], bits[:, 0:1], 1 << (b - 1), None, ALU.bitwise_or)
                got = total(signed[:, :], bits[:, 3:4].bitcast(F32), ALU.is_ge, b)
                link(eng.tensor_scalar(bits[:, 2:3], got, sign[:, 1:2], None, ALU.is_ge))
                if b:
                    eng.scalar_tensor_tensor(bits[:, 3:4], bits[:, 2:3], b, bits[:, 1:2],
                                             ALU.logical_shift_left, ALU.bitwise_or)
                link(eng.scalar_tensor_tensor(bits[:, 0:1], bits[:, 2:3], b, bits[:, 0:1],
                                              ALU.logical_shift_left, ALU.bitwise_or))
            link(eng.tensor_tensor(sign[:, 2:3], bits[:, 0:1].bitcast(F32), sign[:, 0:1], ALU.mult))

            eng.tensor_scalar(above[:, :], by_e[:, :], sign[:, 2:3], None, ALU.is_gt)
            link(eng.tensor_scalar(equal[:, :], by_e[:, :], sign[:, 2:3], None, ALU.is_equal))
            got = total(by_e[:, :], sign[:, 2:3], ALU.is_gt)
            link(eng.tensor_scalar(sign[:, 3:4], got, -1.0, float(CAP), ALU.mult, ALU.add))
            prefix(equal)
            eng.wait_ge(counts_out, 34)
            link(eng.tensor_tensor(sign[:, 3:4], sign[:, 3:4], ring[:, 3, 0:1], ALU.subtract))
            link(eng.scalar_tensor_tensor(equal[:, :], running[:, :], sign[:, 3:4], equal[:, :], ALU.is_le, ALU.mult))
            link(eng.tensor_tensor(above[:, :], above[:, :], equal[:, :], ALU.add))
            prefix(above)
            eng.wait_ge(counts_out, 35)
            link(eng.tensor_copy(count[:, 2:3], ring[:, 3, 0:1]))
            eng.scalar_tensor_tensor(slot1[:, :], running[:, :], count[:, 2:3], above[:, :], ALU.add, ALU.mult).then_inc(slot_done, 1)

            eng.wait_ge(tokens_done, 1)
            link(eng.tensor_scalar(slot_i[:, :, :, :].rearrange("p q j e -> p (q j e)"),
                                   ring[:, 0:2].rearrange("p a b -> p (a b)"), -1.0, None, ALU.add))
            eng.tensor_scalar(taken[:, :, :, :], slot_i[:, :, :, :], 0.0, None, ALU.is_ge)
            eng.tensor_scalar(digit_i[:, 0], slot_i[:, :, :, :], LO - 1, None, ALU.bitwise_and)
            link(eng.tensor_scalar(digit_i[:, 1], slot_i[:, :, :, :], 5, None, ALU.arith_shift_right))
            for m, dst in ((0, lo_b), (1, hi_b)):
                link(eng.tensor_copy(dst[:, :, :].rearrange("p e t -> p t e"),
                                     digit_i[:, m].rearrange("p q j e -> p (q j) e")))
            eng.wait_ge(soft, 4)
            link(eng.tensor_tensor(part[:, :, :], probs[:, :, :], taken[:, :, :, :].rearrange("p q j e -> p (q j) e"), ALU.mult))
            link(eng.tensor_reduce(tile_sum[:, :], part[:, :, :], AX_X, ALU.add))
            link(eng.tensor_scalar(tile_max[:, :], tile_sum[:, :], 0.0, None, ALU.is_le))
            link(eng.tensor_tensor(tile_sum[:, :], tile_sum[:, :], tile_max[:, :], ALU.add))
            link(eng.reciprocal(tile_sum[:, :], tile_sum[:, :]))
            for q in range(NQ):
                tiles = slice(q * NJ, q * NJ + NJ)
                ins = eng.tensor_tensor(shares[:, :, q], part[:, tiles], tile_sum[:, tiles].unsqueeze(2).broadcast_to([P, NJ, E]),
                                        ALU.mult)
            ins.then_inc(shares_ready, 1)

            def hot_stage(c):
                c.wait(eng, list_done, c.n - 1)
                eng.tensor_tensor(hot_hi[:, c.parity], iota_hi[:, :, :],
                                  hi_b[:, c.n].unsqueeze(1).broadcast_to([P, HI, NT]), ALU.is_equal).then_inc(hot_hi_ready, 1)
                eng.tensor_tensor(hot_lo[:, c.parity], iota_lo[:, :, :],
                                  lo_b[:, c.n].unsqueeze(1).broadcast_to([P, LO, NT]), ALU.is_equal).then_inc(hot_lo_ready, 1)

            def list_stage(c):
                eng.wait_ge(list_done, c.n + 1)
                if not (c.fixed and c.n == 0):
                    eng.wait_ge(list_read, c.n)
                eng.tensor_copy(part_sum[:, :], ps_y[0:LO, c.parity, 0:2 * HI]).then_inc(list_sum, 1)
                eng.wait_ge(list_sum, c.n + 1)
                eng.scalar_tensor_tensor(lists[:, c.n], part_sum[:, HI:2 * HI], float(P), part_sum[:, 0:HI],
                                         ALU.mult, ALU.add).then_inc(list_read, 1)

            hot_stage(Place(0, 0))
            hot_stage(Place(0, 1))
            for m in range(2):
                list_stage(Place(0, m))
                hot_stage(Place(1, m))
            with eng.Fori(1, E // 2 - 1) as i:
                for m in range(2):
                    list_stage(Place(i, m))
                    hot_stage(Place(i, m).shift(2))
            for m in range(2):
                list_stage(Place(E // 2 - 1, m))

            def stages(at, k):
                if has(k, 1) and (k is None or k >= -1):
                    c = at.shift(1)
                    for q in range(KD):
                        eng.wait_ge(etr_done, KD * c.n + q + 1)
                        eng.tensor_scalar(xe[:, q], ps_tr[:, q], normw[:, q:q + 1], None, ALU.mult).then_inc(etr_read, 1)
                if has(k, 0):
                    eng.wait_ge(w_in[at.parity], 64 * at.pair + 64)
                    if k is None or k >= 2:
                        eng.wait_ge(scattered, 16 * SLOTS * (at.n - 1))
                    if k is None or k >= 1:
                        eng.wait_ge(y_ready, SLOTS * at.n)
                    for s in range(SLOTS):
                        eng.wait_ge(y_done, SLOTS * at.n + s + 1)
                        eng.tensor_tensor(ysum[:, s], ps_y[:, s % 2, 0:D], b2[:, at.parity], ALU.add).then_inc(y_read, 1)
                        eng.wait_ge(y_read, SLOTS * at.n + s + 1)
                        if s == 0:
                            eng.wait_ge(share_ready, at.n + 1)
                        eng.tensor_scalar(ye[:, at.parity, s], ysum[:, s], share[:, at.parity, s:s + 1], None, ALU.mult).then_inc(y_ready, 1)
                if has(k, 1) and (k is None or k >= -1):
                    c = at.shift(1)
                    eng.wait_ge(gathered[c.parity], 16 * SLOTS * c.pair + 16 * SLOTS)
                    eng.tensor_copy(share[:, c.parity], rows[:, c.parity, :, bass.ds(c.n + D, 1)].rearrange("p s o -> p (s o)")).then_inc(share_ready, 1)

            experts(eng, stages)


def state_space_block(nc, x_in, x_out, w):
    M = 2 * NS
    NT = L // P
    NH = L // CH
    BC = 2 * NS
    XD = 3 * BC + DTR
    x_rows = x_in.rearrange("(b t p) d -> b p t d", p=P, t=NT)
    y_rows = x_out.rearrange("(b t p) d -> b t p d", p=P, t=NT)
    TASKS = (("delta", 2, 0, "units"), ("gate", 2, 1, "units"), ("gate", 3, 2, "units"),
             ("out", 0, 3, "out"), ("out", 2, 4, "out"), ("out", 4, 5, "out"), ("out", 6, 6, "out"),
             ("turn", 0, 7, "prep"), ("turn", 1, 8, "prep"), ("project", 0, 9, "prep"), ("convolve", 0, 10, "prep"),
             ("delta", 3, 11, "units"), ("project", 1, 12, "prep"), ("convolve", 1, 13, "prep"),
             ("project", 2, 15, "prep"), ("project", 3, 17, "prep"), ("convolve", 2, 19, "prep"),
             ("convolve", 3, 20, "prep"), ("xdbl", 0, 23, "prep"), ("delta", 0, 25, "prep"),
             ("gate", 0, 26, "prep"), ("delta", 1, 28, "prep"), ("gate", 1, 29, "prep"))

    def has(task, units, out, prep):
        return {"units": units, "out": out, "prep": prep}[task[3]]

    def after(eng, sem, count):
        if not isinstance(count, int) or count > 0:
            eng.wait_ge(sem, count)

    with ExitStack() as ctx:
        def sb(name, shape, dt=F32):
            return ctx.enter_context(nc.sbuf_tensor("b_" + name, shape, dt))

        def sem(name):
            return nc.alloc_semaphore("b_" + name)

        def ps(name, shape):
            return ctx.enter_context(nc.psum_tensor("b_" + name, shape, F32))

        w_in = sb("w_in", [P, KD, 2 * DI])
        w_x = sb("w_x", [P, KI, XD])
        w_dt = sb("w_dt", [P, DI])
        w_out = sb("w_out", [P, KI, D])
        taps = sb("taps", [P, KI, KC])
        tab = sb("tab", [P, 3, KI])
        a_log = sb("a_log", [P, KI, NS])
        ident = sb("ident", [P, P])
        diag_conv = sb("diag_conv", [P, KI, KC, P])
        diag_d = sb("diag_d", [P, KI, P])
        pick_i = sb("pick_i", [P, BC], U32)
        pick_r = sb("pick_r", [P, 2], U32)
        pick_f = sb("pick_f", [P, BC])
        pick_rf = sb("pick_rf", [P, 1])
        pick = sb("pick", [P, BC], BF16)
        one = sb("one", [P, 1])
        xt = sb("xt", [P, NT, D])
        stats = sb("stats", [P, NT, 6])
        mv = sb("mv", [P, NT, 2])
        var = sb("var", [P, NT])
        std = sb("std", [P, NT])
        inv = sb("inv", [P, NT])
        u_cols = sb("u_cols", [P, KD, L])
        PAD = KC - 1
        xin = sb("xin", [P, 2, PAD + L])
        xc = sb("xc", [P, KI, L])
        sres = sb("sres", [P, KI, L])
        xd = sb("xd", [P, L])
        parts = sb("parts", [P, L], BF16)
        next_parts = sb("next_parts", [P, L], BF16)
        rest = sb("rest", [P, L])
        delta = sb("delta", [P, KI, L])
        soft = sb("soft", [P, L])
        du = sb("du", [P, KI, L])
        bbc = sb("bbc", [P, 2, L])
        cbc = sb("cbc", [P, 2, L])
        da = sb("da", [P, 2, 2, L])
        hc = sb("hc", [P, 2, 2, L])
        yg = sb("yg", [P, KI, L])
        xr = sb("xr", [P, 2, D])
        yt = sb("yt", [P, 2, D])
        ps_y = ps("ps_y", [P, 2, L])
        ps_bc = ps("ps_bc", [P, L])
        side = ps("side", [P, 2, CH])

        weights_in, consts, ident0 = sem("weights_in"), sem("consts"), sem("ident0")
        setup, a_exp = sem("setup"), sem("a_exp")
        x_loaded = sem("x_loaded")
        ln_steps, stats_ready, std_ready, rows_ready = sem("ln_steps"), sem("stats_ready"), sem("std_ready"), sem("rows_ready")
        passed, pool_passed = sem("passed"), sem("pool_passed")
        side_done, side_read = [sem("side_done0"), sem("side_done1")], [sem("side_read0"), sem("side_read1")]
        xc_ready, gate_ready = sem("xc_ready"), sem("gate_ready")
        high_ready, rest_ready, mid_ready = sem("high_ready"), sem("rest_ready"), sem("mid_ready")
        low_ready, parts_ready = sem("low_ready"), sem("parts_ready")
        soft_abs, soft_exp, soft_ready = sem("soft_abs"), sem("soft_exp"), sem("soft_ready")
        delta_ready, du_ready = sem("delta_ready"), sem("du_ready")
        bc_done, bbc_ready, cbc_ready = sem("bc_done"), sem("bbc_ready"), sem("cbc_ready")
        da_ready, dbu_ready, scanned, hc_ready, added = sem("da_ready"), sem("dbu_ready"), sem("scanned"), sem("hc_ready"), sem("added")
        y_read = sem("y_read")
        xr_loaded = [sem("xr_loaded0"), sem("xr_loaded1")]
        y_stored = [sem("y_stored0"), sem("y_stored1")]
        NW = 7

        def steps(eng, step):
            step(-1, False, False, True)
            step(0, True, False, True)
            step(1, True, True, True)
            with eng.Fori(2, B - 1) as b:
                step(b, True, True, True)
            step(B - 1, True, True, False)
            step(B, False, True, False)

        def parts_of(b):
            return 0 <= b < B, b > 0, b < B - 1

        def uses(b, name, c):
            def those(step):
                return [t[:2] for t in TASKS if has(t, *parts_of(step))]

            first = b if isinstance(b, int) else 1
            return (sum(len(those(step)) for step in range(-1, first)) + those(first).index((name, c))
                    + (b - first) * len(TASKS))

        def taken(eng, b, name, c):
            for bank in range(2):
                eng.wait_ge(side_read[bank], uses(b, name, c) + 1)

        block = ctx.enter_context(nc.Block())

        @block.sync
        def _(eng):
            eng.dma_start(xt[:, :, :], x_rows[0]).then_inc(x_loaded, 16)
            eng.dma_start(w_in[:, :, :], w["b_in"].rearrange("(k p) n -> p k n", p=P)).then_inc(weights_in, 16)
            eng.dma_start(w_x[:, :, :], w["b_x"].rearrange("(k p) n -> p k n", p=P)).then_inc(weights_in, 16)
            eng.dma_start(w_dt[3 * BC:XD, :], w["b_dt"]).then_inc(weights_in, 16)
            eng.dma_start(w_out[:, :, :], w["b_out"].rearrange("(k p) n -> p k n", p=P)).then_inc(weights_in, 16)
            eng.dma_start(taps[:, :, :], w["b_taps"].rearrange("(k p) n -> p k n", p=P)).then_inc(weights_in, 16)
            eng.dma_start(tab[:, :, :], w["b_tab"]).then_inc(weights_in, 16)
            eng.dma_start(a_log[:, :, :], w["b_a_log"].rearrange("(k p) n -> p k n", p=P)).then_inc(weights_in, 16)

            def step(b, units, out, prep):
                if prep and not (isinstance(b, int) and b == -1):
                    taken(eng, b - 1, "turn", 1)
                    eng.dma_start(xt[:, :, :], x_rows[b + 1]).then_inc(x_loaded, 16)
                if out:
                    def summed(b, t):
                        eng.wait_ge(side_read[t % 2], uses(b, "out", t - t % 2) + 1)

                    for t in range(NT):
                        if t >= 2:
                            summed(b, t - 2)
                        elif not (isinstance(b, int) and b == 1):
                            summed(b - 1, t + NT - 2)
                        eng.dma_start(xr[:, t % 2], x_rows[b - 1][:, t]).then_inc(xr_loaded[t % 2], 16)
                        if t >= 1:
                            summed(b, t - 1)
                            eng.dma_start(y_rows[b - 1][t - 1], yt[:, (t - 1) % 2]).then_inc(y_stored[(t - 1) % 2], 16)
                    summed(b, NT - 1)
                    eng.dma_start(y_rows[b - 1][NT - 1], yt[:, (NT - 1) % 2]).then_inc(y_stored[(NT - 1) % 2], 16)

            steps(eng, step)
            for s in y_stored:
                eng.wait_ge(s, 16 * B * NT // 2)

        @block.gpsimd
        def _(eng):
            eng.memset(ident[:, :], 0.0).then_inc(ident0, 1)
            eng.wait_ge(ident0, 1)
            eng.affine_select(out=ident[:, :], in_=ident[:, :], compare_op=ALU.not_equal, fill=1.0,
                              base=0, pattern=[[-1, P]], channel_multiplier=1).then_inc(consts, 1)
            eng.memset(one[:, :], 1.0).then_inc(consts, 1)
            eng.iota(pick_i[:, :], [[1, BC]], base=0, channel_multiplier=0).then_inc(consts, 1)
            eng.iota(pick_r[:, 0:1], [[0, 1]], base=0, channel_multiplier=1).then_inc(consts, 1)
            for c in range(2):
                eng.memset(xin[:, c, 0:PAD], 0.0).then_inc(consts, 1)
            eng.memset(w_dt[0:64, 0:4], 0.0).then_inc(consts, 1)

            def deltas(b, c):
                eng.wait_ge(soft_ready, 4 * b + c + 1)
                eng.tensor_tensor(delta[:, c], delta[:, c], soft[:, :], ALU.add).then_inc(delta_ready, 1)
                eng.wait_ge(delta_ready, 4 * b + c + 1)
                eng.wait_ge(xc_ready, b + 1)
                eng.tensor_tensor(du[:, c], delta[:, c], xc[:, c], ALU.mult).then_inc(du_ready, 1)

            def step(b, units, out, prep):
                if units:
                    for m in range(M):
                        for i in range(2):
                            c, u = 2 * (m // NS) + i, 2 * m + i
                            if m == 0 or m == NS:
                                eng.wait_ge(du_ready, 4 * b + c + 1)
                            if i == 0:
                                eng.wait_ge(bbc_ready, M * b + m + 1)
                            after(eng, added, 2 * M * b + u - 3)
                            eng.tensor_tensor(hc[:, m % 2, i], du[:, c], bbc[:, m % 2], ALU.mult).then_inc(dbu_ready, 1)
                        if m in (11, 14):
                            deltas(b, 2 if m == 11 else 3)
                        if prep and m in (27, 30):
                            deltas(b + 1, 0 if m == 27 else 1)
                if prep and not units:
                    deltas(b + 1, 0)
                    deltas(b + 1, 1)

            steps(eng, step)

        @block.scalar
        def _(eng):
            eng.wait_ge(weights_in, 16 * NW)
            eng.wait_ge(consts, 6)
            eng.activation(a_log[:, :, :], a_log[:, :, :], ACT.Exp).then_inc(a_exp, 1)
            eng.wait_ge(setup, 8)

            def delta_read(b, c):
                nb, n = b + 1 if c < 2 else b, uses(b, "delta", c)
                after(eng, delta_ready, 4 * nb + c)
                after(eng, soft_ready, 4 * nb + c)
                after(eng, da_ready, 2 * M * b + (2 * NS if c < 2 else 0))
                for half in range(NH):
                    eng.wait_ge(side_done[half], n + 1)
                    z, bias = side[:, half], tab[:, 1, c:c + 1]
                    cols = slice(half * CH, half * CH + CH)
                    eng.activation(delta[:, c, cols], z, ACT.Relu, bias=bias)
                    eng.activation(soft[:, cols], z, ACT.Abs, bias=bias).then_inc(side_read[half], 1)

            def delta_log(b, c):
                nb = b + 1 if c < 2 else b
                taken(eng, b, "delta", c)
                eng.activation(soft[:, :], soft[:, :], ACT.Exp, scale=-1.0).then_inc(soft_exp, 1)
                eng.wait_ge(soft_exp, 4 * nb + c + 1)
                eng.activation(soft[:, :], soft[:, :], ACT.Ln, bias=one[:, 0:1]).then_inc(soft_ready, 1)

            def std_stage(b):
                eng.wait_ge(stats_ready, b + 1)
                eng.activation(std[:, :], var[:, :], ACT.Sqrt).then_inc(std_ready, 1)

            def conv_silu(b):
                taken(eng, b, "convolve", 3)
                eng.activation(xc[:, :, :], xc[:, :, :], ACT.Silu).then_inc(xc_ready, 1)

            def xdbl_high(b):
                n = uses(b, "xdbl", 0)
                after(eng, low_ready, b + 1)
                for half in range(NH):
                    eng.wait_ge(side_done[half], n + 1)
                    eng.activation(xd[0:XD, half * CH:half * CH + CH], side[0:XD, half], ACT.Copy).then_inc(side_read[half], 1)
                taken(eng, b, "xdbl", 0)
                after(eng, parts_ready, b + 1)
                eng.activation(next_parts[0:3 * BC, :], xd[0:3 * BC, :], ACT.Copy).then_inc(high_ready, 1)

            def middle(b):
                eng.wait_ge(rest_ready, 2 * (b + 1) + 2)
                for r in (BC, 2 * BC):
                    ins = eng.activation(next_parts[r:r + BC, :], rest[r:r + BC, :], ACT.Copy)
                ins.then_inc(mid_ready, 1)

            def hand_over(b):
                eng.wait_ge(low_ready, b + 2)
                after(eng, bc_done, 2 * M * (b + 1))
                eng.activation(parts[0:3 * BC, :], next_parts[0:3 * BC, :], ACT.Copy).then_inc(parts_ready, 1)

            def step(b, units, out, prep):
                if units:
                    for m in range(M):
                        U = 2 * M * b + 2 * m
                        for i, (dst, ready, used) in enumerate(((bbc, bbc_ready, dbu_ready), (cbc, cbc_ready, hc_ready))):
                            eng.wait_ge(bc_done, U + i + 1)
                            after(eng, used, U - 2)
                            eng.activation(dst[:, m % 2], ps_bc[:, :], ACT.Copy).then_inc(ready, 1)
                            if prep and m == M - 1 and i == 1:
                                hand_over(b)
                            c = 2 * (m // NS) + i
                            if m == 0 or m == NS:
                                eng.wait_ge(delta_ready, 4 * b + c + 1)
                            after(eng, scanned, U + i - 3)
                            eng.activation(da[:, m % 2, i], delta[:, c], ACT.Exp, scale=a_log[:, c, m % NS:m % NS + 1]).then_inc(da_ready, 1)
                        if m in (0, 11):
                            delta_read(b, 2 if m == 0 else 3)
                        if m in (10, 13):
                            delta_log(b, 2 if m == 10 else 3)
                        if m == 4:
                            if prep:
                                std_stage(b + 1)
                            taken(eng, b, "gate", 3)
                            eng.activation(sres[:, :, :], sres[:, :, :], ACT.Silu).then_inc(gate_ready, 1)
                        if prep and m == 21:
                            conv_silu(b)
                        if prep and m == 24:
                            xdbl_high(b)
                        if prep and m in (25, 28):
                            delta_read(b, 0 if m == 25 else 1)
                        if prep and m in (26, 29):
                            delta_log(b, 0 if m == 26 else 1)
                        if prep and m == 27:
                            middle(b)
                elif prep:
                    std_stage(b + 1)
                    conv_silu(b)
                    xdbl_high(b)
                    middle(b)
                    delta_read(b, 0)
                    delta_log(b, 0)
                    hand_over(b)
                    delta_read(b, 1)
                    delta_log(b, 1)

            steps(eng, step)

        @block.tensor
        def _(eng):
            eng.wait_ge(setup, 8)
            eng.wait_ge(consts, 7)

            def fill(b, name, c, half, part, products):
                after(eng, side_read[half], uses(b, name, c))
                last = len(products) - 1
                for k, (lhs, rhs) in enumerate(products):
                    mm = eng.matmul(part(side[:, half]), lhs, rhs, start=k == 0, stop=k == last)
                mm.then_inc(side_done[half], 1)

            def cols(half, shift=0):
                return slice(half * CH + shift, half * CH + CH + shift)

            def task(b, name, c):
                if name == "turn":
                    eng.wait_ge(rows_ready, b + 2)
                elif name == "project":
                    taken(eng, b, "turn", 1)
                elif name == "convolve":
                    taken(eng, b, "project", c)
                elif name == "xdbl":
                    eng.wait_ge(xc_ready, b + 2)
                elif name == "delta":
                    taken(eng, b if c < 2 else b - 1, "xdbl", 0)
                elif name == "out" and c == 0:
                    eng.wait_ge(y_read, 4 * b)
                for half in range(NH):
                    if name == "turn":
                        after(eng, side_read[half], uses(b, name, c))
                        for t in range(4):
                            mm = eng.transpose(side[:, half, t * P:t * P + P], xt[:, 4 * half + t, c * P:c * P + P], ident[:, :])
                        mm.then_inc(side_done[half], 1)
                    elif name == "project":
                        fill(b, name, c, half, lambda o: o,
                             [(w_in[:, kb, c * P:c * P + P], u_cols[:, kb, cols(half)]) for kb in range(KD)])
                    elif name == "gate":
                        fill(b, name, c, half, lambda o: o,
                             [(w_in[:, kb, DI + c * P:DI + c * P + P], u_cols[:, kb, cols(half)]) for kb in range(KD)])
                    elif name == "convolve":
                        fill(b, name, c, half, lambda o: o,
                             [(diag_conv[:, c, k], xin[:, c % 2, cols(half, k)]) for k in range(KC)])
                    elif name == "xdbl":
                        fill(b, name, c, half, lambda o: o[0:XD],
                             [(w_x[:, kb], xc[:, kb, cols(half)]) for kb in range(KI)])
                    elif name == "delta":
                        fill(b, name, c, half, lambda o: o,
                             [(w_dt[3 * BC:XD, c * P:c * P + P], xd[3 * BC:XD, cols(half)])])
                    else:
                        t = c + half
                        fill(b, name, c, half, lambda o: o[:, 0:D],
                             [(yg[:, kb, t * P:t * P + P], w_out[:, kb]) for kb in range(KI)])

            def add(b, m, i):
                c, u = 2 * (m // NS) + i, 2 * M * b + 2 * m + i
                if m % NS == 0:
                    after(eng, y_read, 4 * b + 2 * (m // NS) - 1 + i)
                    for half in range(NH):
                        eng.matmul(ps_y[:, i, cols(half)], diag_d[:, c], xc[:, c, cols(half)], start=True, stop=False,
                                   skip_group_check=True)
                eng.wait_ge(hc_ready, u + 1)
                for half in range(NH):
                    mm = eng.matmul(ps_y[:, i, cols(half)], ident[:, :], hc[:, m % 2, i, cols(half)], start=False,
                                    stop=m % NS == NS - 1, skip_group_check=True)
                mm.then_inc(added, 1)

            def add_behind(b, m, i, out):
                if m >= 2:
                    add(b, m - 2, i)
                elif out:
                    add(b - 1, m - 2 + M, i)

            def spread(b, m, i):
                if i == 0:
                    after(eng, cbc_ready, M * b + m)
                else:
                    eng.wait_ge(bbc_ready, M * b + m + 1)
                n = NS * i + m % NS
                for half in range(NH):
                    mm = eng.matmul(ps_bc[:, cols(half)], pick[0:3 * BC, n:n + 1].broadcast_to([3 * BC, P]),
                                    parts[0:3 * BC, cols(half)], start=True, stop=True)
                mm.then_inc(bc_done, 1)

            def step(b, units, out, prep):
                if units:
                    eng.wait_ge(parts_ready, b + 1)
                    for m in range(M):
                        here = [t for t in TASKS if t[2] == m and has(t, units, out, prep)]
                        for i in range(2):
                            spread(b, m, i)
                            add_behind(b, m, i, out)
                            for t in here:
                                if (t[0] == "delta") == (i == 0):
                                    task(b, t[0], t[1])
                else:
                    if out:
                        for m in range(2):
                            for i in range(2):
                                add_behind(b, m, i, out)
                    for t in TASKS:
                        if has(t, units, out, prep):
                            task(b, t[0], t[1])

            steps(eng, step)

        @block.vector
        def _(eng):
            eng.wait_ge(consts, 7)
            eng.wait_ge(weights_in, 16 * NW)
            eng.tensor_copy(pick_f[:, :], pick_i[:, :])
            eng.tensor_scalar(pick_r[:, 1:2], pick_r[:, 0:1], BC - 1, None, ALU.bitwise_and).then_inc(setup, 1)
            eng.wait_ge(setup, 1)
            eng.tensor_copy(pick_rf[:, :], pick_r[:, 1:2]).then_inc(setup, 1)
            eng.wait_ge(setup, 2)
            eng.tensor_scalar(pick[:, :], pick_f[:, :], pick_rf[:, 0:1], None, ALU.is_equal).then_inc(setup, 1)
            for c in range(KI):
                for k in range(KC):
                    eng.tensor_scalar(diag_conv[:, c, k], ident[:, :], taps[:, c, k:k + 1], None, ALU.mult)
                eng.tensor_scalar(diag_d[:, c], ident[:, :], tab[:, 2, c:c + 1], None, ALU.mult).then_inc(setup, 1)
            eng.wait_ge(a_exp, 1)
            eng.tensor_scalar(a_log[:, :, :], a_log[:, :, :], -1.0, None, ALU.mult).then_inc(setup, 1)

            def norm(nb):
                eng.wait_ge(x_loaded, 16 * nb + 16)
                for t in range(NT):
                    ins = eng.bn_stats(stats[:, t], xt[:, t])
                ins.then_inc(ln_steps, 1)
                wait_alone(eng, ln_steps, 3 * nb + 1, passed)
                for t in range(NT):
                    ins = eng.bn_aggr(mv[:, t], stats[:, t])
                ins.then_inc(ln_steps, 1)
                eng.wait_ge(ln_steps, 3 * nb + 2)
                eng.tensor_scalar(var[:, :], mv[:, :, 1], LN_EPS, None, ALU.add).then_inc(stats_ready, 1)

            def norm_rows(nb):
                eng.wait_ge(std_ready, nb + 1)
                eng.reciprocal(inv[:, :], std[:, :]).then_inc(ln_steps, 1)
                eng.wait_ge(ln_steps, 3 * nb + 3)
                for t in range(NT):
                    ins = eng.tensor_scalar(xt[:, t], xt[:, t], mv[:, t, 0:1], inv[:, t:t + 1], ALU.subtract, ALU.mult)
                ins.then_inc(rows_ready, 1)

            def task_read(b, name, c):
                n = uses(b, name, c)
                if name == "gate":
                    after(eng, y_read, 4 * b + 2 if c < 2 else 4 * b)
                elif name == "convolve":
                    after(eng, du_ready, 4 * b + c + 1)
                for half in range(NH):
                    cols = slice(half * CH, half * CH + CH)
                    src, s = side[:, half], side_read[half]
                    eng.wait_ge(side_done[half], n + 1)
                    if name == "turn":
                        eng.tensor_copy(u_cols[:, c, cols], src).then_inc(s, 1)
                    elif name == "project":
                        eng.tensor_copy(xin[:, c % 2, PAD + half * CH:PAD + half * CH + CH], src).then_inc(s, 1)
                    elif name == "convolve":
                        eng.tensor_scalar(xc[:, c, cols], src, tab[:, 0, c:c + 1], None, ALU.add).then_inc(s, 1)
                    elif name == "gate":
                        eng.tensor_copy(sres[:, c, cols], src).then_inc(s, 1)
                    else:
                        before = NT // 2 * (b - 1) + c // 2
                        eng.wait_ge(xr_loaded[half], 16 * before + 16)
                        after(eng, y_stored[half], 16 * before)
                        eng.tensor_tensor(yt[:, half], src[:, 0:D], xr[:, half], ALU.add).then_inc(s, 1)

            def gated(b, q):
                eng.wait_ge(gate_ready, b + 1)
                for i in range(2):
                    eng.wait_ge(added, 2 * M * b + 2 * NS * (q + 1) - 1 + i)
                    eng.tensor_tensor(yg[:, 2 * q + i], ps_y[:, i], sres[:, 2 * q + i], ALU.mult).then_inc(y_read, 1)

            def below_high(b):
                eng.wait_ge(high_ready, b + 2)
                for r in (BC, 2 * BC):
                    ins = eng.tensor_tensor(rest[r:r + BC, :], xd[r:r + BC, :], next_parts[r:r + BC, :], ALU.subtract)
                    ins.then_inc(rest_ready, 1)

            def low(b):
                eng.wait_ge(mid_ready, b + 2)
                r = 2 * BC
                eng.tensor_tensor(next_parts[r:r + BC, :], rest[r:r + BC, :], next_parts[r:r + BC, :],
                                  ALU.subtract).then_inc(low_ready, 1)

            def step(b, units, out, prep):
                if units:
                    for m in range(M):
                        U = 2 * M * b + 2 * m
                        for i in range(2):
                            eng.wait_ge(da_ready, U + i + 1)
                            eng.wait_ge(dbu_ready, U + i + 1)
                            eng.tensor_tensor_scan(hc[:, m % 2, i], da[:, m % 2, i], hc[:, m % 2, i], 0.0,
                                                   ALU.mult, ALU.add).then_inc(scanned, 1)
                        for i in range(2):
                            if i == 0:
                                eng.wait_ge(cbc_ready, M * b + m + 1)
                            eng.wait_ge(scanned, U + i + 1)
                            eng.tensor_tensor(hc[:, m % 2, i], hc[:, m % 2, i], cbc[:, m % 2], ALU.mult).then_inc(hc_ready, 1)
                        if m == 0 and out:
                            gated(b - 1, 1)
                        if m == NS:
                            gated(b, 0)
                        if prep and m == 2:
                            norm(b + 1)
                        if prep and m == 5:
                            norm_rows(b + 1)
                        for name, c, at, who in TASKS:
                            if at == m and has((name, c, at, who), units, out, prep) and name not in ("delta", "xdbl"):
                                task_read(b, name, c)
                        if prep and m == 24:
                            below_high(b)
                        if prep and m == 28:
                            low(b)
                else:
                    if prep:
                        norm(b + 1)
                        norm_rows(b + 1)
                    if out:
                        gated(b - 1, 1)
                    for name, c, at, who in TASKS:
                        if has((name, c, at, who), units, out, prep):
                            if name == "xdbl":
                                below_high(b)
                                low(b)
                            elif name != "delta":
                                task_read(b, name, c)

            steps(eng, step)


def program(nc, w, out):
    x1 = nc.dram_tensor("x1", (T, D), F32, kind="Internal").ap()
    rows_tab = nc.dram_tensor("rows_tab", (T, D + E), F32, kind="Internal").ap()
    list_tab = nc.dram_tensor("list_tab", (E, CAP), U32, kind="Internal").ap()
    with nc.cleanup_on_exit():
        recurrence_block(nc, w["x"], x1, w)
    with nc.cleanup_on_exit():
        experts_block(nc, "f_", x1, rows_tab, list_tab, w)
    with nc.cleanup_on_exit():
        state_space_block(nc, x1, out, w)
    with nc.cleanup_on_exit():
        experts_block(nc, "g_", out, rows_tab, list_tab, w)


def kernel(**inputs):
    import numpy as np
    import concourse.bacc as _bacc
    from concourse import mybir as _mybir
    from concourse.bass_utils import run_bass_kernel_spmd as _run

    a = {k: np.asarray(v) for k, v in inputs.items()}

    def g(name):
        return a["L0_" + name]

    def columns(v):
        return np.asarray(v).reshape(-1, 128).T

    cc = np.ascontiguousarray
    arrays = {
        "x": cc(g("attn_a_hidden_states").reshape(T, D)),
        "a_table": cc(np.concatenate([columns(g("attn_a_" + n)) for n in (
            "fc_r_b", "fc_i_b", "fc_b", "fc_gate_b", "mlp_gate_b", "mlp_fc_b", "norm_w", "norm2_w", "alpha")], axis=1)),
        "a_proj": cc(np.stack([g("attn_a_" + n).T for n in ("fc_r_w", "fc_i_w", "fc_w", "fc_gate_w")], axis=1)),
        "a_mlp": cc(np.stack([g("attn_a_mlp_gate_w").T, g("attn_a_mlp_fc_w").T])),
        "a_out": cc(g("attn_a_out_w").T),
        "a_out_b": cc(g("attn_a_out_b")),
        "f_router": cc(g("ffn_router_weight").T),
        "f_router_b": cc(g("ffn_router_bias")),
        "f_norm": cc(columns(g("ffn_norm_weight"))),
        "f_w1": cc(g("ffn_fc1_weight").transpose(0, 2, 1)),
        "f_w2": cc(g("ffn_fc2_weight").transpose(0, 2, 1)),
        "f_b1": cc(g("ffn_fc1_bias").reshape(E, KF, P).transpose(0, 2, 1)),
        "f_b2": cc(g("ffn_fc2_bias")),
        "b_in": cc(g("attn_b_W_in")),
        "b_x": cc(np.concatenate([g("attn_b_W_x")[:, DTR:]] * 3 + [g("attn_b_W_x")[:, :DTR]], axis=1)),
        "b_dt": cc(g("attn_b_W_dt")),
        "b_out": cc(g("attn_b_W_out")),
        "b_taps": cc(g("attn_b_conv_w")),
        "b_tab": cc(np.stack([columns(g("attn_b_" + n)) for n in ("conv_b", "b_dt", "D")], axis=1)),
        "b_a_log": cc(g("attn_b_A_log")),
    }
    nc = _bacc.Bacc("TRN2", target_bir_lowering=False, num_devices=1)
    aps = {}
    for name, v in arrays.items():
        aps[name] = nc.dram_tensor("in_" + name, v.shape, _mybir.dt.from_np(v.dtype), kind="ExternalInput").ap()
    out = nc.dram_tensor("out", (T, D), _mybir.dt.float32, kind="ExternalOutput").ap()
    program(nc, aps, out)
    r = _run(nc, [{"in_" + k: v for k, v in arrays.items()}], core_ids=[0])
    return np.asarray(r.results[0]["out"]).reshape(B, L, D)
```

```python
from contextlib import ExitStack

import concourse.bass as bass
from concourse import mybir

F32 = mybir.dt.float32
BF16 = mybir.dt.bfloat16
F16 = mybir.dt.float16
U32 = mybir.dt.uint32
ALU = mybir.AluOpType
ACT = mybir.ActivationFunctionType
AX_X = mybir.AxisListType.X

P = 128
D = 256
KD = D // P
B, L = 8, 1024
T = B * L
CH = 512
NCH = T // CH
TB = CH // P
H3 = 3 * D
KM = H3 // P
E, F, CAP = 16, 1024, T // 16
KF = F // P
DI, NS, DTR, KC = 2 * D, 16, D // 16, 4
KI = DI // P
LN_EPS, RMS_EPS, FFN_EPS = 1e-5, 1e-6, 1e-5


class Place:

    def __init__(self, pair, parity):
        self.pair, self.parity = pair, parity
        self.n = pair * 2 + parity
        self.fixed = isinstance(self.n, int)

    def shift(self, by):
        return Place(self.pair + (self.parity + by) // 2, (self.parity + by) % 2)

    def wait(self, eng, sem, count, least=1):
        if isinstance(count, int) and count < least:
            return
        eng.wait_ge(sem, count)


def wait_alone(eng, sem, count, passed):
    eng.wait_ge(sem, count)
    eng.sem_inc(passed, 1)



def recurrence_block(nc, x_in, x_out, w):
    x_rows = x_in.rearrange("(c t p) d -> c p t d", p=P, t=TB)
    y_rows = x_out.rearrange("(c t p) d -> c p t d", p=P, t=TB)
    col = {}
    at = 0
    for name, n in (("r", 2), ("i", 2), ("fc", 2), ("gate", 2), ("mg", KM), ("mf", KM),
                    ("norm", 2), ("norm2", 2), ("alpha", 2)):
        col[name] = at
        at += n
    ncols = at
    with ExitStack() as ctx:
        def sb(name, shape, dt=F32):
            return ctx.enter_context(nc.sbuf_tensor("a_" + name, shape, dt))

        def sem(name):
            return nc.alloc_semaphore("a_" + name)

        w_proj = sb("w_proj", [P, KD, 4, D])
        w_mlp = sb("w_mlp", [P, KD, 2, H3])
        w_out = sb("w_out", [P, KM, D])
        table = sb("table", [P, ncols])
        outb = sb("outb", [P, D])
        ident = sb("ident", [P, P])
        mean_w = sb("mean_w", [P, P])
        one = sb("one", [P, 1])
        eps6 = sb("eps6", [P, 1])
        sp = sb("sp", [P, 6, KD])
        xt = sb("xt", [P, 2, TB, D])
        u_rows = sb("u_rows", [P, TB, D])
        h_rows = sb("h_rows", [P, TB, D])
        xr = sb("xr", [P, TB, D])
        xb = sb("xb", [P, TB, D])
        yt = sb("yt", [P, 2, TB, D])
        stats = sb("stats", [P, TB, 6])
        mv = sb("mv", [P, TB, 2])
        var2 = sb("var2", [P, 2, TB])
        std2 = sb("std2", [P, 2, TB])
        inv2 = sb("inv2", [P, 2, TB])
        hscale = sb("hscale", [P, TB])
        u_cols = sb("u_cols", [P, 2, KD, CH])
        h_cols = sb("h_cols", [P, KD, CH])
        sig_r = sb("sig_r", [P, KD, CH])
        sig_i = sb("sig_i", [P, KD, CH])
        decay = sb("decay", [P, KD, CH])
        na2 = sb("na2", [P, KD, CH])
        beta = sb("beta", [P, KD, CH])
        drive = sb("drive", [P, KD, CH])
        state = sb("state", [P, 2, KD, CH])
        gate = sb("gate", [P, KD, CH])
        hs2 = sb("hs2", [P, 2, KD, CH])
        sq = sb("sq", [P, KD, CH])
        rms = sb("rms", [P, CH])
        inv_rms = sb("inv_rms", [P, CH])
        h2 = sb("h2", [P, KD, CH])
        g2 = sb("g2", [P, 2, CH])
        v = sb("v", [P, KM, CH])
        RING = 4
        ring = ctx.enter_context(nc.psum_tensor("a_ring", [P, RING, CH], F32))
        ps_out = ctx.enter_context(nc.psum_tensor("a_ps_out", [P, 2, CH], F32))
        ps_tr = ctx.enter_context(nc.psum_tensor("a_ps_tr", [P, 2, CH], F32))

        table_in, proj_in, weights_in = sem("table_in"), sem("proj_in"), sem("weights_in")
        setup = sem("setup")
        alpha_abs, alpha_exp, alpha_ln = sem("alpha_abs"), sem("alpha_exp"), sem("alpha_ln")
        consts = sem("consts")
        ident0 = sem("ident0")
        x_loaded = [sem("x_loaded0"), sem("x_loaded1")]
        xr_loaded = sem("xr_loaded")
        xb_ready = sem("xb_ready")
        t1_steps, t2_steps = sem("t1_steps"), sem("t2_steps")
        stats_ready, std_ready, rows_ready = sem("stats_ready"), sem("std_ready"), sem("rows_ready")
        tr_done, tr_read = sem("tr_done"), sem("tr_read")
        proj_done = sem("proj_done")
        ri_read, hs_read, g_read = sem("ri_read"), sem("hs_read"), sem("g_read")
        decay_ready, na2_ready, beta_ready = sem("decay_ready"), sem("na2_ready"), sem("beta_ready")
        drive_steps = sem("drive_steps")
        hs2_steps, hs2_ready, sq_ready = sem("hs2_steps"), sem("hs2_ready"), sem("sq_ready")
        norm_steps, stats_steps, dve_passed = sem("norm_steps"), sem("stats_steps"), sem("dve_passed")
        ms_done, rms_ready, inv_ready, h2_ready = sem("ms_done"), sem("rms_ready"), sem("inv_ready"), sem("h2_ready")
        mlp_done, mg_read, mf_read = sem("mlp_done"), sem("mg_read"), sem("mf_read")
        out_done, out_read = sem("out_done"), sem("out_read")
        y_stored = [sem("y_stored0"), sem("y_stored1")]
        NW = 4

        def pipeline(eng, stages):
            for k in range(-1, 4):
                stages(Place(k // 2, k % 2), k)
            with eng.Fori(2, NCH // 2 - 1) as i:
                stages(Place(i, 0), None)
                stages(Place(i, 1), None)
            for k in range(NCH - 2, NCH + 2):
                stages(Place(k // 2, k % 2), k)

        def has(k, stage):
            return k is None or 0 <= k + {"T": 1, "P": 0, "M": -1, "O": -2}[stage] < NCH

        block = ctx.enter_context(nc.Block())

        @block.sync
        def _(eng):
            eng.dma_start(xt[:, 0], x_rows[0]).then_inc(x_loaded[0], 16)
            eng.dma_start(table[:, :], w["a_table"]).then_inc(table_in, 16)
            eng.dma_start(w_proj[:, :, :, :], w["a_proj"].rearrange("(k p) q d -> p k q d", p=P)).then_inc(proj_in, 16)
            eng.dma_start(outb[:, :], w["a_out_b"].partition_broadcast(P)).then_inc(weights_in, 16)
            eng.dma_start(xt[:, 1], x_rows[1]).then_inc(x_loaded[1], 16)
            for q in range(2):
                eng.dma_start(w_mlp[:, :, q, :], w["a_mlp"][q].rearrange("(k p) d -> p k d", p=P)).then_inc(weights_in, 16)
            eng.dma_start(w_out[:, :, :], w["a_out"].rearrange("(k p) d -> p k d", p=P)).then_inc(weights_in, 16)

            def stages(at, k):
                if has(k, "O"):
                    c = at.shift(-2)
                    c.wait(eng, xb_ready, c.n)
                    eng.dma_start(xr[:, :, :], x_rows[c.n]).then_inc(xr_loaded, 16)
                if has(k, "T") and (k is None or k + 3 < NCH):
                    nxt = at.shift(1)
                    eng.wait_ge(rows_ready, nxt.n + 1)
                    eng.dma_start(xt[:, nxt.parity], x_rows[at.shift(3).n]).then_inc(x_loaded[nxt.parity], 16)
                if has(k, "O"):
                    c = at.shift(-2)
                    eng.wait_ge(out_read, TB * c.n + TB)
                    eng.dma_start(y_rows[c.n], yt[:, c.parity]).then_inc(y_stored[c.parity], 16)

            for k in range(-1, 4):
                stages(Place(k // 2, k % 2), k)
            with eng.Fori(2, NCH // 2 - 2) as i:
                stages(Place(i, 0), None)
                stages(Place(i, 1), None)
            for k in range(NCH - 4, NCH + 2):
                stages(Place(k // 2, k % 2), k)
            for s in y_stored:
                eng.wait_ge(s, 16 * (NCH // 2))

        @block.gpsimd
        def _(eng):
            eng.memset(mean_w[:, :], 1.0 / D).then_inc(consts, 1)
            eng.memset(one[:, :], 1.0).then_inc(consts, 1)
            eng.memset(eps6[:, :], RMS_EPS).then_inc(consts, 1)
            eng.memset(ident[:, :], 0.0).then_inc(ident0, 1)
            eng.wait_ge(ident0, 1)
            eng.affine_select(out=ident[:, :], in_=ident[:, :], compare_op=ALU.not_equal, fill=1.0,
                              base=0, pattern=[[-1, P]], channel_multiplier=1).then_inc(consts, 1)
            eng.wait_ge(weights_in, 16 * NW)

            def stages(at, k):
                if has(k, "O"):
                    c = at.shift(-2)
                    eng.wait_ge(xr_loaded, 16 * c.n + 16)
                    c.wait(eng, out_read, TB * c.n)
                    eng.tensor_tensor(xb[:, :, :], xr[:, :, :],
                                      outb[:, :].unsqueeze(1).broadcast_to([P, TB, D]), ALU.add).then_inc(xb_ready, 1)
                if has(k, "P"):
                    eng.wait_ge(hs2_ready, at.n + 1)
                    eng.tensor_tensor(sq[:, :, :], hs2[:, at.parity], hs2[:, at.parity], ALU.mult).then_inc(sq_ready, 1)

            pipeline(eng, stages)

        @block.scalar
        def _(eng):
            eng.wait_ge(table_in, 16)
            eng.wait_ge(consts, 4)
            eng.activation(sp[:, 0], table[:, col["alpha"]:col["alpha"] + 2], ACT.Abs).then_inc(alpha_abs, 1)
            eng.wait_ge(alpha_abs, 1)
            eng.activation(sp[:, 1], sp[:, 0], ACT.Exp, scale=-1.0).then_inc(alpha_exp, 1)
            eng.wait_ge(alpha_exp, 1)
            eng.activation(sp[:, 2], sp[:, 1], ACT.Ln, bias=one[:, 0:1]).then_inc(alpha_ln, 1)

            def stages(at, k):
                if k == 0:
                    eng.wait_ge(setup, 3)
                if has(k, "P"):
                    at.wait(eng, hs_read, KD * at.n)
                    for j, (dst, name) in enumerate(((sig_r, "r"), (sig_r, "r"), (sig_i, "i"), (sig_i, "i"))):
                        eng.wait_ge(proj_done, 8 * at.n + j + 1)
                        half = j % 2
                        bias = table[:, col[name] + half:col[name] + half + 1]
                        eng.activation(dst[:, half], ring[:, j % RING], ACT.Sigmoid, bias=bias).then_inc(ri_read, 1)
                    at.wait(eng, drive_steps, 3 * at.n)
                    eng.wait_ge(ri_read, 4 * at.n + 2)
                    for half in range(KD):
                        eng.activation(decay[:, half], sig_r[:, half], ACT.Exp, scale=sp[:, 5, half:half + 1]).then_inc(decay_ready, 1)
                if has(k, "M"):
                    c = at.shift(-1)
                    eng.wait_ge(ms_done, c.n + 1)
                    c.wait(eng, inv_ready, c.n)
                    eng.activation(rms[:, :], ps_tr[:, 1], ACT.Sqrt, bias=eps6[:, 0:1]).then_inc(rms_ready, 1)
                if has(k, "T"):
                    c = at.shift(1)
                    eng.wait_ge(stats_ready, c.n + 1)
                    eng.activation(std2[:, :, :], var2[:, :, :], ACT.Sqrt).then_inc(std_ready, 1)
                if has(k, "P"):
                    eng.wait_ge(na2_ready, at.n + 1)
                    eng.activation(beta[:, :, :], na2[:, :, :], ACT.Sqrt, bias=one[:, 0:1]).then_inc(beta_ready, 1)
                    at.wait(eng, hs2_ready, at.n)
                    for half in range(KD):
                        eng.wait_ge(proj_done, 8 * at.n + 7 + half)
                        bias = table[:, col["gate"] + half:col["gate"] + half + 1]
                        eng.activation(gate[:, half], ring[:, (6 + half) % RING], ACT.Gelu, bias=bias).then_inc(g_read, 1)
                if has(k, "M"):
                    c = at.shift(-1)
                    for j in range(KM):
                        eng.wait_ge(mlp_done, 2 * KM * c.n + 2 * j + 1)
                        if j >= 2 or not (c.fixed and c.n == 0):
                            eng.wait_ge(mf_read, KM * c.n + j - 1)
                        bias = table[:, col["mg"] + j:col["mg"] + j + 1]
                        eng.activation(g2[:, j % 2], ring[:, (8 + 2 * j) % RING], ACT.Gelu, bias=bias).then_inc(mg_read, 1)

            pipeline(eng, stages)

        @block.tensor
        def _(eng):
            eng.wait_ge(consts, 4)

            def stages(at, k):
                if k == 0:
                    eng.wait_ge(setup, 3 + KD)
                if k == 1:
                    eng.wait_ge(setup, 3 + 2 * KD)
                    eng.wait_ge(weights_in, 16 * NW)
                if has(k, "P"):
                    eng.wait_ge(tr_read, 4 * at.n + 4)
                    prev = at.shift(-2)
                    for j in range(8):
                        if j < RING:
                            s = 20 + j - RING - 8
                            at.wait(eng, mf_read if s % 2 else mg_read, KM * prev.n + s // 2 + 1)
                        else:
                            eng.wait_ge(ri_read, 4 * at.n + j - RING + 1)
                        for kb in range(KD):
                            mm = eng.matmul(ring[:, j % RING], w_proj[:, kb, j // 2, (j % 2) * P:(j % 2) * P + P],
                                            h_cols[:, kb], start=kb == 0, stop=kb == KD - 1)
                        mm.then_inc(proj_done, 1)
                if has(k, "O"):
                    c = at.shift(-2)
                    eng.wait_ge(mf_read, KM * c.n + KM)
                    for t in range(TB):
                        if t >= 2 or not (c.fixed and c.n == 0):
                            eng.wait_ge(out_read, TB * c.n + t - 1)
                        dst = ps_out[:, t % 2, 0:D]
                        for j in range(KM):
                            eng.matmul(dst, v[:, j, t * P:t * P + P], w_out[:, j], start=j == 0, stop=False,
                                       skip_group_check=True)
                        for kb in range(KD):
                            mm = eng.matmul(dst[:, kb * P:kb * P + P], hs2[:, c.parity, kb, t * P:t * P + P],
                                            ident[:, :], start=False, stop=True, skip_group_check=True)
                        mm.then_inc(out_done, 1)
                if has(k, "T"):
                    c = at.shift(1)
                    eng.wait_ge(rows_ready, c.n + 1)
                    for q in range(4):
                        src = (u_rows, h_rows)[q // 2]
                        if q < 2:
                            c.wait(eng, tr_read, 4 * c.n)
                            if q == 1:
                                last = at.shift(-1)
                                last.wait(eng, rms_ready, last.n + 1)
                        else:
                            eng.wait_ge(tr_read, 4 * c.n + q - 1)
                        for t in range(TB):
                            mm = eng.transpose(ps_tr[:, q % 2, t * P:t * P + P], src[:, t, (q % 2) * P:(q % 2) * P + P],
                                               ident[:, :])
                        mm.then_inc(tr_done, 1)
                if has(k, "M"):
                    c = at.shift(-1)
                    eng.wait_ge(h2_ready, c.n + 1)
                    for s in range(8, 20):
                        j = (s - 8) // 2
                        if s - RING >= 8:
                            q = s - RING - 8
                            eng.wait_ge(mf_read if q % 2 else mg_read, KM * c.n + q // 2 + 1)
                        elif has(k, "P"):
                            q = s - RING
                            if q < 4:
                                eng.wait_ge(ri_read, 4 * at.n + q + 1)
                            elif q < 6:
                                eng.wait_ge(hs_read, KD * at.n + q - 3)
                            else:
                                eng.wait_ge(g_read, KD * at.n + q - 5)
                        elif s == 8:
                            eng.wait_ge(mf_read, KM * c.n)
                            eng.wait_ge(mg_read, KM * c.n)
                            eng.wait_ge(g_read, KD * NCH)
                        for kb in range(KD):
                            mm = eng.matmul(ring[:, s % RING], w_mlp[:, kb, s % 2, j * P:j * P + P], h2[:, kb],
                                            start=kb == 0, stop=kb == KD - 1)
                        mm.then_inc(mlp_done, 1)
                if has(k, "P"):
                    eng.wait_ge(sq_ready, at.n + 1)
                    if has(k, "T"):
                        eng.wait_ge(tr_read, 4 * at.n + 8)
                    for kb in range(KD):
                        mm = eng.matmul(ps_tr[:, 1], mean_w[:, :], sq[:, kb], start=kb == 0, stop=kb == KD - 1)
                    mm.then_inc(ms_done, 1)

            pipeline(eng, stages)

        @block.vector
        def _(eng):
            def setup_stage(k):
                if k == -1:
                    eng.wait_ge(table_in, 16)
                    eng.tensor_scalar(sp[:, 3], table[:, col["alpha"]:col["alpha"] + 2], 0.0, None, ALU.max).then_inc(setup, 1)
                    eng.wait_ge(alpha_ln, 1)
                    eng.wait_ge(setup, 1)
                    eng.tensor_tensor(sp[:, 4], sp[:, 3], sp[:, 2], ALU.add).then_inc(setup, 1)
                    eng.wait_ge(setup, 2)
                    eng.tensor_scalar(sp[:, 5], sp[:, 4], -8.0, None, ALU.mult).then_inc(setup, 1)
                    eng.wait_ge(proj_in, 16)
                    for kb in range(KD):
                        n1 = col["norm"] + kb
                        eng.tensor_scalar(w_proj[:, kb], w_proj[:, kb], table[:, n1:n1 + 1], None, ALU.mult).then_inc(setup, 1)
                elif k == 0:
                    eng.wait_ge(weights_in, 16 * NW)
                    for kb in range(KD):
                        n2 = col["norm2"] + kb
                        eng.tensor_scalar(w_mlp[:, kb], w_mlp[:, kb], table[:, n2:n2 + 1], None, ALU.mult).then_inc(setup, 1)

            def stats_stage(c):
                steps = [0]

                def link(ins):
                    steps[0] += 1
                    ins.then_inc(t1_steps, 1)
                    eng.wait_ge(t1_steps, 3 * c.n + steps[0])

                eng.wait_ge(x_loaded[c.parity], 16 * c.pair + 16)
                for t in range(TB):
                    ins = eng.bn_stats(stats[:, t], xt[:, c.parity, t])
                ins.then_inc(stats_steps, 1)
                wait_alone(eng, stats_steps, c.n + 1, dve_passed)
                for t in range(TB):
                    ins = eng.bn_aggr(mv[:, t], stats[:, t])
                link(ins)
                link(eng.tensor_scalar(var2[:, 0], mv[:, :, 1], LN_EPS, None, ALU.add))
                link(eng.reciprocal(inv2[:, 0], var2[:, 0]))
                eng.tensor_tensor(inv2[:, 1], inv2[:, 0], mv[:, :, 1], ALU.mult).then_inc(norm_steps, 1)
                eng.wait_ge(norm_steps, c.n + 1)
                eng.tensor_scalar(var2[:, 1], inv2[:, 1], RMS_EPS, None, ALU.add).then_inc(stats_ready, 1)

            def rows_stage(c):
                eng.wait_ge(std_ready, c.n + 1)
                eng.reciprocal(inv2[:, :, :], std2[:, :, :]).then_inc(t2_steps, 1)
                eng.wait_ge(t2_steps, 2 * c.n + 1)
                eng.tensor_tensor(hscale[:, :], inv2[:, 0], inv2[:, 1], ALU.mult).then_inc(t2_steps, 1)
                eng.wait_ge(t2_steps, 2 * c.n + 2)
                c.wait(eng, tr_done, 4 * c.n)
                for t in range(TB):
                    eng.tensor_scalar(u_rows[:, t], xt[:, c.parity, t], mv[:, t, 0:1], inv2[:, 0, t:t + 1],
                                      ALU.subtract, ALU.mult)
                    ins = eng.tensor_scalar(h_rows[:, t], xt[:, c.parity, t], mv[:, t, 0:1], hscale[:, t:t + 1],
                                            ALU.subtract, ALU.mult)
                ins.then_inc(rows_ready, 1)

            def turn_stage(c):
                for q in range(4):
                    eng.wait_ge(tr_done, 4 * c.n + q + 1)
                    dst = u_cols[:, c.parity, q] if q < 2 else h_cols[:, q - 2]
                    eng.tensor_copy(dst, ps_tr[:, q % 2]).then_inc(tr_read, 1)

            def out_read_stage(c, t):
                eng.wait_ge(out_done, TB * c.n + t + 1)
                if t == 0:
                    eng.wait_ge(xb_ready, c.n + 1)
                    c.wait(eng, y_stored[c.parity], 16 * c.pair)
                eng.tensor_tensor(yt[:, c.parity, t], ps_out[:, t % 2, 0:D], xb[:, t], ALU.add).then_inc(out_read, 1)

            def stages(at, k):
                if has(k, "P"):
                    for half in range(KD):
                        eng.wait_ge(proj_done, 8 * at.n + 5 + half)
                        eng.wait_ge(ri_read, 4 * at.n + 3 + half)
                        bias = table[:, col["fc"] + half:col["fc"] + half + 1]
                        eng.scalar_tensor_tensor(drive[:, half], ring[:, (4 + half) % RING], bias, sig_i[:, half],
                                                 ALU.add, ALU.mult).then_inc(hs_read, 1)
                if has(k, "T"):
                    stats_stage(at.shift(1))
                if has(k, "P"):
                    eng.wait_ge(decay_ready, KD * at.n + KD)
                    at.wait(eng, beta_ready, at.n)
                    eng.scalar_tensor_tensor(na2[:, :, :], decay[:, :, :], -1.0, decay[:, :, :],
                                             ALU.mult, ALU.mult).then_inc(na2_ready, 1)
                if has(k, "O"):
                    out_read_stage(at.shift(-2), 0)
                if has(k, "M"):
                    c = at.shift(-1)
                    eng.wait_ge(rms_ready, c.n + 1)
                    eng.reciprocal(inv_rms[:, :], rms[:, :]).then_inc(inv_ready, 1)
                    eng.wait_ge(inv_ready, c.n + 1)
                    eng.tensor_tensor(h2[:, :, :], hs2[:, c.parity], inv_rms[:, :].unsqueeze(1).broadcast_to([P, KD, CH]),
                                      ALU.mult).then_inc(h2_ready, 1)
                if has(k, "O"):
                    out_read_stage(at.shift(-2), 1)
                if has(k, "T"):
                    rows_stage(at.shift(1))
                if has(k, "O"):
                    out_read_stage(at.shift(-2), 2)
                if has(k, "P"):
                    eng.wait_ge(beta_ready, at.n + 1)
                    eng.wait_ge(hs_read, KD * at.n + KD)
                    eng.tensor_tensor(drive[:, :, :], drive[:, :, :], beta[:, :, :], ALU.mult).then_inc(drive_steps, 1)
                    eng.wait_ge(drive_steps, 3 * at.n + 1)
                    for half in range(KD):
                        initial = 0.0 if at.parity == 0 else state[:, 0, half, CH - 1:CH]
                        eng.tensor_tensor_scan(state[:, at.parity, half], decay[:, half], drive[:, half], initial,
                                               ALU.mult, ALU.add).then_inc(drive_steps, 1)
                if has(k, "O"):
                    out_read_stage(at.shift(-2), 3)
                if has(k, "T"):
                    turn_stage(at.shift(1))
                if has(k, "P"):
                    eng.wait_ge(g_read, KD * at.n + KD)
                    eng.wait_ge(drive_steps, 3 * at.n + 3)
                    eng.tensor_tensor(gate[:, :, :], state[:, at.parity], gate[:, :, :], ALU.mult).then_inc(hs2_steps, 1)
                    eng.wait_ge(hs2_steps, at.n + 1)
                    eng.tensor_tensor(hs2[:, at.parity], gate[:, :, :], u_cols[:, at.parity], ALU.add).then_inc(hs2_ready, 1)
                if has(k, "M"):
                    c = at.shift(-1)
                    for j in range(KM):
                        eng.wait_ge(mlp_done, 2 * KM * c.n + 2 * j + 2)
                        eng.wait_ge(mg_read, KM * c.n + j + 1)
                        bias = table[:, col["mf"] + j:col["mf"] + j + 1]
                        eng.scalar_tensor_tensor(v[:, j], ring[:, (9 + 2 * j) % RING], bias, g2[:, j % 2],
                                                 ALU.add, ALU.mult).then_inc(mf_read, 1)
                setup_stage(k)

            pipeline(eng, stages)


def experts_block(nc, tag, x_tab, rows_tab, list_tab, w):
    NT = T // P
    NJ = P // E
    NQ = NT // NJ
    SPAN = NQ * P
    LO, HI = 32, CAP // 32
    SLOTS = CAP // P
    RW = D + E
    x_chunks = x_tab.rearrange("(c t p) d -> c p t d", p=P, t=TB)
    rows_chunks = rows_tab.rearrange("(c t p) d -> c p t d", p=P, t=TB)
    with ExitStack() as ctx:
        def sb(name, shape, dt=F32):
            return ctx.enter_context(nc.sbuf_tensor(tag + name, shape, dt))

        def sem(name):
            return nc.alloc_semaphore(tag + name)

        def ps(name, shape):
            return ctx.enter_context(nc.psum_tensor(tag + name, shape, F32))

        ident = sb("ident", [P, P])
        xt = sb("xt", [P, 2, TB, D])
        xn = sb("xn", [P, 2, TB, D])
        stats = sb("stats", [P, TB, 6])
        mv = sb("mv", [P, TB, 2])
        var2 = sb("var2", [P, 2, TB])
        std2 = sb("std2", [P, 2, TB])
        inv2 = sb("inv2", [P, 2, TB])
        hscale = sb("hscale", [P, TB])
        xcols = sb("xcols", [P, 2, KD, CH])
        w_router = sb("w_router", [P, KD, E])
        b_router = sb("b_router", [P, E])
        normw = sb("normw", [P, KD])
        logits = sb("logits", [P, NT, E])
        probs = sb("probs", [P, NT, E])
        tile_max = sb("tile_max", [P, NT])
        tile_sum = sb("tile_sum", [P, NT])
        by_e = sb("by_e", [P, SPAN])
        signed = sb("signed", [P, SPAN])
        flags = sb("flags", [P, SPAN])
        above = sb("above", [P, SPAN])
        equal = sb("equal", [P, SPAN])
        running = sb("running", [P, SPAN])
        ones = sb("ones", [P, SPAN])
        slot1 = sb("slot1", [P, SPAN])
        same_e = sb("same_e", [P, P])
        before = sb("before", [P, P])
        col_e = sb("col_e", [P, P])
        col_j = sb("col_j", [P, P])
        row_e = sb("row_e", [P, 1])
        row_j = sb("row_j", [P, 1])
        row_n = sb("row_n", [P, 1])
        iota_i = sb("iota_i", [P, LO, NT], U32)
        row_i = sb("row_i", [P, 3], U32)
        count = sb("count", [P, 1])
        partial = sb("partial", [P, 2], F16)
        same_h = sb("same_h", [P, P], F16)
        sign = sb("sign", [P, 4])
        zero1 = sb("zero1", [P, 1])
        bits = sb("bits", [P, 4], U32)
        slot_i = sb("slot_i", [P, NQ, NJ, E], mybir.dt.int32)
        digit_i = sb("digit_i", [P, 2, NQ, NJ, E], mybir.dt.int32)
        lo_b = sb("lo_b", [P, E, NT], BF16)
        hi_b = sb("hi_b", [P, E, NT], BF16)
        taken = sb("taken", [P, NQ, NJ, E])
        part = sb("part", [P, NT, E])
        shares = sb("shares", [P, NJ, NQ, E])
        iota_lo = sb("iota_lo", [P, LO, NT], BF16)
        iota_hi = sb("iota_hi", [P, HI, NT], BF16)
        tile_no = sb("tile_no", [P, NT], BF16)
        hot_lo = sb("hot_lo", [P, 2, LO, NT], BF16)
        hot_hi = sb("hot_hi", [P, 2, HI, NT], BF16)
        values = sb("values", [P, 2, 2, HI, NT], BF16)
        part_sum = sb("part_sum", [LO, 2 * HI])
        lists = sb("lists", [LO, E, HI], U32)
        slots = sb("slots", [P, E, SLOTS], U32)
        w1 = sb("w1", [P, 2, KD, F])
        w2 = sb("w2", [P, 2, KF, D])
        b1 = sb("b1", [P, 2, KF])
        b2 = sb("b2", [P, 2, D])
        gather_at = sb("gather_at", [P, 2, SLOTS], U32)
        scatter_at = sb("scatter_at", [P, 2, SLOTS], U32)
        rows = sb("rows", [P, 2, SLOTS, RW])
        share = sb("share", [P, 2, SLOTS])
        xe = sb("xe", [P, KD, CAP])
        hid = sb("hid", [P, KF, CAP])
        ysum = sb("ysum", [P, SLOTS, D])
        ye = sb("ye", [P, 2, SLOTS, D])
        RING = 4
        ring = ps("ring", [P, RING, CH])
        ps_tr = ps("ps_tr", [P, 2, CH])
        ps_y = ps("ps_y", [P, 2, CH])

        weights_in, consts, ident0 = sem("weights_in"), sem("consts"), sem("ident0")
        x_loaded = [sem("x_loaded0"), sem("x_loaded1")]
        rows_stored = [sem("rows_stored0"), sem("rows_stored1")]
        stats_steps, t_steps, passed = sem("stats_steps"), sem("t_steps"), sem("passed")
        stats_ready, std_ready, rows_ready = sem("stats_ready"), sem("std_ready"), sem("rows_ready")
        tr_done, tr_read, logits_done, logits_read = sem("tr_done"), sem("tr_read"), sem("logits_done"), sem("logits_read")
        soft, exp_in, exp_done = sem("soft"), sem("exp_in"), sem("exp_done")
        by_e_done, counts_in, counts_out = sem("by_e_done"), sem("counts_in"), sem("counts_out")
        sel = sem("sel")
        slot_done, tokens_done = sem("slot_done"), sem("tokens_done")
        shares_ready, shares_stored = sem("shares_ready"), sem("shares_stored")
        hot_hi_ready, hot_lo_ready, list_done, list_read = sem("hot_hi_ready"), sem("hot_lo_ready"), sem("list_done"), sem("list_read")
        row_values_ready, tile_values_ready = sem("row_values_ready"), [sem("tile_values_ready0"), sem("tile_values_ready1")]
        list_stored, slots_in = sem("list_stored"), sem("slots_in")
        w_in = [sem("w_in0"), sem("w_in1")]
        gather_idx, scatter_idx = sem("gather_idx"), sem("scatter_idx")
        gathered, scattered = [sem("gathered0"), sem("gathered1")], sem("scattered")
        etr_done, etr_read, share_ready = sem("etr_done"), sem("etr_read"), sem("share_ready")
        hid_done, hid_ready = sem("hid_done"), sem("hid_ready")
        y_done, y_read, y_ready = sem("y_done"), sem("y_read"), sem("y_ready")
        pool_passed = sem("pool_passed")
        list_sum = sem("list_sum")
        NCONST = 9

        def experts(eng, stages, first=-2):
            for k in range(first, 2):
                stages(Place(k // 2, k % 2), k)
            with eng.Fori(1, E // 2 - 1) as i:
                stages(Place(i, 0), None)
                stages(Place(i, 1), None)
            for k in range(E - 2, E):
                stages(Place(k // 2, k % 2), k)

        def tile_values(eng, c):
            eng.wait_ge(hot_hi_ready, c.n + 1)
            eng.tensor_tensor(values[:, c.parity, 1], hot_hi[:, c.parity],
                              tile_no[:, :].unsqueeze(1).broadcast_to([P, HI, NT]), ALU.mult).then_inc(tile_values_ready[c.parity], 1)

        def router_steps(eng, step):
            for k in range(-1, 4):
                step(Place(k // 2, k % 2), k)
            with eng.Fori(2, NCH // 2 - 1) as i:
                step(Place(i, 0), None)
                step(Place(i, 1), None)
            for k in range(NCH - 2, NCH + 2):
                step(Place(k // 2, k % 2), k)

        def in_router(k, ahead):
            return k is None or 0 <= k + ahead < NCH

        def has(k, ahead):
            return k is None or 0 <= k + ahead < E

        block = ctx.enter_context(nc.Block())

        @block.sync
        def _(eng):
            eng.dma_start(w_router[:, :, :], w["f_router"].rearrange("(k p) e -> p k e", p=P)).then_inc(weights_in, 16)
            eng.dma_start(b_router[:, :], w["f_router_b"].partition_broadcast(P)).then_inc(weights_in, 16)
            eng.dma_start(normw[:, :], w["f_norm"]).then_inc(weights_in, 16)
            for c in range(2):
                eng.dma_start(xt[:, c], x_chunks[c]).then_inc(x_loaded[c], 16)

            def router(c, more):
                eng.wait_ge(rows_ready, c.n + 1)
                eng.dma_start(rows_chunks[c.n][:, :, 0:D], xn[:, c.parity]).then_inc(rows_stored[c.parity], 16)
                if more:
                    eng.dma_start(xt[:, c.parity], x_chunks[c.shift(2).n]).then_inc(x_loaded[c.parity], 16)

            with eng.Fori(0, NCH // 2 - 1) as i:
                router(Place(i, 0), True)
                router(Place(i, 1), True)
            router(Place(NCH // 2 - 1, 0), False)
            router(Place(NCH // 2 - 1, 1), False)
            def stages(at, k):
                if has(k, 2):
                    c = at.shift(2)
                    if k is None or k >= 0:
                        eng.wait_ge(y_read, SLOTS * at.n + SLOTS)
                    s = w_in[c.parity]
                    eng.dma_start(w1[:, c.parity], w["f_w1"][c.n].rearrange("(k p) f -> p k f", p=P)).then_inc(s, 16)
                    eng.dma_start(b1[:, c.parity], w["f_b1"][c.n]).then_inc(s, 16)
                    eng.dma_start(w2[:, c.parity], w["f_w2"][c.n].rearrange("(k p) d -> p k d", p=P)).then_inc(s, 16)
                    eng.dma_start(b2[:, c.parity], w["f_b2"][c.n].partition_broadcast(P)).then_inc(s, 16)

            for k in range(-2, 0):
                stages(Place(k // 2, k % 2), k)
            eng.wait_ge(shares_ready, 1)
            eng.dma_start(rows_tab.rearrange("(t p) d -> p t d", p=P)[:, :, D:RW],
                          shares[:, :, :, :].rearrange("p j q e -> p (j q) e")).then_inc(shares_stored, 16)
            for n, some in enumerate((slice(0, 2), slice(2, E))):
                eng.wait_ge(list_read, some.stop)
                eng.dma_start(list_tab[some].rearrange("e (l h) -> l e h", l=LO), lists[:, some]).then_inc(list_stored, 16)
                eng.wait_ge(list_stored, 16 * n + 16)
                eng.dma_start(slots[:, some], list_tab[some].rearrange("e (p s) -> p e s", p=P)).then_inc(slots_in, 16)

            experts(eng, stages, 0)

        @block.gpsimd
        def _(eng):
            eng.memset(ident[:, :], 0.0).then_inc(ident0, 1)
            eng.wait_ge(ident0, 1)
            eng.affine_select(out=ident[:, :], in_=ident[:, :], compare_op=ALU.not_equal, fill=1.0,
                              base=0, pattern=[[-1, P]], channel_multiplier=1).then_inc(consts, 1)
            eng.memset(zero1[:, :], 0.0).then_inc(consts, 1)
            eng.iota(row_i[:, 0:1], [[0, 1]], base=0, channel_multiplier=1).then_inc(consts, 1)
            eng.iota(iota_i[:, :, :], [[1, LO], [0, NT]], base=0, channel_multiplier=0).then_inc(consts, 1)
            eng.iota(col_e[:, :].bitcast(U32), [[0, NJ], [1, E]], base=0, channel_multiplier=0).then_inc(consts, 1)
            eng.iota(col_j[:, :].bitcast(U32), [[1, NJ], [0, E]], base=0, channel_multiplier=0).then_inc(consts, 1)
            eng.iota(bits[:, 0:4], [[0, 4]], base=0, channel_multiplier=0).then_inc(consts, 1)
            eng.iota(slot_i[:, 0, 0:4, :].bitcast(U32), [[1, NQ], [NQ, NJ]], base=0, channel_multiplier=0).then_inc(consts, 1)
            eng.memset(ones[:, :], 1.0).then_inc(consts, 1)

            def stages(at, k):
                if has(k, 2):
                    c = at.shift(2)
                    if k is None or k >= 0:
                        eng.wait_ge(etr_done, KD * at.n + KD)
                        eng.sem_inc(pool_passed, 1)
                        wait_alone(eng, share_ready, at.n + 1, pool_passed)
                    eng.tensor_copy(gather_at[:, c.parity], slots[:, c.n]).then_inc(gather_idx, 1)
                    wait_alone(eng, gather_idx, c.n + 1, pool_passed)
                    for s in range(SLOTS):
                        eng.indirect_dma_start(
                            out=rows[:, c.parity, s], out_offset=None, in_=rows_tab,
                            in_offset=bass.IndirectOffsetOnAxis(ap=gather_at[:, c.parity, s:s + 1], axis=0),
                        ).then_inc(gathered[c.parity], 16)
                if has(k, 0):
                    if k is None or k >= 1:
                        wait_alone(eng, scattered, 16 * SLOTS * at.n, pool_passed)
                    eng.tensor_copy(scatter_at[:, at.parity], slots[:, at.n]).then_inc(scatter_idx, 1)
                    wait_alone(eng, scatter_idx, at.n + 1, pool_passed)
                    for s in range(SLOTS):
                        wait_alone(eng, y_ready, SLOTS * at.n + s + 1, pool_passed)
                        eng.indirect_dma_start(
                            out=x_tab, out_offset=bass.IndirectOffsetOnAxis(ap=scatter_at[:, at.parity, s:s + 1], axis=0),
                            in_=ye[:, at.parity, s], in_offset=None, compute_op=ALU.add,
                        ).then_inc(scattered, 16)

            EARLY = 5
            with eng.Fori(0, EARLY) as i:
                tile_values(eng, Place(i, 0))
            eng.wait_ge(slots_in, 16)
            eng.wait_ge(shares_stored, 16)
            for s in rows_stored:
                eng.wait_ge(s, 16 * (NCH // 2))
            stages(Place(-1, 0), -2)
            with eng.Fori(EARLY, E // 2) as i:
                tile_values(eng, Place(i, 0))
            eng.wait_ge(slots_in, 32)
            experts(eng, stages, -1)
            eng.wait_ge(scattered, 16 * SLOTS * E)

        @block.scalar
        def _(eng):
            eng.wait_ge(weights_in, 16 * 3)

            def std_stage(c):
                eng.wait_ge(stats_ready, c.n + 1)
                eng.activation(std2[:, :, :], var2[:, :, :], ACT.Sqrt).then_inc(std_ready, 1)

            def turned_stage(c):
                c.wait(eng, logits_done, c.n - 1)
                for q in range(KD):
                    eng.wait_ge(tr_done, KD * c.n + q + 1)
                    eng.activation(xcols[:, c.parity, q], ps_tr[:, q], ACT.Copy, scale=normw[:, q:q + 1]).then_inc(tr_read, 1)

            def router(at, k):
                if in_router(k, -1):
                    turned_stage(at.shift(-1))
                if in_router(k, 1):
                    std_stage(at.shift(1))

            router_steps(eng, router)
            eng.wait_ge(exp_in, 1)
            eng.activation(probs[:, :, :], probs[:, :, :], ACT.Exp).then_inc(exp_done, 1)

            def row_values(c):
                eng.wait_ge(hot_hi_ready, c.n + 1)
                eng.activation(values[:, c.parity, 0], hot_hi[:, c.parity], ACT.Copy, scale=row_n[:, 0:1]).then_inc(row_values_ready, 1)

            with eng.Fori(0, E // 2) as i:
                row_values(Place(i, 0))
                row_values(Place(i, 1))

            def stages(at, k):
                if has(k, 0):
                    eng.wait_ge(w_in[at.parity], 64 * at.pair + 64)
                    for j in range(KF):
                        eng.wait_ge(hid_done, KF * at.n + j + 1)
                        eng.activation(hid[:, j], ring[:, j % RING], ACT.Gelu, bias=b1[:, at.parity, j:j + 1]).then_inc(hid_ready, 1)

            experts(eng, stages)

        @block.tensor
        def _(eng):
            eng.wait_ge(consts, 1)
            eng.wait_ge(weights_in, 16 * 3)

            def turn(c):
                eng.wait_ge(rows_ready, c.n + 1)
                for q in range(KD):
                    if not (c.fixed and c.n == 0):
                        eng.wait_ge(tr_read, KD * (c.n - 1) + q + 1)
                    for t in range(TB):
                        mm = eng.transpose(ps_tr[:, q, t * P:t * P + P], xn[:, c.parity, t, q * P:q * P + P], ident[:, :])
                    mm.then_inc(tr_done, 1)

            def route(c):
                eng.wait_ge(tr_read, KD * c.n + KD)
                c.wait(eng, logits_read, c.n - 1)
                for t in range(TB):
                    for kb in range(KD):
                        mm = eng.matmul(ps_y[:, c.parity, t * E:t * E + E], xcols[:, c.parity, kb, t * P:t * P + P],
                                        w_router[:, kb], start=kb == 0, stop=kb == KD - 1)
                mm.then_inc(logits_done, 1)

            def router(at, k):
                if in_router(k, 0):
                    turn(at)
                if in_router(k, -1):
                    route(at.shift(-1))

            router_steps(eng, router)

            eng.wait_ge(logits_read, NCH)
            for q in range(NQ):
                mm = eng.transpose(ring[:, q // 4, (q % 4) * P:(q % 4) * P + P], logits[:, q * NJ:q * NJ + NJ].rearrange("p j e -> p (j e)"), ident[:, :])
            mm.then_inc(by_e_done, 1)
            for n in range(1 + 31 + 1):
                eng.wait_ge(counts_in, n + 1)
                eng.matmul(ring[:, 2, 0:1], same_h[:, :], partial[:, n % 2:n % 2 + 1], start=True, stop=True).then_inc(counts_out, 1)
            for n in range(2):
                eng.wait_ge(counts_in, 34 + n)
                eng.matmul(ring[:, 3, 0:1], before[:, :], running[:, SPAN - 1:SPAN], start=True, stop=True).then_inc(counts_out, 1)
            eng.wait_ge(slot_done, 1)
            for q in range(NQ):
                mm = eng.transpose(ring[:, q // 4, (q % 4) * P:(q % 4) * P + P], slot1[:, q * P:q * P + P], ident[:, :])
            mm.then_inc(tokens_done, 1)

            def listed(c):
                eng.wait_ge(hot_lo_ready, c.n + 1)
                eng.wait_ge(row_values_ready, c.n + 1)
                eng.wait_ge(tile_values_ready[c.parity], c.pair + 1)
                c.wait(eng, list_read, c.n - 1)
                for t in range(NT):
                    mm = eng.matmul(ps_y[0:LO, c.parity, 0:2 * HI], hot_lo[:, c.parity, :, t],
                                    values[:, c.parity, :, :, t].rearrange("p v h -> p (v h)"),
                                    start=t == 0, stop=t == NT - 1)
                mm.then_inc(list_done, 1)

            for n in range(2):
                listed(Place(0, n))
            with eng.Fori(1, E // 2) as i:
                for n in range(2):
                    listed(Place(i, n))

            eng.wait_ge(list_read, E)

            def stages(at, k):
                if has(k, 0):
                    eng.wait_ge(w_in[at.parity], 64 * at.pair + 64)
                    eng.wait_ge(etr_read, KD * at.n + KD)
                    for j in range(KF):
                        if j >= RING or not (at.fixed and at.n == 0):
                            eng.wait_ge(hid_ready, KF * at.n + j - RING + 1)
                        for kb in range(KD):
                            mm = eng.matmul(ring[:, j % RING], w1[:, at.parity, kb, j * P:j * P + P], xe[:, kb],
                                            start=kb == 0, stop=kb == KD - 1)
                        mm.then_inc(hid_done, 1)
                if has(k, 1) and (k is None or k >= -1):
                    c = at.shift(1)
                    eng.wait_ge(gathered[c.parity], 16 * SLOTS * c.pair + 16 * SLOTS)
                    if not (c.fixed and c.n == 0):
                        eng.wait_ge(etr_read, KD * c.n)
                    for q in range(KD):
                        for s in range(SLOTS):
                            mm = eng.transpose(ps_tr[:, q, s * P:s * P + P], rows[:, c.parity, s, q * P:q * P + P], ident[:, :])
                        mm.then_inc(etr_done, 1)
                if has(k, 0):
                    for s in range(SLOTS):
                        if s >= 2 or not (at.fixed and at.n == 0):
                            eng.wait_ge(y_read, SLOTS * at.n + s - 1)
                        for j in range(KF):
                            if s == 0:
                                eng.wait_ge(hid_ready, KF * at.n + j + 1)
                            mm = eng.matmul(ps_y[:, s % 2, 0:D], hid[:, j, s * P:s * P + P], w2[:, at.parity, j],
                                            start=j == 0, stop=j == KF - 1)
                        mm.then_inc(y_done, 1)

            experts(eng, stages)

        @block.vector
        def _(eng):
            n = [0]

            def link(ins):
                n[0] += 1
                ins.then_inc(sel, 1)
                eng.wait_ge(sel, n[0])

            eng.wait_ge(weights_in, 16 * 3)

            def link_router(c, n, ins):
                ins.then_inc(t_steps, 1)
                eng.wait_ge(t_steps, 6 * c.n + n)

            def stats_stage(c):
                eng.wait_ge(x_loaded[c.parity], 16 * c.pair + 16)
                for t in range(TB):
                    ins = eng.bn_stats(stats[:, t], xt[:, c.parity, t])
                ins.then_inc(stats_steps, 1)
                c.wait(eng, rows_ready, c.n)
                wait_alone(eng, stats_steps, c.n + 1, passed)
                for t in range(TB):
                    ins = eng.bn_aggr(mv[:, t], stats[:, t])
                link_router(c, 1, ins)
                link_router(c, 2, eng.tensor_scalar(var2[:, 0], mv[:, :, 1], LN_EPS, None, ALU.add))
                link_router(c, 3, eng.reciprocal(inv2[:, 0], var2[:, 0]))
                link_router(c, 4, eng.tensor_tensor(inv2[:, 1], inv2[:, 0], mv[:, :, 1], ALU.mult))
                eng.tensor_scalar(var2[:, 1], inv2[:, 1], FFN_EPS, None, ALU.add).then_inc(stats_ready, 1)

            def rows_stage(c):
                eng.wait_ge(std_ready, c.n + 1)
                link_router(c, 5, eng.reciprocal(inv2[:, :, :], std2[:, :, :]))
                link_router(c, 6, eng.tensor_tensor(hscale[:, :], inv2[:, 0], inv2[:, 1], ALU.mult))
                if not (c.fixed and c.n < 2):
                    eng.wait_ge(rows_stored[c.parity], 16 * c.pair)
                    eng.wait_ge(tr_done, KD * (c.n - 1))
                for t in range(TB):
                    ins = eng.tensor_scalar(xn[:, c.parity, t], xt[:, c.parity, t], mv[:, t, 0:1], hscale[:, t:t + 1],
                                            ALU.subtract, ALU.mult)
                ins.then_inc(rows_ready, 1)

            def logits_stage(c):
                eng.wait_ge(logits_done, c.n + 1)
                eng.tensor_tensor(logits[:, :, :].rearrange("p (q j) e -> p q j e", j=NJ)[:, TB * c.parity:TB * c.parity + TB, c.pair],
                                  ps_y[:, c.parity, 0:TB * E].rearrange("p (t e) -> p t e", e=E),
                                  b_router[:, :].unsqueeze(1).broadcast_to([P, TB, E]), ALU.add).then_inc(logits_read, 1)

            def router(at, k):
                if in_router(k, 0):
                    rows_stage(at)
                if in_router(k, -2):
                    logits_stage(at.shift(-2))
                if in_router(k, 1):
                    stats_stage(at.shift(1))

            router_steps(eng, router)

            eng.wait_ge(consts, NCONST)
            eng.tensor_copy(iota_lo[:, :, :], iota_i[:, :, :])
            eng.tensor_copy(iota_hi[:, :, :], iota_i[:, 0:HI])
            eng.tensor_copy(tile_no[:, :], slot_i[:, 0, 0:4, :].rearrange("p a b -> p (a b)"))
            eng.tensor_copy(same_e[:, :], col_e[:, :].bitcast(U32))
            eng.tensor_copy(before[:, :], col_j[:, :].bitcast(U32))
            eng.tensor_copy(row_n[:, :], row_i[:, 0:1])
            eng.tensor_scalar(row_i[:, 1:2], row_i[:, 0:1], E - 1, None, ALU.bitwise_and)
            link(eng.tensor_scalar(row_i[:, 2:3], row_i[:, 0:1], 4, None, ALU.logical_shift_right))
            eng.tensor_copy(row_e[:, :], row_i[:, 1:2])
            link(eng.tensor_copy(row_j[:, :], row_i[:, 2:3]))
            link(eng.tensor_scalar(same_e[:, :], same_e[:, :], row_e[:, 0:1], None, ALU.is_equal))
            link(eng.tensor_copy(same_h[:, :], same_e[:, :]))
            link(eng.scalar_tensor_tensor(before[:, :], before[:, :], row_j[:, 0:1], same_e[:, :], ALU.is_gt, ALU.mult))

            eng.wait_ge(logits_read, NCH)

            def softmax_step(b):
                if b == 30:
                    eng.tensor_reduce(tile_max[:, :], logits[:, :, :], AX_X, ALU.max).then_inc(soft, 1)
                elif b == 29:
                    eng.wait_ge(soft, 1)
                    eng.tensor_tensor(probs[:, :, :], logits[:, :, :], tile_max[:, :].unsqueeze(2).broadcast_to([P, NT, E]),
                                      ALU.subtract).then_inc(exp_in, 1)
                elif b == 26:
                    eng.wait_ge(exp_done, 1)
                    eng.tensor_reduce(tile_sum[:, :], probs[:, :, :], AX_X, ALU.add).then_inc(soft, 1)
                elif b == 25:
                    eng.wait_ge(soft, 2)
                    eng.reciprocal(tile_sum[:, :], tile_sum[:, :]).then_inc(soft, 1)
                elif b == 24:
                    eng.wait_ge(soft, 3)
                    eng.tensor_tensor(probs[:, :, :], probs[:, :, :], tile_sum[:, :].unsqueeze(2).broadcast_to([P, NT, E]),
                                      ALU.mult).then_inc(soft, 1)

            eng.wait_ge(by_e_done, 1)
            link(eng.tensor_copy(by_e[:, :], ring[:, 0:2].rearrange("p a b -> p (a b)")))
            rounds = [0]

            def total(src, threshold, op, b=None):
                m = rounds[0]
                rounds[0] += 1
                eng.tensor_scalar(flags[:, :], src, threshold, None, op, ALU.add,
                                  accum_out=partial[:, m % 2:m % 2 + 1]).then_inc(counts_in, 1)
                softmax_step(b)
                eng.wait_ge(counts_out, m + 1)
                return ring[:, 2, 0:1]

            def prefix(src):
                ins = eng.tensor_tensor_scan(running[:, :], ones[:, :], src[:, :], 0.0, ALU.mult, ALU.add)
                ins.then_inc(counts_in, 1)
                eng.wait_ge(counts_in, prefix_at[0])
                prefix_at[0] += 1

            prefix_at = [34]
            c0 = total(by_e[:, :], zero1[:, 0:1], ALU.is_ge)
            link(eng.tensor_scalar(sign[:, 3:4], c0, float(CAP), None, ALU.is_ge))
            eng.tensor_scalar(sign[:, 0:1], sign[:, 3:4], 2.0, -1.0, ALU.mult, ALU.add)
            link(eng.tensor_scalar(sign[:, 1:2], sign[:, 3:4], float(2 * CAP - T - 1), float(T - CAP + 1), ALU.mult, ALU.add))
            link(eng.tensor_scalar(signed[:, :], by_e[:, :], sign[:, 0:1], None, ALU.mult))
            link(eng.tensor_scalar(bits[:, 3:4], bits[:, 0:1], 1 << 30, None, ALU.bitwise_or))
            for b in range(30, -1, -1):
                if b:
                    eng.tensor_scalar(bits[:, 1:2], bits[:, 0:1], 1 << (b - 1), None, ALU.bitwise_or)
                got = total(signed[:, :], bits[:, 3:4].bitcast(F32), ALU.is_ge, b)
                link(eng.tensor_scalar(bits[:, 2:3], got, sign[:, 1:2], None, ALU.is_ge))
                if b:
                    eng.scalar_tensor_tensor(bits[:, 3:4], bits[:, 2:3], b, bits[:, 1:2],
                                             ALU.logical_shift_left, ALU.bitwise_or)
                link(eng.scalar_tensor_tensor(bits[:, 0:1], bits[:, 2:3], b, bits[:, 0:1],
                                              ALU.logical_shift_left, ALU.bitwise_or))
            link(eng.tensor_tensor(sign[:, 2:3], bits[:, 0:1].bitcast(F32), sign[:, 0:1], ALU.mult))

            eng.tensor_scalar(above[:, :], by_e[:, :], sign[:, 2:3], None, ALU.is_gt)
            link(eng.tensor_scalar(equal[:, :], by_e[:, :], sign[:, 2:3], None, ALU.is_equal))
            got = total(by_e[:, :], sign[:, 2:3], ALU.is_gt)
            link(eng.tensor_scalar(sign[:, 3:4], got, -1.0, float(CAP), ALU.mult, ALU.add))
            prefix(equal)
            eng.wait_ge(counts_out, 34)
            link(eng.tensor_tensor(sign[:, 3:4], sign[:, 3:4], ring[:, 3, 0:1], ALU.subtract))
            link(eng.scalar_tensor_tensor(equal[:, :], running[:, :], sign[:, 3:4], equal[:, :], ALU.is_le, ALU.mult))
            link(eng.tensor_tensor(above[:, :], above[:, :], equal[:, :], ALU.add))
            prefix(above)
            eng.wait_ge(counts_out, 35)
            link(eng.tensor_copy(count[:, :], ring[:, 3, 0:1]))
            eng.scalar_tensor_tensor(slot1[:, :], running[:, :], count[:, 0:1], above[:, :], ALU.add, ALU.mult).then_inc(slot_done, 1)

            eng.wait_ge(tokens_done, 1)
            link(eng.tensor_scalar(slot_i[:, :, :, :].rearrange("p q j e -> p (q j e)"),
                                   ring[:, 0:2].rearrange("p a b -> p (a b)"), -1.0, None, ALU.add))
            eng.tensor_scalar(taken[:, :, :, :], slot_i[:, :, :, :], 0.0, None, ALU.is_ge)
            eng.tensor_scalar(digit_i[:, 0], slot_i[:, :, :, :], LO - 1, None, ALU.bitwise_and)
            link(eng.tensor_scalar(digit_i[:, 1], slot_i[:, :, :, :], 5, None, ALU.arith_shift_right))
            for m, dst in ((0, lo_b), (1, hi_b)):
                link(eng.tensor_copy(dst[:, :, :].rearrange("p e t -> p t e"),
                                     digit_i[:, m].rearrange("p q j e -> p (q j) e")))
            def hot_stage(c):
                c.wait(eng, list_done, c.n - 1)
                eng.tensor_tensor(hot_hi[:, c.parity], iota_hi[:, :, :],
                                  hi_b[:, c.n].unsqueeze(1).broadcast_to([P, HI, NT]), ALU.is_equal).then_inc(hot_hi_ready, 1)
                eng.tensor_tensor(hot_lo[:, c.parity], iota_lo[:, :, :],
                                  lo_b[:, c.n].unsqueeze(1).broadcast_to([P, LO, NT]), ALU.is_equal).then_inc(hot_lo_ready, 1)
                if c.parity == 1:
                    tile_values(eng, c)

            def list_stage(c):
                eng.wait_ge(list_done, c.n + 1)
                if not (c.fixed and c.n == 0):
                    eng.wait_ge(list_read, c.n)
                eng.tensor_copy(part_sum[:, :], ps_y[0:LO, c.parity, 0:2 * HI]).then_inc(list_sum, 1)
                eng.wait_ge(list_sum, c.n + 1)
                eng.scalar_tensor_tensor(lists[:, c.n], part_sum[:, HI:2 * HI], float(P), part_sum[:, 0:HI],
                                         ALU.mult, ALU.add).then_inc(list_read, 1)

            def shares_stage():
                eng.wait_ge(soft, 4)
                link(eng.tensor_tensor(part[:, :, :], probs[:, :, :], taken[:, :, :, :].rearrange("p q j e -> p (q j) e"), ALU.mult))
                link(eng.tensor_reduce(tile_sum[:, :], part[:, :, :], AX_X, ALU.add))
                link(eng.tensor_scalar(tile_max[:, :], tile_sum[:, :], 0.0, None, ALU.is_le))
                link(eng.tensor_tensor(tile_sum[:, :], tile_sum[:, :], tile_max[:, :], ALU.add))
                link(eng.reciprocal(tile_sum[:, :], tile_sum[:, :]))
                for q in range(NQ):
                    tiles = slice(q * NJ, q * NJ + NJ)
                    ins = eng.tensor_tensor(shares[:, :, q], part[:, tiles], tile_sum[:, tiles].unsqueeze(2).broadcast_to([P, NJ, E]),
                                            ALU.mult)
                ins.then_inc(shares_ready, 1)

            hot_stage(Place(0, 0))
            hot_stage(Place(0, 1))
            for m in range(2):
                list_stage(Place(0, m))
                hot_stage(Place(1, m))
            shares_stage()
            with eng.Fori(1, E // 2 - 1) as i:
                for m in range(2):
                    list_stage(Place(i, m))
                    hot_stage(Place(i, m).shift(2))
            for m in range(2):
                list_stage(Place(E // 2 - 1, m))

            def stages(at, k):
                if has(k, 1) and (k is None or k >= -1):
                    c = at.shift(1)
                    for q in range(KD):
                        eng.wait_ge(etr_done, KD * c.n + q + 1)
                        eng.tensor_scalar(xe[:, q], ps_tr[:, q], normw[:, q:q + 1], None, ALU.mult).then_inc(etr_read, 1)
                if has(k, 0):
                    eng.wait_ge(w_in[at.parity], 64 * at.pair + 64)
                    if k is None or k >= 2:
                        eng.wait_ge(scattered, 16 * SLOTS * (at.n - 1))
                    if k is None or k >= 1:
                        eng.wait_ge(y_ready, SLOTS * at.n)
                    for s in range(SLOTS):
                        eng.wait_ge(y_done, SLOTS * at.n + s + 1)
                        eng.tensor_tensor(ysum[:, s], ps_y[:, s % 2, 0:D], b2[:, at.parity], ALU.add).then_inc(y_read, 1)
                        eng.wait_ge(y_read, SLOTS * at.n + s + 1)
                        if s == 0:
                            eng.wait_ge(share_ready, at.n + 1)
                        eng.tensor_scalar(ye[:, at.parity, s], ysum[:, s], share[:, at.parity, s:s + 1], None, ALU.mult).then_inc(y_ready, 1)
                if has(k, 1) and (k is None or k >= -1):
                    c = at.shift(1)
                    eng.wait_ge(gathered[c.parity], 16 * SLOTS * c.pair + 16 * SLOTS)
                    eng.tensor_copy(share[:, c.parity], rows[:, c.parity, :, bass.ds(c.n + D, 1)].rearrange("p s o -> p (s o)")).then_inc(share_ready, 1)

            experts(eng, stages)


def state_space_block(nc, x_in, x_out, w):
    M = 2 * NS
    NT = L // P
    NH = L // CH
    BC = 2 * NS
    XD = 3 * BC + DTR
    x_rows = x_in.rearrange("(b t p) d -> b p t d", p=P, t=NT)
    y_rows = x_out.rearrange("(b t p) d -> b t p d", p=P, t=NT)
    TASKS = (("delta", 2, 0, "units"), ("gate", 2, 1, "units"), ("gate", 3, 2, "units"), ("out", 0, 3, "out"),
             ("out", 2, 4, "out"), ("out", 4, 5, "out"), ("turn", 0, 7, "prep"), ("turn", 1, 8, "prep"),
             ("project", 0, 9, "prep"), ("convolve", 0, 10, "prep"), ("project", 1, 11, "prep"),
             ("delta", 3, 12, "units"), ("convolve", 1, 13, "prep"), ("project", 2, 14, "prep"),
             ("project", 3, 17, "prep"), ("convolve", 2, 18, "prep"), ("convolve", 3, 19, "prep"),
             ("xdbl", 0, 22, "prep"), ("delta", 0, 24, "prep"), ("gate", 0, 25, "prep"), ("delta", 1, 27, "prep"),
             ("gate", 1, 29, "prep"), ("out", 6, 31, "out"))

    def has(task, units, out, prep):
        return {"units": units, "out": out, "prep": prep}[task[3]]

    def after(eng, sem, count):
        if not isinstance(count, int) or count > 0:
            eng.wait_ge(sem, count)

    with ExitStack() as ctx:
        def sb(name, shape, dt=F32):
            return ctx.enter_context(nc.sbuf_tensor("b_" + name, shape, dt))

        def sem(name):
            return nc.alloc_semaphore("b_" + name)

        def ps(name, shape):
            return ctx.enter_context(nc.psum_tensor("b_" + name, shape, F32))

        w_in = sb("w_in", [P, KD, 2 * DI])
        w_x = sb("w_x", [P, KI, XD])
        w_dt = sb("w_dt", [P, DI])
        w_out = sb("w_out", [P, KI, D])
        taps = sb("taps", [P, KI, KC])
        tab = sb("tab", [P, 3, KI])
        a_log = sb("a_log", [P, KI, NS])
        ident = sb("ident", [P, P])
        diag_conv = sb("diag_conv", [P, KI, KC, P])
        diag_d = sb("diag_d", [P, KI, P])
        pick_i = sb("pick_i", [P, BC], U32)
        pick_r = sb("pick_r", [P, 2], U32)
        pick_f = sb("pick_f", [P, BC])
        pick_rf = sb("pick_rf", [P, 1])
        pick = sb("pick", [P, BC], BF16)
        one = sb("one", [P, 1])
        xt = sb("xt", [P, NT, D])
        stats = sb("stats", [P, NT, 6])
        mv = sb("mv", [P, NT, 2])
        var = sb("var", [P, NT])
        std = sb("std", [P, NT])
        inv = sb("inv", [P, NT])
        u_cols = sb("u_cols", [P, KD, L])
        PAD = KC - 1
        xin = sb("xin", [P, KI, PAD + CH])
        tail = sb("tail", [P, 2, KI, PAD])
        xc = sb("xc", [P, KI, L])
        sres = sb("sres", [P, KI, L])
        xd = sb("xd", [P, L])
        parts = sb("parts", [P, L], BF16)
        next_parts = sb("next_parts", [P, L], BF16)
        rest = sb("rest", [P, L])
        delta = sb("delta", [P, KI, L])
        soft = sb("soft", [P, 2, CH])
        du = sb("du", [P, KI, L])
        bbc = sb("bbc", [P, 2, CH])
        cbc = sb("cbc", [P, 2, CH])
        carry = sb("carry", [P, NS, 2, 2])
        da = sb("da", [P, 2, 2, 2, CH])
        hc = sb("hc", [P, 2, 2, 2, CH])
        yg = sb("yg", [P, KI, L])
        xr = sb("xr", [P, 2, D])
        yt = sb("yt", [P, 2, D])
        ps_y = ps("ps_y", [P, KI, CH])
        ps_bc = ps("ps_bc", [P, 2, CH])
        side = ps("side", [P, 2, CH])

        weights_in, consts, ident0 = sem("weights_in"), sem("consts"), sem("ident0")
        setup, a_exp = sem("setup"), sem("a_exp")
        x_loaded = sem("x_loaded")
        ln_steps, stats_ready, std_ready, rows_ready = sem("ln_steps"), sem("stats_ready"), sem("std_ready"), sem("rows_ready")
        passed = sem("passed")
        side_done, side_read = [sem("side_done0"), sem("side_done1")], [sem("side_read0"), sem("side_read1")]
        xc_ready, gate_ready = sem("xc_ready"), sem("gate_ready")
        high_ready, rest_ready, mid_ready = sem("high_ready"), sem("rest_ready"), sem("mid_ready")
        low_ready, parts_ready = sem("low_ready"), sem("parts_ready")
        soft_abs, soft_exp, soft_ready = sem("soft_abs"), sem("soft_exp"), sem("soft_ready")
        delta_ready, du_ready = sem("delta_ready"), sem("du_ready")
        bc_done, bbc_ready, cbc_ready = sem("bc_done"), sem("bbc_ready"), sem("cbc_ready")
        da_ready, dbu_ready, scanned, hc_ready, added = sem("da_ready"), sem("dbu_ready"), sem("scanned"), sem("hc_ready"), sem("added")
        y_read, carried = sem("y_read"), sem("carried")
        xr_loaded = [sem("xr_loaded0"), sem("xr_loaded1")]
        y_stored = [sem("y_stored0"), sem("y_stored1")]
        NW = 7

        def steps(eng, step):
            step(-1, False, False, True)
            step(0, True, False, True)
            step(1, True, True, True)
            with eng.Fori(2, B - 1) as b:
                step(b, True, True, True)
            step(B - 1, True, True, False)
            step(B, False, True, False)

        def parts_of(b):
            return 0 <= b < B, b > 0, b < B - 1

        def uses(b, name, c):
            def those(step):
                return [t[:2] for t in TASKS if has(t, *parts_of(step))]

            first = b if isinstance(b, int) else 1
            return (sum(len(those(step)) for step in range(-1, first)) + those(first).index((name, c))
                    + (b - first) * len(TASKS))

        def blocks(buf, i, half):
            return buf[:, 2 * i:2 * i + 2, half * CH:half * CH + CH]

        def spread_over(buf):
            return buf.unsqueeze(1).broadcast_to([P, 2, CH])

        def taken(eng, b, name, c):
            for bank in range(2):
                eng.wait_ge(side_read[bank], uses(b, name, c) + 1)

        block = ctx.enter_context(nc.Block())

        @block.sync
        def _(eng):
            eng.dma_start(xt[:, :, :], x_rows[0]).then_inc(x_loaded, 16)
            eng.dma_start(w_in[:, :, :], w["b_in"].rearrange("(k p) n -> p k n", p=P)).then_inc(weights_in, 16)
            eng.dma_start(w_x[:, :, :], w["b_x"].rearrange("(k p) n -> p k n", p=P)).then_inc(weights_in, 16)
            eng.dma_start(w_dt[3 * BC:XD, :], w["b_dt"]).then_inc(weights_in, 16)
            eng.dma_start(w_out[:, :, :], w["b_out"].rearrange("(k p) n -> p k n", p=P)).then_inc(weights_in, 16)
            eng.dma_start(taps[:, :, :], w["b_taps"].rearrange("(k p) n -> p k n", p=P)).then_inc(weights_in, 16)
            eng.dma_start(tab[:, :, :], w["b_tab"]).then_inc(weights_in, 16)
            eng.dma_start(a_log[:, :, :], w["b_a_log"].rearrange("(k p) n -> p k n", p=P)).then_inc(weights_in, 16)

            def step(b, units, out, prep):
                if prep and not (isinstance(b, int) and b == -1):
                    taken(eng, b - 1, "turn", 1)
                    eng.dma_start(xt[:, :, :], x_rows[b + 1]).then_inc(x_loaded, 16)
                if out:
                    def summed(b, t):
                        eng.wait_ge(side_read[t % 2], uses(b, "out", t - t % 2) + 1)

                    for t in range(NT):
                        if t >= 2:
                            summed(b, t - 2)
                        elif not (isinstance(b, int) and b == 1):
                            summed(b - 1, t + NT - 2)
                        eng.dma_start(xr[:, t % 2], x_rows[b - 1][:, t]).then_inc(xr_loaded[t % 2], 16)
                        if t >= 1:
                            summed(b, t - 1)
                            eng.dma_start(y_rows[b - 1][t - 1], yt[:, (t - 1) % 2]).then_inc(y_stored[(t - 1) % 2], 16)
                    summed(b, NT - 1)
                    eng.dma_start(y_rows[b - 1][NT - 1], yt[:, (NT - 1) % 2]).then_inc(y_stored[(NT - 1) % 2], 16)

            steps(eng, step)
            for s in y_stored:
                eng.wait_ge(s, 16 * B * NT // 2)

        @block.gpsimd
        def _(eng):
            eng.memset(ident[:, :], 0.0).then_inc(ident0, 1)
            eng.wait_ge(ident0, 1)
            eng.affine_select(out=ident[:, :], in_=ident[:, :], compare_op=ALU.not_equal, fill=1.0,
                              base=0, pattern=[[-1, P]], channel_multiplier=1).then_inc(consts, 1)
            eng.memset(one[:, :], 1.0).then_inc(consts, 1)
            eng.iota(pick_i[:, :], [[1, BC]], base=0, channel_multiplier=0).then_inc(consts, 1)
            eng.iota(pick_r[:, 0:1], [[0, 1]], base=0, channel_multiplier=1).then_inc(consts, 1)
            for c in range(2):
                eng.memset(tail[:, c], 0.0).then_inc(consts, 1)
            eng.memset(w_dt[0:64, 0:4], 0.0).then_inc(consts, 1)

            def deltas(b, k):
                half, i = k // 2, k % 2
                eng.wait_ge(soft_ready, 4 * b + k + 1)
                eng.tensor_tensor(blocks(delta, i, half), blocks(delta, i, half), soft[:, :, :], ALU.add).then_inc(delta_ready, 1)
                eng.wait_ge(delta_ready, 4 * b + k + 1)
                eng.wait_ge(xc_ready, b + 1)
                eng.tensor_tensor(blocks(du, i, half), blocks(delta, i, half), blocks(xc, i, half), ALU.mult).then_inc(du_ready, 1)

            def step(b, units, out, prep):
                if units:
                    for m in range(M):
                        for i in range(2):
                            half, u = m // NS, 2 * m + i
                            if m == 0 or m == NS:
                                eng.wait_ge(du_ready, 4 * b + 2 * half + i + 1)
                            if i == 0:
                                eng.wait_ge(bbc_ready, M * b + m + 1)
                            after(eng, added, 2 * M * b + u - 3)
                            eng.tensor_tensor(hc[:, m % 2, i], blocks(du, i, half), spread_over(bbc[:, m % 2]), ALU.mult).then_inc(dbu_ready, 1)
                        if m in (3, 14):
                            deltas(b, 2 if m == 3 else 3)
                        if prep and m in (26, 29):
                            deltas(b + 1, 0 if m == 26 else 1)
                if prep and not units:
                    deltas(b + 1, 0)
                    deltas(b + 1, 1)

            steps(eng, step)

        @block.scalar
        def _(eng):
            eng.wait_ge(stats_ready, 1)
            eng.activation(std[:, :], var[:, :], ACT.Sqrt).then_inc(std_ready, 1)
            eng.wait_ge(weights_in, 16 * NW)
            eng.wait_ge(consts, 6)
            eng.activation(a_log[:, :, :], a_log[:, :, :], ACT.Exp).then_inc(a_exp, 1)
            eng.wait_ge(setup, 8)

            def delta_read(b, k):
                nb, n = b + 1 if k < 2 else b, uses(b, "delta", k)
                after(eng, delta_ready, 4 * nb + k)
                after(eng, soft_ready, 4 * nb + k)
                after(eng, da_ready, 2 * M * b + (2 * NS if k < 2 else 0))
                half, i = k // 2, k % 2
                for j in range(2):
                    eng.wait_ge(side_done[j], n + 1)
                    z, bias = side[:, j], tab[:, 1, 2 * i + j:2 * i + j + 1]
                    eng.activation(blocks(delta, i, half)[:, j], z, ACT.Relu, bias=bias)
                    eng.activation(soft[:, j], z, ACT.Abs, bias=bias).then_inc(side_read[j], 1)

            def delta_log(b, k):
                nb = b + 1 if k < 2 else b
                taken(eng, b, "delta", k)
                eng.activation(soft[:, :, :], soft[:, :, :], ACT.Exp, scale=-1.0).then_inc(soft_exp, 1)
                eng.wait_ge(soft_exp, 4 * nb + k + 1)
                eng.activation(soft[:, :, :], soft[:, :, :], ACT.Ln, bias=one[:, 0:1]).then_inc(soft_ready, 1)

            def std_stage(b):
                eng.wait_ge(stats_ready, b + 1)
                eng.activation(std[:, :], var[:, :], ACT.Sqrt).then_inc(std_ready, 1)

            def conv_silu(b):
                taken(eng, b, "convolve", 3)
                eng.activation(xc[:, :, :], xc[:, :, :], ACT.Silu).then_inc(xc_ready, 1)

            def xdbl_high(b):
                n = uses(b, "xdbl", 0)
                after(eng, low_ready, b + 1)
                for half in range(NH):
                    eng.wait_ge(side_done[half], n + 1)
                    eng.activation(xd[0:XD, half * CH:half * CH + CH], side[0:XD, half], ACT.Copy).then_inc(side_read[half], 1)
                taken(eng, b, "xdbl", 0)
                after(eng, parts_ready, b + 1)
                eng.activation(next_parts[0:3 * BC, :], xd[0:3 * BC, :], ACT.Copy).then_inc(high_ready, 1)

            def middle(b):
                eng.wait_ge(rest_ready, 2 * (b + 1) + 2)
                for r in (BC, 2 * BC):
                    ins = eng.activation(next_parts[r:r + BC, :], rest[r:r + BC, :], ACT.Copy)
                ins.then_inc(mid_ready, 1)

            def hand_over(b):
                eng.wait_ge(low_ready, b + 2)
                after(eng, bc_done, 2 * M * (b + 1))
                eng.activation(parts[0:3 * BC, :], next_parts[0:3 * BC, :], ACT.Copy).then_inc(parts_ready, 1)

            def step(b, units, out, prep):
                if units:
                    for m in range(M):
                        U = 2 * M * b + 2 * m
                        for i, (dst, ready, used) in enumerate(((bbc, bbc_ready, dbu_ready), (cbc, cbc_ready, hc_ready))):
                            eng.wait_ge(bc_done, U + i + 1)
                            after(eng, used, U - 2)
                            eng.activation(dst[:, m % 2], ps_bc[:, i], ACT.Copy).then_inc(ready, 1)
                            if prep and m == M - 1 and i == 1:
                                hand_over(b)
                            half = m // NS
                            if m == 0 or m == NS:
                                eng.wait_ge(delta_ready, 4 * b + 2 * half + i + 1)
                            after(eng, scanned, U + i - 3)
                            for j in range(2):
                                ins = eng.activation(da[:, m % 2, i, j], blocks(delta, i, half)[:, j], ACT.Exp,
                                                     scale=a_log[:, 2 * i + j, m % NS:m % NS + 1])
                            ins.then_inc(da_ready, 1)
                        if m in (0, 12):
                            delta_read(b, 2 if m == 0 else 3)
                        if m in (2, 13):
                            delta_log(b, 2 if m == 2 else 3)
                        if m == 4:
                            if prep:
                                std_stage(b + 1)
                            taken(eng, b, "gate", 3)
                            eng.activation(sres[:, :, :], sres[:, :, :], ACT.Silu).then_inc(gate_ready, 1)
                        if prep and m == 20:
                            conv_silu(b)
                        if prep and m == 23:
                            xdbl_high(b)
                        if prep and m in (24, 27):
                            delta_read(b, 0 if m == 24 else 1)
                        if prep and m in (25, 28):
                            delta_log(b, 0 if m == 25 else 1)
                        if prep and m == 26:
                            middle(b)
                elif prep:
                    conv_silu(b)
                    xdbl_high(b)
                    middle(b)
                    delta_read(b, 0)
                    delta_log(b, 0)
                    hand_over(b)
                    delta_read(b, 1)
                    delta_log(b, 1)

            steps(eng, step)

        @block.tensor
        def _(eng):
            eng.wait_ge(consts, 7)

            def fill(b, name, k, bank, out, products):
                after(eng, side_read[bank], uses(b, name, k))
                last = len(products) - 1
                for n, (lhs, rhs) in enumerate(products):
                    mm = eng.matmul(out, lhs, rhs, start=n == 0, stop=n == last)
                mm.then_inc(side_done[bank], 1)

            def cols(half):
                return slice(half * CH, half * CH + CH)

            def task(b, name, k):
                if isinstance(b, int) and b == -1:
                    if (name, k) == ("project", 0):
                        eng.wait_ge(weights_in, 16 * NW)
                    elif (name, k) == ("convolve", 0):
                        eng.wait_ge(setup, 8)
                if name == "turn":
                    eng.wait_ge(rows_ready, b + 2)
                elif name == "project":
                    taken(eng, b, "turn", 1)
                elif name == "convolve":
                    taken(eng, b, "project", k)
                elif name == "xdbl":
                    eng.wait_ge(xc_ready, b + 2)
                elif name == "delta":
                    taken(eng, b if k < 2 else b - 1, "xdbl", 0)
                elif name == "out" and k == 0:
                    eng.wait_ge(y_read, 4 * b)
                half = k // 2
                for bank in range(2):
                    c, dst = 2 * (k % 2) + bank, side[:, bank]
                    if name == "turn":
                        after(eng, side_read[bank], uses(b, name, k))
                        for t in range(TB):
                            mm = eng.transpose(dst[:, t * P:t * P + P], xt[:, TB * k + t, bank * P:bank * P + P], ident[:, :])
                        mm.then_inc(side_done[bank], 1)
                    elif name == "project":
                        fill(b, name, k, bank, dst,
                             [(w_in[:, kb, c * P:c * P + P], u_cols[:, kb, cols(half)]) for kb in range(KD)])
                    elif name == "gate":
                        fill(b, name, k, bank, dst,
                             [(w_in[:, kb, DI + c * P:DI + c * P + P], u_cols[:, kb, cols(half)]) for kb in range(KD)])
                    elif name == "convolve":
                        fill(b, name, k, bank, dst,
                             [(diag_conv[:, c, tap], xin[:, c, tap:tap + CH]) for tap in range(KC)])
                    elif name == "xdbl":
                        fill(b, name, k, bank, dst[0:XD], [(w_x[:, kb], xc[:, kb, cols(bank)]) for kb in range(KI)])
                    elif name == "delta":
                        fill(b, name, k, bank, dst, [(w_dt[3 * BC:XD, c * P:c * P + P], xd[3 * BC:XD, cols(half)])])
                    else:
                        t = k + bank
                        fill(b, name, k, bank, dst[:, 0:D],
                             [(yg[:, kb, t * P:t * P + P], w_out[:, kb]) for kb in range(KI)])

            def add(b, m, i):
                half, u = m // NS, 2 * M * b + 2 * m + i
                if m % NS == 0:
                    after(eng, y_read, 4 * b + 2 * half - 1 + i)
                    for c in (2 * i, 2 * i + 1):
                        eng.matmul(ps_y[:, c], diag_d[:, c], xc[:, c, cols(half)], start=True, stop=False,
                                   skip_group_check=True)
                eng.wait_ge(hc_ready, u + 1)
                for j in range(2):
                    mm = eng.matmul(ps_y[:, 2 * i + j], ident[:, :], hc[:, m % 2, i, j], start=False,
                                    stop=m % NS == NS - 1, skip_group_check=True)
                mm.then_inc(added, 1)

            def add_behind(b, m, i, out):
                if m >= 2:
                    add(b, m - 2, i)
                elif out:
                    add(b - 1, m - 2 + M, i)

            def spread(b, m, i):
                after(eng, cbc_ready if i else bbc_ready, M * b + m)
                n = NS * i + m % NS
                eng.matmul(ps_bc[:, i], pick[0:3 * BC, n:n + 1].broadcast_to([3 * BC, P]),
                           parts[0:3 * BC, cols(m // NS)], start=True, stop=True).then_inc(bc_done, 1)

            def step(b, units, out, prep):
                if units:
                    eng.wait_ge(parts_ready, b + 1)
                    for m in range(M):
                        here = [t for t in TASKS if t[2] == m and has(t, units, out, prep)]
                        for i in range(2):
                            spread(b, m, i)
                            add_behind(b, m, i, out)
                            for t in here:
                                if (t[0] == "delta") == (i == 0):
                                    task(b, t[0], t[1])
                else:
                    if out:
                        for m in range(2):
                            for i in range(2):
                                add_behind(b, m, i, out)
                    for t in TASKS:
                        if has(t, units, out, prep):
                            task(b, t[0], t[1])

            steps(eng, step)

        @block.vector
        def _(eng):
            def norm(nb):
                eng.wait_ge(x_loaded, 16 * nb + 16)
                for t in range(NT):
                    ins = eng.bn_stats(stats[:, t], xt[:, t])
                ins.then_inc(ln_steps, 1)
                wait_alone(eng, ln_steps, 3 * nb + 1, passed)
                for t in range(NT):
                    ins = eng.bn_aggr(mv[:, t], stats[:, t])
                ins.then_inc(ln_steps, 1)
                eng.wait_ge(ln_steps, 3 * nb + 2)
                eng.tensor_scalar(var[:, :], mv[:, :, 1], LN_EPS, None, ALU.add).then_inc(stats_ready, 1)

            def norm_rows(nb):
                eng.wait_ge(std_ready, nb + 1)
                eng.reciprocal(inv[:, :], std[:, :]).then_inc(ln_steps, 1)
                eng.wait_ge(ln_steps, 3 * nb + 3)
                for t in range(NT):
                    ins = eng.tensor_scalar(xt[:, t], xt[:, t], mv[:, t, 0:1], inv[:, t:t + 1], ALU.subtract, ALU.mult)
                ins.then_inc(rows_ready, 1)

            norm(0)
            norm_rows(0)
            eng.wait_ge(consts, 7)
            eng.wait_ge(weights_in, 16 * NW)
            eng.tensor_copy(pick_f[:, :], pick_i[:, :])
            eng.tensor_scalar(pick_r[:, 1:2], pick_r[:, 0:1], BC - 1, None, ALU.bitwise_and).then_inc(setup, 1)
            eng.wait_ge(setup, 1)
            eng.tensor_copy(pick_rf[:, :], pick_r[:, 1:2]).then_inc(setup, 1)
            eng.wait_ge(setup, 2)
            eng.tensor_scalar(pick[:, :], pick_f[:, :], pick_rf[:, 0:1], None, ALU.is_equal).then_inc(setup, 1)
            for c in range(KI):
                for k in range(KC):
                    eng.tensor_scalar(diag_conv[:, c, k], ident[:, :], taps[:, c, k:k + 1], None, ALU.mult)
                eng.tensor_scalar(diag_d[:, c], ident[:, :], tab[:, 2, c:c + 1], None, ALU.mult).then_inc(setup, 1)
            eng.wait_ge(a_exp, 1)
            eng.tensor_scalar(a_log[:, :, :], a_log[:, :, :], -1.0, None, ALU.mult).then_inc(setup, 1)

            def task_read(b, name, k):
                n, half = uses(b, name, k), k // 2
                tokens = slice(half * CH, half * CH + CH)
                if name == "gate":
                    after(eng, y_read, 4 * b + 2 if k < 2 else 4 * b)
                elif name == "convolve":
                    after(eng, du_ready, 4 * b + k + 1)
                for bank in range(2):
                    c, src, s = 2 * (k % 2) + bank, side[:, bank], side_read[bank]
                    eng.wait_ge(side_done[bank], n + 1)
                    if name == "turn":
                        eng.tensor_copy(u_cols[:, bank, k * CH:k * CH + CH], src).then_inc(s, 1)
                    elif name == "project":
                        if half == 0:
                            eng.tensor_copy(tail[:, 1, c], src[:, CH - PAD:CH])
                        else:
                            eng.wait_ge(s, uses(b, name, k - 2) + 1)
                        eng.tensor_copy(xin[:, c, 0:PAD], tail[:, half, c])
                        eng.tensor_copy(xin[:, c, PAD:PAD + CH], src).then_inc(s, 1)
                    elif name == "convolve":
                        eng.tensor_scalar(xc[:, c, tokens], src, tab[:, 0, c:c + 1], None, ALU.add).then_inc(s, 1)
                    elif name == "gate":
                        eng.tensor_copy(sres[:, c, tokens], src).then_inc(s, 1)
                    else:
                        before = NT // 2 * (b - 1) + k // 2
                        eng.wait_ge(xr_loaded[bank], 16 * before + 16)
                        after(eng, y_stored[bank], 16 * before)
                        eng.tensor_tensor(yt[:, bank], src[:, 0:D], xr[:, bank], ALU.add).then_inc(s, 1)

            def gated(b, half):
                eng.wait_ge(gate_ready, b + 1)
                for i in range(2):
                    eng.wait_ge(added, 2 * M * b + 2 * NS * (half + 1) - 1 + i)
                    eng.tensor_tensor(blocks(yg, i, half), ps_y[:, 2 * i:2 * i + 2], blocks(sres, i, half), ALU.mult).then_inc(y_read, 1)

            def below_high(b):
                eng.wait_ge(high_ready, b + 2)
                for r in (BC, 2 * BC):
                    ins = eng.tensor_tensor(rest[r:r + BC, :], xd[r:r + BC, :], next_parts[r:r + BC, :], ALU.subtract)
                    ins.then_inc(rest_ready, 1)

            def low(b):
                eng.wait_ge(mid_ready, b + 2)
                r = 2 * BC
                eng.tensor_tensor(next_parts[r:r + BC, :], rest[r:r + BC, :], next_parts[r:r + BC, :],
                                  ALU.subtract).then_inc(low_ready, 1)

            def step(b, units, out, prep):
                if units:
                    for m in range(M):
                        U = 2 * M * b + 2 * m
                        for i in range(2):
                            eng.wait_ge(da_ready, U + i + 1)
                            eng.wait_ge(dbu_ready, U + i + 1)
                            if i == 0 and m >= NS:
                                eng.wait_ge(carried, NS * b + m - NS + 1)
                            for j in range(2):
                                first = carry[:, m - NS, i, j:j + 1] if m >= NS else 0.0
                                ins = eng.tensor_tensor_scan(hc[:, m % 2, i, j], da[:, m % 2, i, j], hc[:, m % 2, i, j], first,
                                                             ALU.mult, ALU.add)
                            ins.then_inc(scanned, 1)
                        if m < NS:
                            eng.wait_ge(scanned, U + 2)
                            eng.tensor_copy(carry[:, m], hc[:, m % 2, :, :, CH - 1]).then_inc(carried, 1)
                            eng.wait_ge(carried, NS * b + m + 1)
                        for name, k, at, who in TASKS:
                            if at == m and has((name, k, at, who), units, out, prep) and name not in ("delta", "xdbl"):
                                task_read(b, name, k)
                        for i in range(2):
                            if i == 0:
                                eng.wait_ge(cbc_ready, M * b + m + 1)
                            eng.wait_ge(scanned, U + i + 1)
                            eng.tensor_tensor(hc[:, m % 2, i], hc[:, m % 2, i], spread_over(cbc[:, m % 2]), ALU.mult).then_inc(hc_ready, 1)
                        if m == 0 and out:
                            gated(b - 1, 1)
                        if m == NS:
                            gated(b, 0)
                        if prep and m == 2:
                            norm(b + 1)
                        if prep and m == 5:
                            norm_rows(b + 1)
                        if prep and m == 24:
                            below_high(b)
                        if prep and m == 27:
                            low(b)
                else:
                    if out:
                        gated(b - 1, 1)
                    for name, c, at, who in TASKS:
                        if has((name, c, at, who), units, out, prep):
                            if name == "xdbl":
                                below_high(b)
                                low(b)
                            elif name != "delta":
                                task_read(b, name, c)

            steps(eng, step)


def program(nc, w, out):
    x1 = nc.dram_tensor("x1", (T, D), F32, kind="Internal").ap()
    rows_tab = nc.dram_tensor("rows_tab", (T, D + E), F32, kind="Internal").ap()
    list_tab = nc.dram_tensor("list_tab", (E, CAP), U32, kind="Internal").ap()
    with nc.cleanup_on_exit():
        recurrence_block(nc, w["x"], x1, w)
    with nc.cleanup_on_exit():
        experts_block(nc, "f_", x1, rows_tab, list_tab, w)
    with nc.cleanup_on_exit():
        state_space_block(nc, x1, out, w)
    with nc.cleanup_on_exit():
        experts_block(nc, "g_", out, rows_tab, list_tab, w)


def kernel(**inputs):
    import numpy as np
    import concourse.bacc as _bacc
    from concourse import mybir as _mybir
    from concourse.bass_utils import run_bass_kernel_spmd as _run

    a = {k: np.asarray(v) for k, v in inputs.items()}

    def g(name):
        return a["L0_" + name]

    def columns(v):
        return np.asarray(v).reshape(-1, 128).T

    cc = np.ascontiguousarray
    arrays = {
        "x": cc(g("attn_a_hidden_states").reshape(T, D)),
        "a_table": cc(np.concatenate([columns(g("attn_a_" + n)) for n in (
            "fc_r_b", "fc_i_b", "fc_b", "fc_gate_b", "mlp_gate_b", "mlp_fc_b", "norm_w", "norm2_w", "alpha")], axis=1)),
        "a_proj": cc(np.stack([g("attn_a_" + n).T for n in ("fc_r_w", "fc_i_w", "fc_w", "fc_gate_w")], axis=1)),
        "a_mlp": cc(np.stack([g("attn_a_mlp_gate_w").T, g("attn_a_mlp_fc_w").T])),
        "a_out": cc(g("attn_a_out_w").T),
        "a_out_b": cc(g("attn_a_out_b")),
        "f_router": cc(g("ffn_router_weight").T),
        "f_router_b": cc(g("ffn_router_bias")),
        "f_norm": cc(columns(g("ffn_norm_weight"))),
        "f_w1": cc(g("ffn_fc1_weight").transpose(0, 2, 1)),
        "f_w2": cc(g("ffn_fc2_weight").transpose(0, 2, 1)),
        "f_b1": cc(g("ffn_fc1_bias").reshape(E, KF, P).transpose(0, 2, 1)),
        "f_b2": cc(g("ffn_fc2_bias")),
        "b_in": cc(g("attn_b_W_in")),
        "b_x": cc(np.concatenate([g("attn_b_W_x")[:, DTR:]] * 3 + [g("attn_b_W_x")[:, :DTR]], axis=1)),
        "b_dt": cc(g("attn_b_W_dt")),
        "b_out": cc(g("attn_b_W_out")),
        "b_taps": cc(g("attn_b_conv_w")),
        "b_tab": cc(np.stack([columns(g("attn_b_" + n)) for n in ("conv_b", "b_dt", "D")], axis=1)),
        "b_a_log": cc(g("attn_b_A_log")),
    }
    nc = _bacc.Bacc("TRN2", target_bir_lowering=False, num_devices=1)
    aps = {}
    for name, v in arrays.items():
        aps[name] = nc.dram_tensor("in_" + name, v.shape, _mybir.dt.from_np(v.dtype), kind="ExternalInput").ap()
    out = nc.dram_tensor("out", (T, D), _mybir.dt.float32, kind="ExternalOutput").ap()
    program(nc, aps, out)
    r = _run(nc, [{"in_" + k: v for k, v in arrays.items()}], core_ids=[0])
    return np.asarray(r.results[0]["out"]).reshape(B, L, D)
```
